# Optimizing a Trainium2 kernel written in Bass

```python
import numpy as np
import jax
import jax.numpy as jnp

def _softmax(x, axis=-1):
    return jax.nn.softmax(x, axis=axis)

def _gelu(x):
    return jax.nn.gelu(x, approximate=True)

def _silu(x):
    return jax.nn.silu(x)

def _sigmoid(x):
    return jax.nn.sigmoid(x)

def _layernorm(x, axis=-1, eps=1e-05):
    m = jnp.mean(x, axis=axis, keepdims=True)
    v = jnp.var(x, axis=axis, keepdims=True)
    return (x - m) / jnp.sqrt(v + eps)

def _scatter_add(tgt, idx, src, axis=0):
    return tgt.at[idx].add(src)

def _segment_sum(src, seg, n):
    return jax.ops.segment_sum(src, seg, n)
kernel_name = 'mk_sandwich_d1_jaxref_r8_6006b4'

def setup_inputs(seed: int=0):
    np.random.seed(seed)
    _w = jnp.asarray

    def _L0_attn_setup():
        import jax, jax.numpy as jnp
        import numpy as np
        B, T, D, H, NT = (2, 256, 128, 16, 7)
        HD = D // H
        TEMP = 0.5
        key = jax.random.key(seed)
        ks = jax.random.split(key, 6)
        x = jax.random.normal(ks[0], (B, T, D), jnp.float32)
        qkv_w = jax.random.normal(ks[1], (3 * D, D), jnp.float32) / np.sqrt(D)
        out_w = jax.random.normal(ks[2], (D, D), jnp.float32) / np.sqrt(D)
        hex_w = jax.random.normal(ks[3], (6, D), jnp.float32) * 0.02
        q6_w = jax.random.normal(ks[4], (6, D), jnp.float32) * 0.02
        tr = np.zeros((NT, 6, 6), dtype=np.float32)
        for i in range(6):
            tr[i] = np.eye(6)
            tr[i, i, i] = -1.0
        tr[6] = -np.eye(6)
        transforms = jnp.asarray(tr)
        transform_weights = jax.random.normal(ks[5], (H, NT), jnp.float32) * 0.01
        hamming_lambda_logit = jnp.asarray(np.log(0.1 / 0.9), jnp.float32)
        scale_logit = jnp.zeros((), jnp.float32)
        sips_alpha = jnp.ones((1,), jnp.float32)
        sips_beta = jnp.full((1,), np.sqrt(HD), jnp.float32)
        return {'x': x, 'qkv_w': qkv_w, 'out_w': out_w, 'hex_w': hex_w, 'hamming_lambda_logit': hamming_lambda_logit, 'q6_w': q6_w, 'transforms': transforms, 'transform_weights': transform_weights, 'scale_logit': scale_logit, 'sips_alpha': sips_alpha, 'sips_beta': sips_beta}
    _L0_attn_in = _L0_attn_setup()

    def _L0_ffn_setup():
        import jax, jax.numpy as jnp
        import numpy as np
        DIM = 128
        DEPTH = 6
        HEADS = 16
        DIM_HEAD = 64
        WINDOW = 32
        INNER = HEADS * DIM_HEAD
        DIM_INNER = int(DIM * 4 * 2 / 3)
        QK_SCALE = 8.0

        def shift_tokens(t):
            a, s = jnp.split(t, 2, -1)
            s = jnp.pad(s, ((0, 0), (1, 0), (0, 0)))[:, :-1]
            return jnp.concatenate([a, s], -1)

        def l2norm(t):
            return t / jnp.maximum(jnp.linalg.norm(t, axis=-1, keepdims=True), 1e-12)

        def rotate_half(x):
            x1, x2 = jnp.split(x, 2, -1)
            return jnp.concatenate([-x2, x1], -1)

        def rotary_tables(n):
            half = jnp.arange(0, DIM_HEAD, 2, dtype=jnp.float32)
            inv_freq = 1.0 / 10000.0 ** (half / DIM_HEAD)
            t = jnp.arange(n, dtype=jnp.float32)
            freqs = t[:, None] * inv_freq[None, :]
            freqs = jnp.concatenate([freqs, freqs], -1)
            base_scale = (half + 0.4 * DIM_HEAD) / (1.4 * DIM_HEAD)
            power = (t - n // 2) / (WINDOW // 2)
            scale = base_scale[None, :] ** power[:, None]
            scale = jnp.concatenate([scale, scale], -1)
            return (freqs, scale)

        def local_attention(q, k, v):
            b, h, n, d = q.shape
            w = WINDOW
            nw = n // w
            bq = q.reshape(b, h, nw, w, d)
            bk = k.reshape(b, h, nw, w, d)
            bv = v.reshape(b, h, nw, w, d)

            def look(t):
                p = jnp.pad(t, ((0, 0), (0, 0), (1, 0), (0, 0), (0, 0)))
                return jnp.concatenate([p[:, :, :nw], p[:, :, 1:]], axis=3)
            bk2, bv2 = (look(bk), look(bv))
            seq = jnp.arange(n).reshape(nw, w)
            seq_p = jnp.pad(seq, ((1, 0), (0, 0)), constant_values=-1)
            jt = jnp.concatenate([seq_p[:nw], seq_p[1:]], axis=1)
            it = seq[:, :, None]
            jb = jt[:, None, :]
            mask = (it < jb) | (it > jb + w) | (jb == -1)
            sim = jnp.einsum('bhwie,bhwje->bhwij', bq, bk2) * QK_SCALE
            sim = jnp.where(mask, -jnp.finfo(sim.dtype).max, sim)
            attn = jax.nn.softmax(sim, -1)
            out = jnp.einsum('bhwij,bhwje->bhwie', attn, bv2)
            return out.reshape(b, h, n, d)

        def attn_layer(x, Wqkv, qs, ksc, Wo):
            b, n, _ = x.shape
            qkv = x @ Wqkv
            q, k, v = jnp.split(qkv, 3, -1)
            sh = lambda t: t.reshape(b, n, HEADS, DIM_HEAD).transpose(0, 2, 1, 3)
            q, k, v = (sh(q), sh(k), sh(v))
            q = l2norm(q) * qs
            k = l2norm(k) * ksc
            freqs, scale = rotary_tables(n)
            cos, sin = (jnp.cos(freqs), jnp.sin(freqs))
            q = q * cos * scale + rotate_half(q) * sin * scale
            inv = 1.0 / scale
            k = k * cos * inv + rotate_half(k) * sin * inv
            out = local_attention(q, k, v)
            out = out.transpose(0, 2, 1, 3).reshape(b, n, INNER)
            return out @ Wo

        def ffn_layer(x, g, bln, W1, b1, W2, b2):
            mu = x.mean(-1, keepdims=True)
            var = ((x - mu) ** 2).mean(-1, keepdims=True)
            xn = (x - mu) / jnp.sqrt(var + 1e-05) * g + bln
            hg = xn @ W1 + b1
            a, gate = jnp.split(hg, 2, -1)
            return a * jax.nn.gelu(gate, approximate=False) @ W2 + b2
        key = jax.random.key(seed)
        ks = jax.random.split(key, 8)
        B, N = (2, 256)
        init = lambda k, shape: jax.random.normal(k, shape, jnp.float32) * 0.02
        return {'x': jax.random.normal(ks[0], (B, N, DIM), jnp.float32), 'Wqkv': init(ks[1], (DEPTH, DIM, 3 * INNER)), 'q_scale': jnp.ones((DEPTH, DIM_HEAD), jnp.float32), 'k_scale': jnp.ones((DEPTH, DIM_HEAD), jnp.float32), 'Wo': init(ks[2], (DEPTH, INNER, DIM)), 'ln_g': jnp.ones((DEPTH, DIM), jnp.float32), 'ln_b': jnp.zeros((DEPTH, DIM), jnp.float32), 'W1': init(ks[3], (DEPTH, DIM, 2 * DIM_INNER)), 'b1': jnp.zeros((DEPTH, 2 * DIM_INNER), jnp.float32), 'W2': init(ks[4], (DEPTH, DIM_INNER, DIM)), 'b2': jnp.zeros((DEPTH, DIM), jnp.float32)}
    _L0_ffn_in = _L0_ffn_setup()
    _d = {'L0_attn_x': _L0_attn_in['x'], 'L0_attn_qkv_w': _L0_attn_in['qkv_w'], 'L0_attn_out_w': _L0_attn_in['out_w'], 'L0_attn_hex_w': _L0_attn_in['hex_w'], 'L0_attn_hamming_lambda_logit': _L0_attn_in['hamming_lambda_logit'], 'L0_attn_q6_w': _L0_attn_in['q6_w'], 'L0_attn_transforms': _L0_attn_in['transforms'], 'L0_attn_transform_weights': _L0_attn_in['transform_weights'], 'L0_attn_scale_logit': _L0_attn_in['scale_logit'], 'L0_attn_sips_alpha': _L0_attn_in['sips_alpha'], 'L0_attn_sips_beta': _L0_attn_in['sips_beta'], 'L0_ffn_Wqkv': _L0_ffn_in['Wqkv'], 'L0_ffn_q_scale': _L0_ffn_in['q_scale'], 'L0_ffn_k_scale': _L0_ffn_in['k_scale'], 'L0_ffn_Wo': _L0_ffn_in['Wo'], 'L0_ffn_ln_g': _L0_ffn_in['ln_g'], 'L0_ffn_ln_b': _L0_ffn_in['ln_b'], 'L0_ffn_W1': _L0_ffn_in['W1'], 'L0_ffn_b1': _L0_ffn_in['b1'], 'L0_ffn_W2': _L0_ffn_in['W2'], 'L0_ffn_b2': _L0_ffn_in['b2']}
    _x0 = _d['L0_attn_x']
    _d['L0_attn_x'] = jax.random.normal(jax.random.fold_in(jax.random.key(seed), 1), (8, 256, 128), dtype=_x0.dtype)
    del _x0
    return _d

def reference(L0_attn_x, L0_attn_qkv_w, L0_attn_out_w, L0_attn_hex_w, L0_attn_hamming_lambda_logit, L0_attn_q6_w, L0_attn_transforms, L0_attn_transform_weights, L0_attn_scale_logit, L0_attn_sips_alpha, L0_attn_sips_beta, L0_ffn_Wqkv, L0_ffn_q_scale, L0_ffn_k_scale, L0_ffn_Wo, L0_ffn_ln_g, L0_ffn_ln_b, L0_ffn_W1, L0_ffn_b1, L0_ffn_W2, L0_ffn_b2):

    def _L0_attn_ref(x, qkv_w, out_w, hex_w, hamming_lambda_logit, q6_w, transforms, transform_weights, scale_logit, sips_alpha, sips_beta):
        import jax, jax.numpy as jnp
        import numpy as np
        B, T, D, H, NT = (2, 256, 128, 16, 7)
        HD = D // H
        TEMP = 0.5
        b, t, _ = x.shape
        qkv = (x @ qkv_w.T).reshape(b, t, 3, H, HD)
        q = jnp.transpose(qkv[:, :, 0], (0, 2, 1, 3))
        k = jnp.transpose(qkv[:, :, 1], (0, 2, 1, 3))
        v = jnpp = jnp.transpose(qkv[:, :, 2], (0, 2, 1, 3))
        raw = jnp.einsum('bhid,bhjd->bhij', q, k)
        scores = sips_alpha[0] * jnp.tanh(raw / sips_beta[0])
        soft_bits = jnp.tanh(x @ hex_w.T)
        hamming = jnp.einsum('bid,bjd->bij', soft_bits, soft_bits) / 2.0
        lam = jax.nn.sigmoid(hamming_lambda_logit)
        scores = scores + lam * hamming[:, None, :, :]
        hexc = jnp.tanh(x @ q6_w.T)
        w = jax.nn.softmax(transform_weights / TEMP, axis=-1)
        Mh = jnp.einsum('ht,tde->hde', w, transforms)
        lat = jnp.einsum('bid,hde,bje->bhij', hexc, Mh, hexc) / 6.0
        lat = lat * (jax.nn.sigmoid(scale_logit) * 2.0)
        scores = scores + lat
        causal = jnp.tril(jnp.ones((t, t), bool))
        scores = jnp.where(causal[None, None], scores, -jnp.inf)
        attn = jax.nn.softmax(scores, axis=-1)
        out = jnp.einsum('bhij,bhjd->bhid', attn, v)
        out = jnp.transpose(out, (0, 2, 1, 3)).reshape(b, t, D)
        return out @ out_w.T

    def _L0_ffn_ref(x, Wqkv, q_scale, k_scale, Wo, ln_g, ln_b, W1, b1, W2, b2):
        import jax, jax.numpy as jnp
        import numpy as np
        DIM = 128
        DEPTH = 6
        HEADS = 16
        DIM_HEAD = 64
        WINDOW = 32
        INNER = HEADS * DIM_HEAD
        DIM_INNER = int(DIM * 4 * 2 / 3)
        QK_SCALE = 8.0

        def shift_tokens(t):
            a, s = jnp.split(t, 2, -1)
            s = jnp.pad(s, ((0, 0), (1, 0), (0, 0)))[:, :-1]
            return jnp.concatenate([a, s], -1)

        def l2norm(t):
            return t / jnp.maximum(jnp.linalg.norm(t, axis=-1, keepdims=True), 1e-12)

        def rotate_half(x):
            x1, x2 = jnp.split(x, 2, -1)
            return jnp.concatenate([-x2, x1], -1)

        def rotary_tables(n):
            half = jnp.arange(0, DIM_HEAD, 2, dtype=jnp.float32)
            inv_freq = 1.0 / 10000.0 ** (half / DIM_HEAD)
            t = jnp.arange(n, dtype=jnp.float32)
            freqs = t[:, None] * inv_freq[None, :]
            freqs = jnp.concatenate([freqs, freqs], -1)
            base_scale = (half + 0.4 * DIM_HEAD) / (1.4 * DIM_HEAD)
            power = (t - n // 2) / (WINDOW // 2)
            scale = base_scale[None, :] ** power[:, None]
            scale = jnp.concatenate([scale, scale], -1)
            return (freqs, scale)

        def local_attention(q, k, v):
            b, h, n, d = q.shape
            w = WINDOW
            nw = n // w
            bq = q.reshape(b, h, nw, w, d)
            bk = k.reshape(b, h, nw, w, d)
            bv = v.reshape(b, h, nw, w, d)

            def look(t):
                p = jnp.pad(t, ((0, 0), (0, 0), (1, 0), (0, 0), (0, 0)))
                return jnp.concatenate([p[:, :, :nw], p[:, :, 1:]], axis=3)
            bk2, bv2 = (look(bk), look(bv))
            seq = jnp.arange(n).reshape(nw, w)
            seq_p = jnp.pad(seq, ((1, 0), (0, 0)), constant_values=-1)
            jt = jnp.concatenate([seq_p[:nw], seq_p[1:]], axis=1)
            it = seq[:, :, None]
            jb = jt[:, None, :]
            mask = (it < jb) | (it > jb + w) | (jb == -1)
            sim = jnp.einsum('bhwie,bhwje->bhwij', bq, bk2) * QK_SCALE
            sim = jnp.where(mask, -jnp.finfo(sim.dtype).max, sim)
            attn = jax.nn.softmax(sim, -1)
            out = jnp.einsum('bhwij,bhwje->bhwie', attn, bv2)
            return out.reshape(b, h, n, d)

        def attn_layer(x, Wqkv, qs, ksc, Wo):
            b, n, _ = x.shape
            qkv = x @ Wqkv
            q, k, v = jnp.split(qkv, 3, -1)
            sh = lambda t: t.reshape(b, n, HEADS, DIM_HEAD).transpose(0, 2, 1, 3)
            q, k, v = (sh(q), sh(k), sh(v))
            q = l2norm(q) * qs
            k = l2norm(k) * ksc
            freqs, scale = rotary_tables(n)
            cos, sin = (jnp.cos(freqs), jnp.sin(freqs))
            q = q * cos * scale + rotate_half(q) * sin * scale
            inv = 1.0 / scale
            k = k * cos * inv + rotate_half(k) * sin * inv
            out = local_attention(q, k, v)
            out = out.transpose(0, 2, 1, 3).reshape(b, n, INNER)
            return out @ Wo

        def ffn_layer(x, g, bln, W1, b1, W2, b2):
            mu = x.mean(-1, keepdims=True)
            var = ((x - mu) ** 2).mean(-1, keepdims=True)
            xn = (x - mu) / jnp.sqrt(var + 1e-05) * g + bln
            hg = xn @ W1 + b1
            a, gate = jnp.split(hg, 2, -1)
            return a * jax.nn.gelu(gate, approximate=False) @ W2 + b2
        for i in range(DEPTH):
            x = attn_layer(shift_tokens(x), Wqkv[i], q_scale[i], k_scale[i], Wo[i]) + x
            x = ffn_layer(shift_tokens(x), ln_g[i], ln_b[i], W1[i], b1[i], W2[i], b2[i]) + x
        return x
    x = L0_attn_x
    x = x + _layernorm(_L0_attn_ref(_layernorm(x, axis=-1), L0_attn_qkv_w, L0_attn_out_w, L0_attn_hex_w, L0_attn_hamming_lambda_logit, L0_attn_q6_w, L0_attn_transforms, L0_attn_transform_weights, L0_attn_scale_logit, L0_attn_sips_alpha, L0_attn_sips_beta), axis=-1)
    x = x + _layernorm(_L0_ffn_ref(_layernorm(x, axis=-1), L0_ffn_Wqkv, L0_ffn_q_scale, L0_ffn_k_scale, L0_ffn_Wo, L0_ffn_ln_g, L0_ffn_ln_b, L0_ffn_W1, L0_ffn_b1, L0_ffn_W2, L0_ffn_b2), axis=-1)
    return x

_drawn_inputs = setup_inputs


def setup_inputs(seed=0):
    import zlib

    import numpy as np

    out = dict(_drawn_inputs(seed))
    spreads = {'L0_ffn_q_scale': (1.0, 0.6),
     'L0_ffn_k_scale': (1.0, 0.6),
     'L0_ffn_ln_g': (1.0, 0.6),
     'L0_ffn_ln_b': (0.0, 0.8),
     'L0_ffn_b1': (0.0, 0.8),
     'L0_ffn_b2': (0.0, 0.346)}
    factors = {'L0_attn_hex_w': 8.0,
     'L0_attn_q6_w': 8.0,
     'L0_attn_transforms': 7.971,
     'L0_attn_transform_weights': 8.0,
     'L0_ffn_W1': 4.552,
     'L0_ffn_W2': 4.473}
    for name, (base, spread) in spreads.items():
        noise = np.random.default_rng([zlib.crc32(name.encode()), seed]).standard_normal(out[name].shape)
        drawn = base * np.exp(spread * noise) if base else spread * noise
        out[name] = jnp.asarray(drawn.astype(out[name].dtype))
    for name, factor in factors.items():
        out[name] = (out[name] * factor).astype(out[name].dtype)
    return out
```

```python
from contextlib import ExitStack

import numpy as np
import concourse.bass as bass
from concourse import mybir

F32 = mybir.dt.float32
F32R = mybir.dt.float32r
BF16 = mybir.dt.bfloat16
I32 = mybir.dt.int32
ALU = mybir.AluOpType
ACT = mybir.ActivationFunctionType
AX = mybir.AxisListType

P = 128
B, T, D = 8, 256, 128
NT = B * T // P
TT = T // P
GH = 16
GD = D // GH
GC = GH // 4
NTR, NB = 7, 6
TEMP = 0.5
GS = P + T
DEPTH, H, HD, WIN = 6, 16, 64, 32
INNER = H * HD
DIN = D * 4 * 2 // 3
FC = -(-DIN // P)
NW = T // WIN
NU = NW // 2
KW = 2 * WIN
QC = INNER // P
NP = QC
NV = 2 * NU
NG = H // 4
VW = HD + 1
QK_SCALE = 8.0
EPS = 1e-5
RSQRT_MAGIC = 0x5F3759DF
NEWTON = 3
RSQRT_STEPS = 2 + 3 * NEWTON
UP = 1
NORM_FLOOR = 1e-24


class Steps:

    def __init__(self, eng, s):
        self.eng, self.s, self.before, self.here = eng, s, 0, 0

    def body(self, before):
        self.before, self.here = before, 0

    def then_wait(self, ins, apart=None):
        self.here += 1
        ins.then_inc(self.s, 1)
        if apart is None:
            self.eng.wait_ge(self.s, self.before + self.here)
        else:
            wait_apart(self.eng, apart, self.s, self.before + self.here)


def wait_apart(eng, up, s, count):
    count = count if isinstance(count, int) else eng.to_reg(count)
    eng.wait_ge(up, 1)
    eng.wait_ge(s, count)


def rsqrt(nc, step, v, t, y):
    step.then_wait(nc.vector.tensor_scalar(y.bitcast(I32), v.bitcast(I32), 1, None, ALU.logical_shift_right))
    step.then_wait(nc.vector.tensor_scalar(y.bitcast(I32), y.bitcast(I32), -1.0, float(RSQRT_MAGIC), ALU.mult, ALU.add))
    for _ in range(NEWTON):
        step.then_wait(nc.vector.tensor_tensor(t, v, y, ALU.mult))
        step.then_wait(nc.vector.scalar_tensor_tensor(t, t, -0.5, y, ALU.mult, ALU.mult))
        step.then_wait(nc.vector.scalar_tensor_tensor(y, t, 1.5, y, ALU.add, ALU.mult))


STATS_STEPS = 4 + RSQRT_STEPS


def token_norm(nc, dve, step, src, dst, stat, squared, squares_wanted, squares_ready, k):
    s, m, v, t, y = (stat[:, i, :] for i in range(5))
    step.then_wait(nc.vector.tensor_reduce(s, src, AX.X, ALU.add))
    step.then_wait(nc.vector.tensor_scalar(m, s, 1.0 / D, None, ALU.mult))
    nc.vector.tensor_tensor(dst, src, m.unsqueeze(2).to_broadcast([P, NT, D]), ALU.subtract).then_inc(squares_wanted, 1)
    dve.wait_ge(squares_ready, k)
    step.then_wait(nc.vector.tensor_reduce(s, squared, AX.X, ALU.add))
    step.then_wait(nc.vector.tensor_scalar(v, s, 1.0 / D, EPS, ALU.mult, ALU.add))
    rsqrt(nc, step, v, t, y)
    return y.unsqueeze(2).to_broadcast([P, NT, D])


def build_global(nc, x1, X, idf, idb, stage, x, g_qk, g_v, g_bits, g_out, g_tr, g_trw, g_scal, bit_eye, g_mask,
                 ident, w_qkv, w_loaded):
    ctx = ExitStack()
    with ctx:
        def sb(name, shape, dt=F32):
            return ctx.enter_context(nc.sbuf_tensor("g_" + name, shape, dt))

        def sem(name):
            return ctx.enter_context(nc.semaphore("g_" + name))

        xin = sb("xin", [P, NT, D])
        squares = sb("squares", [P, NT, D])
        xnT = sb("xnT", [P, NT, P])
        xb = sb("xb", [P, 2, T])
        y = sb("y", [P, NT, D])
        stat = sb("stat", [P, 5, NT])
        qk = sb("qk", [P, 2 * GC, T])
        left = sb("left", [P, GC, T])
        bits = sb("bits", [P, T])
        val = sb("val", [P, TT, D])
        th = sb("th", [P, 2, GS])
        sc = sb("sc", [P, 2, GS])
        pr = sb("pr", [P, 2, GS])
        pT = sb("pT", [P, 2, 3, P])
        mx = sb("mx", [P, GH, TT])
        nmx = sb("nmx", [P, GH, TT])
        total = sb("total", [P, GH, TT])
        rtotal = sb("rtotal", [P, GH, TT])
        o = sb("o", [P, TT, GH, GD])
        oT = sb("oT", [P, T])
        scal = sb("scal", [P, 8])
        tw = sb("tw", [GH, 48])
        twT = sb("twT", [NTR, GH])
        tr = sb("tr", [NTR, NB, 2 * NB])
        wqk = sb("wqk", [P, 2 * GC, P])
        wv = sb("wv", [P, D])
        wbits = sb("wbits", [P, P])
        wout = sb("wout", [P, D])
        eye = sb("eye", [2 * NB, P])
        mix = sb("mix", [2 * NB, GC * P])
        mask = sb("mask", [P, GS], BF16)

        bank = [ctx.enter_context(nc.psum_tensor(f"g_bank{i}", [P, 512], F32)) for i in range(8)]

        x_loaded, id_loaded, w_in = sem("x_loaded"), sem("id_loaded"), sem("weights_loaded")
        dev_ready, squared, normed, step_s = sem("dev_ready"), sem("squared"), sem("normed"), sem("vector_step")
        xt_ready, xt_copied, cleared, mask_ready = sem("xT_ready"), sem("xT_copied"), sem("cleared"), sem("mask_ready")
        half_tanh, tw_shifted, tw_exp, tw_ready = sem("half_tanh"), sem("tw_shifted"), sem("tw_exp"), sem("tw_ready")
        twT_ready, twT_copied, mixed, mix_ready, scal_ready = sem("twT_ready"), sem("twT_copied"), sem("mixed"), sem("mix_ready"), sem("scal_ready")
        xb_ready, qk_ready, qk_copied = sem("xb_ready"), sem("qk_ready"), sem("qk_copied")
        bits_ready, bits_tanh, left_ready, left_copied = sem("bits_ready"), sem("bits_tanh"), sem("left_ready"), sem("left_copied")
        val_ready, val_copied = sem("val_ready"), sem("val_copied")
        raw_ready, raw_tanh, add_ready, scored, max_ready, exped = (
            sem("raw_ready"), sem("raw_tanh"), sem("addend_ready"), sem("scored"), sem("max_ready"), sem("exped"))
        pT_ready, pT_copied, o_ready, o_read = sem("pT_ready"), sem("pT_copied"), sem("o_ready"), sem("o_read")
        oT_ready, oT_copied, y_ready, y_copied = sem("oT_ready"), sem("oT_copied"), sem("y_ready"), sem("y_copied")

        raised = (scored, pT_ready, exped, raw_tanh, o_ready, pT_copied, oT_ready, y_copied, val_ready, o_read)
        LOADS = 9
        block = ctx.enter_context(nc.Block())

        @block.sync
        def _(sp):
            for s in raised:
                sp.sem_inc(s, UP)
            sp.dma_start(x1[:], x.rearrange("(n p) d -> p n d", p=P)).then_inc(x_loaded, 16)
            sp.dma_start(idf[:], ident).then_inc(id_loaded, 16)
            for dst, src in ((scal[:, 0:4], g_scal), (tw[:, 0:NTR], g_trw), (tr[:], g_tr), (eye[:], bit_eye),
                             (wqk[:], g_qk), (wbits[:], g_bits), (wv[:], g_v), (wout[:], g_out), (sc[:, 1, :], g_mask)):
                sp.dma_start(dst, src).then_inc(w_in, 16)
            sp.dma_start(stage[:], w_qkv[0]).then_inc(w_loaded, 16)

        @block.gpsimd
        def _(pool):
            nc.gpsimd.memset(X[:, :, 0:1], 0.0)
            nc.gpsimd.memset(mix[:], 0.0).then_inc(cleared, 1)
            pool.wait_ge(w_in, 16 * LOADS)
            pool.wait_ge(id_loaded, 16)
            nc.gpsimd.tensor_copy(idb[:], idf[:])
            nc.gpsimd.tensor_copy(mask[:], sc[:, 1, :]).then_inc(mask_ready, 1)
            pool.wait_ge(xt_copied, NT // 4)
            with pool.Fori(0, B // 2) as bb:
                for i in range(2):
                    b = bb * 2 + i
                    wait_apart(pool, cleared, val_ready, UP + (b - 1 if i else bb * 2))
                    nc.gpsimd.tensor_copy(xb[:, i, :], xnT[:, bass.ds(b * TT, TT), :].rearrange("p t k -> p (t k)")).then_inc(xb_ready, 1)

        @block.scalar
        def _(act):
            def square(k):
                act.wait_ge(dev_ready, k)
                nc.scalar.activation(squares[:], xin[:], ACT.Square).then_inc(squared, 1)

            square(1)
            act.wait_ge(w_in, 16 * LOADS)
            nc.scalar.activation(scal[:, 4:6], scal[:, 0:2], ACT.Tanh, scale=0.5).then_inc(half_tanh, 1)
            act.wait_ge(tw_shifted, 1)
            nc.scalar.activation(tw[:, 16:16 + NTR], tw[:, 8:8 + NTR], ACT.Exp, scale=1.0 / TEMP,
                                 accum_out=tw[:, 24:25]).then_inc(tw_exp, 1)
            for i in range(NT // 4):
                act.wait_ge(xt_ready, i + 1)
                nc.scalar.activation(xnT[:, 4 * i:4 * i + 4, :], bank[i % 2][:].rearrange("p (n k) -> p n k", n=4),
                                     ACT.Copy).then_inc(xt_copied, 1)
            act.wait_ge(scal_ready, 1)
            with act.Fori(0, B) as b:
                for c in range(2 * GC):
                    act.wait_ge(qk_ready, b * 2 * GC + c + 1)
                    nc.scalar.activation(qk[:, c, :], bank[c % 2][:, 0:T], ACT.Copy).then_inc(qk_copied, 1)
                act.wait_ge(bits_ready, b + 1)
                nc.scalar.activation(bits[:], bank[2][:, 0:T], ACT.Tanh).then_inc(bits_tanh, 1)
                act.wait_ge(val_ready, UP + b + 1)
                nc.scalar.activation(val[:], bank[3][:, 0:T].rearrange("p (t d) -> p t d", t=TT), ACT.Copy).then_inc(val_copied, 1)
                for c in range(GC):
                    act.wait_ge(left_ready, b * GC + c + 1)
                    nc.scalar.activation(left[:, c, :], bank[c % 2][:, 0:T], ACT.Copy).then_inc(left_copied, 1)

                def exps(h):
                    act.wait_ge(max_ready, b * GH + h + 1)
                    act.wait_ge(pT_ready, UP + b * GH + max(h - 1, 0))
                    nc.scalar.activation(pr[:, h % 2, 0:P], sc[:, h % 2, 0:P], ACT.Exp, bias=nmx[:, h, 0:1],
                                         accum_out=total[:, h, 0:1])
                    nc.scalar.activation(pr[:, h % 2, P:GS], sc[:, h % 2, P:GS], ACT.Exp, bias=nmx[:, h, 1:2],
                                         accum_out=total[:, h, 1:2]).then_inc(exped, 1)

                for h in range(GH):
                    act.wait_ge(raw_ready, b * GH + h + 1)
                    act.wait_ge(scored, UP + b * GH + max(h - 1, 0))
                    nc.scalar.activation(th[:, h % 2, :], bank[h % 2][:, 0:GS], ACT.Tanh, scale=scal[:, 6:7]).then_inc(raw_tanh, 1)
                    if h:
                        exps(h - 1)
                exps(GH - 1)
                act.wait_ge(oT_ready, UP + b + 1)
                nc.scalar.activation(oT[:], bank[7][:, 0:T], ACT.Copy).then_inc(oT_copied, 1)
                act.wait_ge(y_ready, b + 1)
                nc.scalar.activation(y[:, bass.ds(b * TT, TT), :], bank[7][:, T:2 * T].rearrange("p (t d) -> p t d", t=TT),
                                     ACT.Copy).then_inc(y_copied, 1)
            square(2)
            square(3)
            for i in range(NT // 4):
                act.wait_ge(xt_ready, NT // 4 + i + 1)
                nc.scalar.activation(X[:, 2 * i:2 * i + 2, 1:1 + T], bank[i % 2][:].rearrange("p (b t) -> p b t", b=2),
                                     ACT.Copy).then_inc(xt_copied, 1)

        @block.vector
        def _(dve):
            step = Steps(dve, step_s)
            dve.wait_ge(x_loaded, 16)
            r = token_norm(nc, dve, step, x1[:], xin[:], stat, squares[:], dev_ready, squared, 1)
            nc.vector.tensor_tensor(xin[:], xin[:], r, ALU.mult).then_inc(normed, 1)
            dve.wait_ge(w_in, 16 * LOADS)
            step.then_wait(nc.vector.tensor_reduce(tw[:, 25:26], tw[:, 0:NTR], AX.X, ALU.max))
            nc.vector.tensor_scalar(tw[:, 8:8 + NTR], tw[:, 0:NTR], tw[:, 25:26], None, ALU.subtract).then_inc(tw_shifted, 1)
            dve.wait_ge(tw_exp, 1)
            step.then_wait(nc.vector.reciprocal(tw[:, 26:27], tw[:, 24:25]))
            nc.vector.tensor_scalar(tw[:, 32:32 + NTR], tw[:, 16:16 + NTR], tw[:, 26:27], None, ALU.mult).then_inc(tw_ready, 1)
            dve.wait_ge(half_tanh, 1)
            nc.vector.tensor_scalar(scal[:, 4:5], scal[:, 4:5], 0.25, 0.25, ALU.mult, ALU.add)
            nc.vector.tensor_scalar(scal[:, 5:6], scal[:, 5:6], 1.0 / NB, 1.0 / NB, ALU.mult, ALU.add)
            nc.vector.reciprocal(scal[:, 6:7], scal[:, 3:4]).then_inc(scal_ready, 1)
            dve.wait_ge(scal_ready, 1)
            dve.wait_ge(twT_ready, 1)
            nc.vector.tensor_copy(twT[:], bank[7][0:NTR, 0:GH]).then_inc(twT_copied, 1)
            dve.wait_ge(mixed, 1)
            dve.wait_ge(cleared, 1)
            step.then_wait(nc.vector.tensor_scalar(mix[:].rearrange("p (h e) -> p h e", h=GH)[:, :, NB:2 * NB],
                                                   bank[6][0:2 * NB, 0:NB * GH].rearrange("p (e h) -> p h e", e=NB),
                                                   scal[0:2 * NB, 5:6], None, ALU.mult))
            for c in range(GC):
                last = nc.vector.scalar_tensor_tensor(mix[:, P * c:P * c + P], eye[:], scal[0:2 * NB, 4:5],
                                                      mix[:, P * c:P * c + P], ALU.mult, ALU.add)
            last.then_inc(mix_ready, 1)
            base = step.here
            BODY = GH + 1

            with dve.Fori(0, B) as b:
                step.body(base + b * BODY)

                def score(h):
                    dve.wait_ge(raw_tanh, UP + b * GH + h + 1)
                    dve.wait_ge(add_ready, b * GH + h + 1)
                    dve.wait_ge(exped, UP + b * GH + max(h - 1, 0))
                    nc.vector.scalar_tensor_tensor(sc[:, h % 2, :], th[:, h % 2, :], scal[:, 2:3], bank[2 + h % 2][:, 0:GS],
                                                   ALU.mult, ALU.add).then_inc(scored, 1)
                    dve.wait_ge(scored, UP + b * GH + h + 1)
                    nc.vector.tensor_reduce(mx[:, h, 0:1], sc[:, h % 2, 0:P], AX.X, ALU.max)
                    step.then_wait(nc.vector.tensor_reduce(mx[:, h, 1:2], sc[:, h % 2, P:GS], AX.X, ALU.max))
                    nc.vector.tensor_scalar(nmx[:, h, :], mx[:, h, :], -1.0, None, ALU.mult).then_inc(max_ready, 1)

                def copy_pT(h):
                    dve.wait_ge(pT_ready, UP + b * GH + h + 1)
                    dve.wait_ge(o_ready, UP + b * GH + max(h - 1, 0))
                    nc.vector.tensor_copy(pT[:, h % 2, :, :], bank[4 + h % 2][:, 0:GS].rearrange("p (t q) -> p t q", t=3)).then_inc(pT_copied, 1)

                for h in range(GH):
                    score(h)
                    if h:
                        copy_pT(h - 1)
                copy_pT(GH - 1)
                step.then_wait(nc.vector.reciprocal(rtotal[:], total[:]))
                dve.wait_ge(o_ready, UP + (b + 1) * GH)
                dve.wait_ge(oT_ready, UP + b)
                nc.vector.tensor_tensor(o[:], bank[6][:, 0:T].rearrange("p (t h d) -> p t h d", t=TT, h=GH),
                                        rtotal[:].rearrange("p h t -> p t h").unsqueeze(3).to_broadcast([P, TT, GH, GD]),
                                        ALU.mult).then_inc(o_read, 1)
                assert step.here == BODY
            step.body(base + B * BODY)
            dve.wait_ge(y_copied, UP + B)
            r = token_norm(nc, dve, step, y[:], xin[:], stat, squares[:], dev_ready, squared, 2)
            step.then_wait(nc.vector.tensor_tensor(xin[:], xin[:], r, ALU.mult))
            step.then_wait(nc.vector.tensor_tensor(x1[:], x1[:], xin[:], ALU.add))
            r = token_norm(nc, dve, step, x1[:], xin[:], stat, squares[:], dev_ready, squared, 3)
            nc.vector.tensor_tensor(xin[:], xin[:], r, ALU.mult).then_inc(normed, 1)

        @block.tensor
        def _(pe):
            mm = nc.tensor.matmul

            def to_features(k):
                for i in range(NT // 4):
                    if i >= 2:
                        pe.wait_ge(xt_copied, k * NT // 4 + i - 1)
                    for q in range(4):
                        last = nc.tensor.transpose(bank[i % 2][:, P * q:P * q + P], xin[:, 4 * i + q, :], idf[:])
                    last.then_inc(xt_ready, 1)

            pe.wait_ge(id_loaded, 16)
            pe.wait_ge(normed, 1)
            to_features(0)
            pe.wait_ge(tw_ready, 1)
            nc.tensor.transpose(bank[7][0:NTR, 0:GH], tw[:, 32:32 + NTR], idf[0:GH, 0:GH]).then_inc(twT_ready, 1)
            pe.wait_ge(w_in, 16 * LOADS)
            pe.wait_ge(twT_copied, 1)
            for e in range(NB):
                last = mm(bank[6][0:2 * NB, GH * e:GH * e + GH], tr[:, e, :], twT[:], start=True, stop=True)
            last.then_inc(mixed, 1)
            pe.wait_ge(mix_ready, 1)
            pe.wait_ge(mask_ready, 1)
            pe.wait_ge(xt_copied, NT // 4)

            with pe.Fori(0, B // 2) as bb:
                for i in range(2):
                    b = bb * 2 + i
                    xs = xb[:, i, :]
                    pe.wait_ge(xb_ready, b + 1)
                    pe.wait_ge(raw_tanh, UP + b * GH)
                    pe.wait_ge(scored, UP + b * GH)
                    for c in range(2 * GC):
                        if c >= 2:
                            pe.wait_ge(qk_copied, b * 2 * GC + c - 1)
                        mm(bank[c % 2][:, 0:T], wqk[:, c, :], xs, start=True, stop=True).then_inc(qk_ready, 1)
                    mm(bank[2][:, 0:T], wbits[:], xs, start=True, stop=True).then_inc(bits_ready, 1)
                    for t in range(TT):
                        last = mm(bank[3][:, D * t:D * t + D], xs[:, P * t:P * t + P], wv[:], start=True, stop=True)
                    last.then_inc(val_ready, 1)
                    pe.wait_ge(bits_tanh, b + 1)
                    for c in range(GC):
                        pe.wait_ge(qk_copied, b * 2 * GC + 2 * GC - 1 + min(c, 1))
                        if c >= 2:
                            pe.wait_ge(left_copied, b * GC + c - 1)
                        mm(bank[c % 2][:, 0:T], mix[:, P * c:P * c + P], bits[0:2 * NB, :], start=True, stop=True).then_inc(left_ready, 1)

                    def scores(h):
                        c, r0 = h // 4, 32 * (h % 4)
                        if h < 2:
                            pe.wait_ge(left_copied, (b + 1) * GC)
                            pe.wait_ge(val_copied, b + 1)
                        else:
                            pe.wait_ge(raw_tanh, UP + b * GH + h - 1)
                            pe.wait_ge(scored, UP + b * GH + h - 1)
                        q, k = qk[r0:r0 + GD, c, :], qk[r0:r0 + GD, GC + c, :]
                        mm(bank[h % 2][:, 0:P], q[:, 0:P], k[:, 0:P], start=True, stop=True, tile_position=(r0, 0))
                        mm(bank[h % 2][:, P:GS], q[:, P:T], k, start=True, stop=True, tile_position=(r0, 0)).then_inc(raw_ready, 1)
                        lf, rt = left[r0:r0 + 2 * NB, c, :], bits[r0:r0 + 2 * NB, :]
                        mm(bank[2 + h % 2][:, 0:GS], idb[:], mask[:], start=True, stop=False)
                        mm(bank[2 + h % 2][:, 0:P], lf[:, 0:P], rt[:, 0:P], start=False, stop=False, tile_position=(r0, 0))
                        mm(bank[2 + h % 2][:, P:GS], lf[:, P:T], rt, start=False, stop=True, tile_position=(r0, 0)).then_inc(add_ready, 1)

                    def transpose_probs(h):
                        pe.wait_ge(exped, UP + b * GH + h + 1)
                        pe.wait_ge(pT_copied, UP + b * GH + max(h - 1, 0))
                        for t in range(3):
                            last = nc.tensor.transpose(bank[4 + h % 2][:, P * t:P * t + P], pr[:, h % 2, P * t:P * t + P], idf[:])
                        last.then_inc(pT_ready, 1)

                    def weigh_values(h):
                        pe.wait_ge(pT_copied, UP + b * GH + h + 1)
                        if h == 0:
                            pe.wait_ge(o_read, UP + b)
                        at = GD * h
                        mm(bank[6][:, at:at + GD], pT[:, h % 2, 0, :], val[:, 0, at:at + GD], start=True, stop=True)
                        for t in range(TT):
                            last = mm(bank[6][:, D + at:D + at + GD], pT[:, h % 2, 1 + t, :], val[:, t, at:at + GD],
                                      start=t == 0, stop=t == TT - 1)
                        last.then_inc(o_ready, 1)

                    scores(0)
                    scores(1)
                    for h in range(GH):
                        transpose_probs(h)
                        if h + 2 < GH:
                            scores(h + 2)
                        weigh_values(h)
                    pe.wait_ge(o_read, UP + b + 1)
                    pe.wait_ge(y_copied, UP + b)
                    for t in range(TT):
                        last = nc.tensor.transpose(bank[7][:, P * t:P * t + P], o[:, t, :, :].rearrange("p h d -> p (h d)"), idf[:])
                    last.then_inc(oT_ready, 1)
                    pe.wait_ge(oT_copied, b + 1)
                    for t in range(TT):
                        last = mm(bank[7][:, T + D * t:T + D * t + D], oT[:, P * t:P * t + P], wout[:], start=True, stop=True)
                    last.then_inc(y_ready, 1)
            pe.wait_ge(normed, 2)
            to_features(1)


def build_layers(nc, x1, X, idf, idb, stage, w_loaded, w_qkv, qk_scale, w_o, ffn_par, w_1, w_2, rot, w_mask, pat, sel, out):
    ctx = ExitStack()
    with ctx:
        def sb(name, shape, dt=F32):
            return ctx.enter_context(nc.sbuf_tensor(name, shape, dt))

        def sem(name):
            return ctx.enter_context(nc.semaphore(name))

        WQ = 2 * INNER
        wh = sb("wh", [P, 3 * INNER], F32R)
        wl = sb("wl", [P, 3 * INNER], F32R)
        wsh = sb("wsh", [P, WQ], F32R)
        wsl = sb("wsl", [P, WQ], F32R)
        wo = sb("wo", [P, QC, D])
        w1 = sb("w1", [P, 2 * FC, P])
        w2 = sb("w2", [P, FC, D])
        fpar = sb("fpar", [P, 3 + 2 * FC])
        qks = sb("qks", [P, DEPTH, 4])
        rotb = sb("rotb", [P, 4, T])
        rots = sb("rots", [P, 4, T])
        xh = sb("xh", [P, WIN + T], F32R)
        xl = sb("xl", [P, WIN + T], F32R)
        xvh = sb("xvh", [P, NU, 2, KW], F32R)
        xvl = sb("xvl", [P, NU, 2, KW], F32R)
        sq = sb("sq", [P, 2, 2, T])
        patb = sb("patb", [P, 4 * H])
        selb = sb("sel", [2 * H, 2 * QC, P], F32R)
        part = sb("part", [P, 2 * QC, T])
        sinp = sb("sinp", [P, 2, 2, T])
        nrm = sb("nrm", [2 * H, 3, T])
        rh = sb("rh", [2 * H, T], F32R)
        rl = sb("rl", [2 * H, T], F32R)
        qT = sb("qT", [P, QC, T])
        kT = sb("kT", [P, QC, WIN + T])
        V = sb("V", [P, NU, H, VW])
        wmask = sb("wmask", [P, NW * KW], BF16)
        mx = sb("mx", [P, 2, NW])
        pr = sb("pr", [P, 2, NW * KW])
        pT = sb("pT", [P, 2, NU, P])
        rden = sb("rden", [P, TT, 4])
        O = sb("O", [P, TT, H, HD])
        OT = sb("OT", [P, QC, T])
        xf = sb("xf", [P, T])
        dev = sb("dev", [P, T])
        dsq = sb("dsq", [P, T])
        vn = sb("vn", [P, 3, T])
        xn = sb("xn", [P, T])
        mean1 = sb("mean1", [P, P])
        gl = sb("gl", [P, 2, T])
        hid = sb("hid", [P, FC, T])
        stat = sb("stat", [P, 5, NT])

        bank = [ctx.enter_context(nc.psum_tensor(f"bank{i}", [P, 512], F32)) for i in range(8)]
        NRM = bank[4][0:2 * H, 0:T]

        const_in, tail_in = sem("constants_loaded"), sem("tail_weights_loaded")
        cleared, wmask_ready, sel_ready = sem("cleared"), sem("wmask_ready"), sem("sel_ready")
        v_step, p_step = sem("vector_step"), sem("pool_step")
        w_high, w_low, rot_ready = sem("w_high"), sem("w_low"), sem("rot_ready")
        xs_ready, raw_ready, squared, turned, summed, norm_done, rn_ready = (
            sem("xs_ready"), sem("raw_ready"), sem("squared"), sem("turned"), sem("summed"), sem("norm_done"), sem("rnorm_ready"))
        v_ready, v_copied, rb_ready, scaled = sem("v_ready"), sem("v_copied"), sem("rbroadcast_ready"), sem("qk_scaled")
        s_ready, centered, exped, pt_ready, pt_copied, o_ready, o_read = (
            sem("scores_ready"), sem("centered"), sem("exped"), sem("pT_ready"), sem("pT_copied"), sem("o_ready"), sem("o_read"))
        ot_ready, ot_copied, y_ready, xf_ready = sem("oT_ready"), sem("oT_copied"), sem("y_ready"), sem("xf_ready")
        mean_ready, dev_ready, dsq_ready, var_ready, xn_ready = (
            sem("mean_ready"), sem("dev_ready"), sem("dsq_ready"), sem("var_ready"), sem("xn_ready"))
        h_ready, gelu_ready, hid_ready, y2_ready, x_updated = (
            sem("hidden_ready"), sem("gelu_ready"), sem("gated"), sem("ffn_ready"), sem("x_updated"))
        xt_ready, fdev_ready, fsquared, finished, stored = (
            sem("xT_ready"), sem("final_dev_ready"), sem("final_squared"), sem("finished"), sem("stored"))

        raised = (norm_done, summed, o_ready, pt_ready, ot_ready, y_ready, hid_ready, v_ready, x_updated, centered, pt_copied, o_read)
        CONSTS, TAILS = 5, 4
        partf = part[:].rearrange("p a t -> p (a t)")
        mask_in = part[:, 2 * QC - 2:2 * QC, :].rearrange("p a t -> p (a t)")
        sel_in = partf[0:2 * H, 0:2 * QC * P]
        fdev = partf[:, 0:NT * D].rearrange("p (n d) -> p n d", d=D)
        fy = partf[:, NT * D:2 * NT * D].rearrange("p (n d) -> p n d", d=D)
        fsq = stage[:, 0:NT * D].rearrange("p (n d) -> p n d", d=D)

        def swap(t):
            return t.rearrange("p (h s d) -> p h s d", s=2, d=HD // 2)

        def pair(t):
            return t.rearrange("p (a t) -> p a t", a=2)

        block = ctx.enter_context(nc.Block())

        @block.sync
        def _(sp):
            for s in raised:
                sp.sem_inc(s, UP)
            for dst, src in ((rotb[:], rot), (qks[:], qk_scale), (mask_in, w_mask), (patb[:], pat), (sel_in, sel)):
                sp.dma_start(dst, src).then_inc(const_in, 16)

            def load_tail(l):
                for dst, src in ((wo[:], w_o), (w1[:], w_1), (w2[:], w_2), (fpar[:], ffn_par)):
                    sp.dma_start(dst, src[l]).then_inc(tail_in, 16)

            load_tail(0)
            with sp.Fori(1, DEPTH) as l:
                sp.wait_ge(w_low, l)
                sp.dma_start(stage[:], w_qkv[l]).then_inc(w_loaded, 16)
                sp.wait_ge(x_updated, UP + l * B)
                load_tail(l)

        @block.gpsimd
        def _(pool):
            step = Steps(pool, p_step)
            nc.gpsimd.memset(mean1[:], 1.0 / D)
            nc.gpsimd.memset(V[:, :, :, HD:VW], 1.0)
            nc.gpsimd.memset(kT[:, :, 0:WIN], 0.0)
            nc.gpsimd.memset(xh[:, 0:WIN].bitcast(F32), 0.0)
            nc.gpsimd.memset(xl[:, 0:WIN].bitcast(F32), 0.0).then_inc(cleared, 1)
            pool.wait_ge(cleared, 1)
            pool.wait_ge(const_in, 16 * CONSTS)
            nc.gpsimd.tensor_copy(wmask[:], mask_in).then_inc(wmask_ready, 1)
            pool.wait_ge(wmask_ready, 1)
            nc.gpsimd.tensor_copy(selb[:].rearrange("p c m -> p (c m)"), sel_in).then_inc(sel_ready, 1)
            pool.wait_ge(sel_ready, 1)
            BODY = 2

            def prepare(n, b):
                step.body(n * BODY)
                wait_apart(pool, cleared, v_ready, UP + n * NV)
                nc.gpsimd.tensor_copy(xh[0:64, WIN:WIN + T], X[0:64, b, 1:1 + T])
                step.then_wait(nc.gpsimd.tensor_copy(xh[64:P, WIN:WIN + T], X[64:P, b, 0:T]), cleared)
                nc.gpsimd.tensor_tensor(xl[0:64, WIN:WIN + T], X[0:64, b, 1:1 + T], xh[0:64, WIN:WIN + T].bitcast(F32), ALU.subtract)
                step.then_wait(nc.gpsimd.tensor_tensor(xl[64:P, WIN:WIN + T], X[64:P, b, 0:T], xh[64:P, WIN:WIN + T].bitcast(F32), ALU.subtract), cleared)
                for src, dst in ((xh, xvh), (xl, xvl)):
                    for half in range(2):
                        last = nc.gpsimd.tensor_copy(dst[:, :, half, :], src[:, WIN * half:WIN * half + T].bitcast(F32).rearrange("p (u k) -> p u k", u=NU))
                last.then_inc(xs_ready, 1)

            def add_parts(n):
                for p in range(NP):
                    pool.wait_ge(turned, n * NP + p + 1)
                    nc.gpsimd.tensor_tensor(part[:, 2 * p:2 * p + 2, :], part[:, 2 * p:2 * p + 2, :], sinp[:, p % 2, :, :],
                                            ALU.add).then_inc(summed, 1)

            with pool.Fori(0, DEPTH) as l:
                with pool.Fori(0, B) as b:
                    n = l * B + b
                    wait_apart(pool, cleared, x_updated, UP + n)
                    prepare(n, b)
                    add_parts(n)
                    assert step.here == BODY

        @block.scalar
        def _(act):
            def split_high(l):
                act.wait_ge(w_loaded, 16 * (l + 1))
                act.wait_ge(v_ready, UP + l * B * NV)
                nc.scalar.activation(wh[:], stage[:], ACT.Copy)
                nc.scalar.activation(swap(wsh[:])[:, :, 0, :], swap(stage[:, 0:WQ])[:, :, 1, :], ACT.Copy)
                nc.scalar.activation(swap(wsh[:])[:, :, 1, :], swap(stage[:, 0:WQ])[:, :, 0, :], ACT.Copy).then_inc(w_high, 1)

            def squares(n):
                for p in range(NP):
                    act.wait_ge(raw_ready, n * NP + p + 1)
                    act.wait_ge(norm_done, UP + n * NP + max(p - 1, 0))
                    nc.scalar.activation(sq[:, p % 2, :, :], pair(bank[2 + p % 2][:]), ACT.Square).then_inc(squared, 1)

            def copy_values(n):
                act.wait_ge(o_ready, UP + n * NG)
                for j in range(NV):
                    act.wait_ge(v_ready, UP + n * NV + j + 1)
                    u, half = j // 2, j % 2
                    nc.scalar.activation(V[:, u, 8 * half:8 * half + 8, 0:HD], bank[j % 4][:].rearrange("p (h d) -> p h d", d=HD),
                                         ACT.Copy).then_inc(v_copied, 1)

            def probs(n, g):
                act.wait_ge(centered, UP + n * NG + g + 1)
                nc.scalar.activation(pr[:, g % 2, :], pr[:, g % 2, :], ACT.Exp, scale=QK_SCALE).then_inc(exped, 1)

            def copy_pT(n, g):
                act.wait_ge(pt_ready, UP + n * NG + g + 1)
                act.wait_ge(o_ready, UP + n * NG + max(g - 1, 0))
                nc.scalar.activation(pT[:, g % 2, :, :], bank[2 + g % 2][:].rearrange("p (u q) -> p u q", u=NU), ACT.Copy).then_inc(pt_copied, 1)

            def copy_oT(n):
                act.wait_ge(y_ready, UP + n)
                for m in range(4):
                    act.wait_ge(ot_ready, UP + n * 4 + m + 1)
                    i, c = m // 2, 4 * (m % 2)
                    nc.scalar.activation(OT[:, c:c + 4, P * i:P * i + P], bank[6 + m % 2][:].rearrange("p (c q) -> p c q", c=4),
                                         ACT.Copy).then_inc(ot_copied, 1)

            def square_dev(n):
                act.wait_ge(dev_ready, n + 1)
                nc.scalar.activation(dsq[:], dev[:], ACT.Square).then_inc(dsq_ready, 1)

            def gelu(n):
                for j in range(FC):
                    act.wait_ge(h_ready, n * FC + j + 1)
                    act.wait_ge(hid_ready, UP + n * FC + max(j - 1, 0))
                    nc.scalar.activation(gl[:, j % 2, :], bank[7 - j % 2][:, 0:T], ACT.Gelu, bias=fpar[:, 3 + FC + j:4 + FC + j]).then_inc(gelu_ready, 1)

            with act.Fori(0, DEPTH) as l:
                split_high(l)
                with act.Fori(0, B) as b:
                    n = l * B + b
                    squares(n)
                    copy_values(n)
                    for g in range(NG):
                        probs(n, g)
                        copy_pT(n, g)
                    copy_oT(n)
                    square_dev(n)
                    act.wait_ge(tail_in, 16 * TAILS * (l + 1))
                    gelu(n)
            act.wait_ge(fdev_ready, 1)
            nc.scalar.activation(fsq, fdev, ACT.Square).then_inc(fsquared, 1)
            act.wait_ge(finished, 1)
            act.dma_start(out.rearrange("(n p) d -> p n d", p=P), x1[:]).then_inc(stored, 16)
            act.wait_ge(stored, 16)

        @block.vector
        def _(dve):
            step = Steps(dve, v_step)

            def split_low(l):
                dve.wait_ge(w_high, l + 1)
                nc.vector.tensor_tensor(wl[:], stage[:], wh[:].bitcast(F32), ALU.subtract)
                for s in range(2):
                    last = nc.vector.tensor_tensor(swap(wsl[:])[:, :, s, :], swap(stage[:, 0:WQ])[:, :, 1 - s, :],
                                                   swap(wsh[:].bitcast(F32))[:, :, s, :], ALU.subtract)
                last.then_inc(w_low, 1)
                for k in range(4):
                    last = nc.vector.tensor_scalar(rots[:, k, :], rotb[:, k, :], qks[:, bass.ds(l, 1), k:k + 1].rearrange("p l k -> p (l k)"), None, ALU.mult)
                last.then_inc(rot_ready, 1)
                wait_apart(dve, cleared, rot_ready, l + 1)

            def rotate(n):
                for p in range(NP):
                    k = 0 if p < NP // 2 else 2
                    dve.wait_ge(raw_ready, n * NP + p + 1)
                    nc.vector.tensor_tensor(part[:, 2 * p:2 * p + 2, :], pair(bank[p % 2][:]),
                                            rots[:, k, :].unsqueeze(1).to_broadcast([P, 2, T]), ALU.mult)
                    dve.wait_ge(squared, n * NP + p + 1)
                    dve.wait_ge(summed, UP + n * NP + max(p - 1, 0))
                    nc.vector.tensor_tensor(sinp[:, p % 2, :, :], pair(bank[2 + p % 2][:]),
                                            rots[:, k + 1, :].unsqueeze(1).to_broadcast([P, 2, T]), ALU.mult).then_inc(turned, 1)

            def norms(n):
                dve.wait_ge(norm_done, UP + (n + 1) * NP)
                v, t, y = nrm[:, 0, :], nrm[:, 1, :], nrm[:, 2, :]
                step.then_wait(nc.vector.tensor_scalar(v, NRM, NORM_FLOOR, None, ALU.max))
                rsqrt(nc, step, v, t, y)
                step.then_wait(nc.vector.tensor_copy(rh[:], y))
                nc.vector.tensor_tensor(rl[:], y, rh[:].bitcast(F32), ALU.subtract).then_inc(rn_ready, 1)

            def scale(n):
                for p in range(NP):
                    dve.wait_ge(rb_ready, n * NP + p + 1)
                    dve.wait_ge(summed, UP + n * NP + p + 1)
                    dst = qT[:, 2 * p:2 * p + 2, :] if p < NP // 2 else kT[:, 2 * p - QC:2 * p - QC + 2, WIN:WIN + T]
                    nc.vector.tensor_tensor(dst, part[:, 2 * p:2 * p + 2, :], pair(bank[p % 4][:]), ALU.mult).then_inc(scaled, 1)

            def center(n, g):
                dve.wait_ge(s_ready, n * NG + g + 1)
                dve.wait_ge(pt_ready, UP + n * NG + max(g - 1, 0))
                s3 = bank[g % 2][:].rearrange("p (w k) -> p w k", w=NW)
                step.then_wait(nc.vector.tensor_reduce(mx[:, g % 2, :], s3, AX.X, ALU.max))
                nc.vector.tensor_tensor(pr[:, g % 2, :].rearrange("p (w k) -> p w k", w=NW), s3,
                                        mx[:, g % 2, :].unsqueeze(2).to_broadcast([P, NW, KW]), ALU.subtract).then_inc(centered, 1)

            def take_o(n, g):
                dve.wait_ge(o_ready, UP + n * NG + g + 1)
                dve.wait_ge(ot_ready, UP + n * 4)
                ov = [bank[4 + i][:, 0:4 * VW].rearrange("p (h v) -> p h v", h=4) for i in range(TT)]
                for i in range(TT):
                    last = nc.vector.reciprocal(rden[:, i, :].unsqueeze(2), ov[i][:, :, HD:VW])
                step.then_wait(last)
                for i in range(TT):
                    last = nc.vector.tensor_tensor(O[:, i, 4 * g:4 * g + 4, :], ov[i][:, :, 0:HD],
                                                   rden[:, i, :].unsqueeze(2).to_broadcast([P, 4, HD]), ALU.mult)
                last.then_inc(o_read, 1)

            def add_attention(n, b):
                dve.wait_ge(y_ready, UP + n + 1)
                step.then_wait(nc.vector.tensor_tensor(X[:, b, 1:1 + T], X[:, b, 1:1 + T], bank[6][:, 0:T], ALU.add), cleared)
                nc.vector.tensor_copy(xf[0:64, :], X[0:64, b, 1:1 + T])
                nc.vector.tensor_copy(xf[64:P, :], X[64:P, b, 0:T]).then_inc(xf_ready, 1)
                dve.wait_ge(xf_ready, n + 1)

            def layernorm(n):
                dve.wait_ge(mean_ready, n + 1)
                nc.vector.tensor_tensor(dev[:], xf[:], bank[7][:, 0:T], ALU.subtract).then_inc(dev_ready, 1)
                dve.wait_ge(var_ready, n + 1)
                v, t, y = vn[:, 0, :], vn[:, 1, :], vn[:, 2, :]
                step.then_wait(nc.vector.tensor_scalar(v, bank[6][:, 0:T], EPS, None, ALU.add))
                rsqrt(nc, step, v, t, y)
                step.then_wait(nc.vector.tensor_tensor(t, dev[:], y, ALU.mult))
                nc.vector.tensor_scalar(xn[:], t, fpar[:, 0:1], fpar[:, 1:2], ALU.mult, ALU.add).then_inc(xn_ready, 1)

            def gate(n):
                for j in range(FC):
                    dve.wait_ge(gelu_ready, n * FC + j + 1)
                    nc.vector.scalar_tensor_tensor(hid[:, j, :], bank[7 - j % 2][:, T:2 * T], fpar[:, 3 + j:4 + j], gl[:, j % 2, :],
                                                   ALU.add, ALU.mult).then_inc(hid_ready, 1)

            def add_ffn(n, b):
                dve.wait_ge(y2_ready, n + 1)
                nc.vector.scalar_tensor_tensor(X[:, b, 1:1 + T], bank[6][:, 0:T], fpar[:, 2:3], X[:, b, 1:1 + T],
                                               ALU.add, ALU.add).then_inc(x_updated, 1)

            dve.wait_ge(const_in, 16 * CONSTS)
            dve.wait_ge(cleared, 1)
            BODY = (1 + RSQRT_STEPS + 1) + 2 * NG + 1 + (1 + RSQRT_STEPS + 1)
            with dve.Fori(0, DEPTH) as l:
                split_low(l)
                with dve.Fori(0, B) as b:
                    n = l * B + b
                    step.body(n * BODY)
                    rotate(n)
                    norms(n)
                    scale(n)
                    for g in range(NG):
                        center(n, g)
                        if g:
                            take_o(n, g - 1)
                    take_o(n, NG - 1)
                    add_attention(n, b)
                    dve.wait_ge(tail_in, 16 * TAILS * (l + 1))
                    layernorm(n)
                    gate(n)
                    add_ffn(n, b)
                    assert step.here == BODY
            step.body(DEPTH * B * BODY)
            for i in range(NT // 4):
                dve.wait_ge(xt_ready, i + 1)
                step.then_wait(nc.vector.tensor_copy(fy[:, 4 * i:4 * i + 4, :], bank[i][:].rearrange("p (n d) -> p n d", n=4)))
            r = token_norm(nc, dve, step, fy, fdev, stat, fsq, fdev_ready, fsquared, 1)
            step.then_wait(nc.vector.tensor_tensor(fdev, fdev, r, ALU.mult))
            nc.vector.tensor_tensor(x1[:], x1[:], fdev, ALU.add).then_inc(finished, 1)

        @block.tensor
        def _(pe):
            mm = nc.tensor.matmul

            def raw(n, p):
                if p >= 2:
                    pe.wait_ge(turned, n * NP + p - 1)
                for t, (hi, lo) in enumerate(((wh, wl), (wsh, wsl))):
                    for a in range(2):
                        c = 2 * p + a
                        ps = bank[2 * t + p % 2][:, T * a:T * a + T]
                        w_hi, w_lo = hi[:, P * c:P * c + P], lo[:, P * c:P * c + P]
                        mm(ps, w_hi, xh[:, WIN:], start=True, stop=False)
                        mm(ps, w_hi, xl[:, WIN:], start=False, stop=False)
                        last = mm(ps, w_lo, xh[:, WIN:], start=False, stop=True)
                last.then_inc(raw_ready, 1)

            def gather_norms(n, p):
                pe.wait_ge(squared, n * NP + p + 1)
                if p == 0:
                    pe.wait_ge(o_read, UP + n * NG)
                for a in range(2):
                    c = 2 * p + a
                    last = mm(NRM, patb[:, 2 * H - 2 * c:4 * H - 2 * c], sq[:, p % 2, a, :], start=c == 0, stop=c == 2 * QC - 1)
                last.then_inc(norm_done, 1)

            def values(n, j):
                if j < 4:
                    pe.wait_ge(turned, (n + 1) * NP)
                else:
                    pe.wait_ge(v_copied, n * NV + j - 3)
                u, half = j // 2, j % 2
                ps = bank[j % 4][:]
                at = 2 * INNER + 512 * half
                x_hi, x_lo = xvh[:, u, :, :].rearrange("p s k -> p (s k)"), xvl[:, u, :, :].rearrange("p s k -> p (s k)")
                mm(ps, x_hi, wh[:, at:at + 512], start=True, stop=False)
                mm(ps, x_hi, wl[:, at:at + 512], start=False, stop=False)
                mm(ps, x_lo, wh[:, at:at + 512], start=False, stop=True).then_inc(v_ready, 1)

            def spread_norms(n, p):
                if p < 4:
                    pe.wait_ge(v_copied, n * NV + NV - 3 + p)
                else:
                    pe.wait_ge(scaled, n * NP + p - 3)
                for a in range(2):
                    c = 2 * p + a
                    ps = bank[p % 4][:, T * a:T * a + T]
                    mm(ps, selb[:, c, :], rh[:], start=True, stop=False)
                    last = mm(ps, selb[:, c, :], rl[:], start=False, stop=True)
                last.then_inc(rb_ready, 1)

            def project(n):
                pe.wait_ge(xs_ready, n + 1)
                pe.wait_ge(centered, UP + n * NG)
                pe.wait_ge(pt_copied, UP + n * NG)
                for p in range(NP):
                    raw(n, p)
                    if p:
                        gather_norms(n, p - 1)
                gather_norms(n, NP - 1)
                for j in range(NV):
                    values(n, j)
                pe.wait_ge(rn_ready, n + 1)
                for p in range(NP):
                    spread_norms(n, p)

            def scores(n, g):
                if g >= 2:
                    pe.wait_ge(centered, UP + n * NG + g - 1)
                ps = bank[g % 2]
                mm(ps[:], idb[:], wmask[:], start=True, stop=False)
                for w in range(NW):
                    for j in range(4):
                        h = 4 * g + j
                        r0, c = HD * (h % 2), h // 2
                        last = mm(ps[WIN * j:WIN * j + WIN, KW * w:KW * w + KW], qT[r0:r0 + HD, c, WIN * w:WIN * w + WIN],
                                  kT[r0:r0 + HD, c, WIN * w:WIN * w + KW], start=False, stop=w == NW - 1, tile_position=(r0, WIN * j))
                last.then_inc(s_ready, 1)

            def transpose_probs(n, g):
                pe.wait_ge(exped, n * NG + g + 1)
                if g >= 2:
                    pe.wait_ge(pt_copied, UP + n * NG + g - 1)
                for u in range(NU):
                    last = nc.tensor.transpose(bank[2 + g % 2][:, P * u:P * u + P], pr[:, g % 2, P * u:P * u + P], idf[:])
                last.then_inc(pt_ready, 1)

            def weigh_values(n, g):
                wait_apart(pe, cleared, pt_copied, UP + n * NG + g + 1)
                pe.wait_ge(o_read, UP + n * NG + g)
                for w in range(NW):
                    r0, u, i, q = KW * (w % 2), w // 2, w // 4, WIN * (w % 4)
                    for j in range(4):
                        last = mm(bank[4 + i][q:q + WIN, VW * j:VW * j + VW], pT[r0:r0 + KW, g % 2, u, WIN * j:WIN * j + WIN],
                                  V[r0:r0 + KW, u, 4 * g + j, :], start=True, stop=True, tile_position=(r0, q))
                last.then_inc(o_ready, 1)

            def attend(n):
                pe.wait_ge(scaled, (n + 1) * NP)
                scores(n, 0)
                scores(n, 1)
                for g in range(NG):
                    transpose_probs(n, g)
                    if g + 2 < NG:
                        scores(n, g + 2)
                    weigh_values(n, g)

            def transpose_o(n, m):
                if m >= 2:
                    pe.wait_ge(ot_copied, n * 4 + m - 1)
                i, c0 = m // 2, 4 * (m % 2)
                for k in range(4):
                    c = c0 + k
                    last = nc.tensor.transpose(bank[6 + m % 2][:, P * k:P * k + P], O[:, i, 2 * c:2 * c + 2, :].rearrange("p h d -> p (h d)"), idf[:])
                last.then_inc(ot_ready, 1)

            def tail(n, l):
                pe.wait_ge(o_read, UP + (n + 1) * NG)
                pe.wait_ge(x_updated, UP + n)
                for m in range(4):
                    transpose_o(n, m)
                pe.wait_ge(tail_in, 16 * TAILS * (l + 1))
                pe.wait_ge(ot_copied, (n + 1) * 4)
                for c in range(QC):
                    last = mm(bank[6][:, 0:T], wo[:, c, :], OT[:, c, :], start=c == 0, stop=c == QC - 1)
                last.then_inc(y_ready, 1)
                pe.wait_ge(xf_ready, n + 1)
                mm(bank[7][:, 0:T], mean1[:], xf[:], start=True, stop=True).then_inc(mean_ready, 1)
                pe.wait_ge(dsq_ready, n + 1)
                mm(bank[6][:, 0:T], mean1[:], dsq[:], start=True, stop=True).then_inc(var_ready, 1)
                pe.wait_ge(xn_ready, n + 1)
                for j in range(FC):
                    if j >= 2:
                        pe.wait_ge(hid_ready, UP + n * FC + j - 1)
                    mm(bank[7 - j % 2][:, 0:T], w1[:, FC + j, :], xn[:], start=True, stop=True)
                    mm(bank[7 - j % 2][:, T:2 * T], w1[:, j, :], xn[:], start=True, stop=True).then_inc(h_ready, 1)
                pe.wait_ge(hid_ready, UP + (n + 1) * FC)
                for j in range(FC):
                    last = mm(bank[6][:, 0:T], w2[:, j, :], hid[:, j, :], start=j == 0, stop=j == FC - 1)
                last.then_inc(y2_ready, 1)

            pe.wait_ge(sel_ready, 1)
            pe.wait_ge(const_in, 16 * CONSTS)
            with pe.Fori(0, DEPTH) as l:
                wait_apart(pe, cleared, w_low, l + 1)
                with pe.Fori(0, B) as b:
                    n = l * B + b
                    project(n)
                    attend(n)
                    tail(n, l)
            pe.wait_ge(x_updated, UP + DEPTH * B)
            for i in range(NT // 4):
                for q in range(4):
                    t = 4 * i + q
                    last = nc.tensor.transpose(bank[i][:, P * q:P * q + P], X[:, t // TT, 1 + P * (t % TT):1 + P * (t % TT) + P], idf[:])
                last.then_inc(xt_ready, 1)


def build(nc, a, out):
    with ExitStack() as ctx:
        def sb(name, shape, dt=F32):
            return ctx.enter_context(nc.sbuf_tensor(name, shape, dt))

        x1 = sb("x1", [P, NT, D])
        X = sb("X", [P, B, 1 + T])
        idf = sb("idf", [P, P])
        idb = sb("idb", [P, P], BF16)
        stage = sb("stage", [P, 3 * INNER])
        w_loaded = ctx.enter_context(nc.semaphore("w_loaded"))
        build_global(nc, x1, X, idf, idb, stage, a["x"], a["g_qk"], a["g_v"], a["g_bits"], a["g_out"], a["g_tr"], a["g_trw"],
                     a["g_scal"], a["bit_eye"], a["g_mask"], a["ident"], a["w_qkv"], w_loaded)
        build_layers(nc, x1, X, idf, idb, stage, w_loaded, a["w_qkv"], a["qk_scale"], a["w_o"], a["ffn_par"], a["w_1"], a["w_2"],
                     a["rot"], a["w_mask"], a["pat"], a["sel"], out)


def constants():
    f = np.float32
    neg = -1e37
    q = np.arange(P)
    g_mask = np.zeros((P, GS), f)
    g_mask[:, 0:P] = np.where(q[None, :] > q[:, None], neg, 0)
    g_mask[:, P:] = np.where(np.arange(T)[None, :] > q[:, None] + P, neg, 0)
    a, j = np.arange(P)[:, None, None] % WIN, np.arange(KW)[None, None, :]
    w = np.arange(NW)[None, :, None]
    seen = (j >= a) & (j <= a + WIN) & ((w > 0) | (j >= WIN))
    w_mask = np.where(seen, 0, neg).astype(f).reshape(P, NW * KW)
    bit_eye = np.zeros((2 * NB, P), f)
    for i in range(NB):
        bit_eye[i, i::32] = 1
    pat = np.zeros((P, 4 * H), f)
    pat[q, 2 * H + q // HD] = 1
    sel = (np.arange(2 * QC * P)[None, :] // HD == np.arange(2 * H)[:, None]).astype(f)
    half = np.arange(0, HD, 2, dtype=f)
    inv_freq = (f(1.0) / np.power(f(10000.0), half / f(HD))).astype(f)
    t = np.arange(T, dtype=f)
    freqs = (inv_freq[:, None] * t[None, :]).astype(f)
    base = ((half + f(0.4 * HD)) / f(1.4 * HD)).astype(f)
    scale = np.power(base[:, None].astype(np.float64), ((t - T // 2) / f(WIN // 2))[None, :].astype(np.float64))
    cos, sin = np.cos(freqs.astype(np.float64)), np.sin(freqs.astype(np.float64))

    def over_heads(lo, hi):
        return np.tile(np.concatenate([lo, hi], 0), (2, 1)).astype(f)

    rot = np.stack([over_heads(cos * scale, cos * scale), over_heads(-sin * scale, sin * scale),
                    over_heads(cos / scale, cos / scale), over_heads(-sin / scale, sin / scale)], 1)
    return dict(g_mask=g_mask, w_mask=w_mask, ident=np.eye(P, dtype=f), bit_eye=bit_eye, pat=pat, sel=sel, rot=np.ascontiguousarray(rot))


def lay_out(i):
    f = np.float32
    i = {k: np.asarray(v) for k, v in i.items()}
    a = dict(x=i["L0_attn_x"].reshape(B * T, D))
    wt = i["L0_attn_qkv_w"].T
    g_qk = np.zeros((P, 2 * GC, 4, 32), f)
    g_qk[:, :, :, 0:GD] = wt[:, 0:2 * D].reshape(P, 2 * GC, 4, GD)
    a["g_qk"] = g_qk.reshape(P, 2 * GC, P)
    a["g_v"] = wt[:, 2 * D:]
    g_bits = np.zeros((P, 4, 32), f)
    g_bits[:, :, 0:NB] = i["L0_attn_hex_w"].T[:, None, :]
    g_bits[:, :, NB:2 * NB] = i["L0_attn_q6_w"].T[:, None, :]
    a["g_bits"] = g_bits.reshape(P, P)
    a["g_out"] = i["L0_attn_out_w"].T
    g_tr = np.zeros((NTR, NB, 2 * NB), f)
    g_tr[:, :, NB:] = i["L0_attn_transforms"].transpose(0, 2, 1)
    a["g_tr"] = g_tr
    a["g_trw"] = i["L0_attn_transform_weights"]
    scal = [i["L0_attn_hamming_lambda_logit"], i["L0_attn_scale_logit"], i["L0_attn_sips_alpha"], i["L0_attn_sips_beta"]]
    a["g_scal"] = np.broadcast_to(np.concatenate([s.reshape(1) for s in scal])[None, :], (P, 4))
    a["w_qkv"] = i["L0_ffn_Wqkv"]
    swapped = (np.arange(HD) + HD // 2) % HD
    cols = [i["L0_ffn_q_scale"], i["L0_ffn_q_scale"][:, swapped], i["L0_ffn_k_scale"], i["L0_ffn_k_scale"][:, swapped]]
    a["qk_scale"] = np.tile(np.stack([c.T for c in cols], 2), (2, 1, 1))
    a["w_o"] = i["L0_ffn_Wo"].reshape(DEPTH, QC, P, D).transpose(0, 2, 1, 3)
    w_1 = np.zeros((DEPTH, D, 2, FC * P), f)
    w_1[:, :, :, 0:DIN] = i["L0_ffn_W1"].reshape(DEPTH, D, 2, DIN)
    a["w_1"] = w_1.reshape(DEPTH, D, 2 * FC, P)
    w_2 = np.zeros((DEPTH, FC * P, D), f)
    w_2[:, 0:DIN] = i["L0_ffn_W2"]
    a["w_2"] = w_2.reshape(DEPTH, FC, P, D).transpose(0, 2, 1, 3)
    b_1 = np.zeros((DEPTH, 2, FC * P), f)
    b_1[:, :, 0:DIN] = i["L0_ffn_b1"].reshape(DEPTH, 2, DIN)
    par = np.zeros((DEPTH, P, 3 + 2 * FC), f)
    par[:, :, 0], par[:, :, 1], par[:, :, 2] = i["L0_ffn_ln_g"], i["L0_ffn_ln_b"], i["L0_ffn_b2"]
    par[:, :, 3:] = b_1.reshape(DEPTH, 2 * FC, P).transpose(0, 2, 1)
    a["ffn_par"] = par
    return a


def kernel(**inputs):
    import concourse.bacc as bacc
    from concourse.bass_utils import run_bass_kernel_spmd

    nc = bacc.Bacc("TRN2", target_bir_lowering=False, num_devices=1)
    arrays = {k: np.ascontiguousarray(v) for k, v in {**lay_out(inputs), **constants()}.items()}
    aps = {k: nc.dram_tensor(k + "_dram", v.shape, mybir.dt.from_np(v.dtype), kind="ExternalInput").ap() for k, v in arrays.items()}
    out = nc.dram_tensor("out_dram", (B * T, D), F32, kind="ExternalOutput").ap()
    build(nc, aps, out)
    r = run_bass_kernel_spmd(nc, [{k + "_dram": v for k, v in arrays.items()}], core_ids=[0])
    return r.results[0]["out_dram"].reshape(B, T, D)
```

```python
from contextlib import ExitStack

import numpy as np
import concourse.bass as bass
from concourse import mybir

F32 = mybir.dt.float32
F32R = mybir.dt.float32r
BF16 = mybir.dt.bfloat16
I32 = mybir.dt.int32
ALU = mybir.AluOpType
ACT = mybir.ActivationFunctionType
AX = mybir.AxisListType

P = 128
B, T, D = 8, 256, 128
NT = B * T // P
TT = T // P
GH = 16
GD = D // GH
GC = GH // 4
NTR, NB = 7, 6
TEMP = 0.5
GS = P + T
DEPTH, H, HD, WIN = 6, 16, 64, 32
INNER = H * HD
DIN = D * 4 * 2 // 3
FC = -(-DIN // P)
NU = T // WIN // 2
QW = 2 * WIN
KW = 3 * WIN
QC = INNER // P
NP = QC
NV = 2 * NU
NO = 4
NS = H // 2
VW = HD + 1
QK_SCALE = 8.0
EPS = 1e-5
RSQRT_MAGIC = 0x5F3759DF
NEWTON = 3
RSQRT_STEPS = 2 + 3 * NEWTON
UP = 1
NORM_FLOOR = 1e-24


class Steps:

    def __init__(self, eng, s):
        self.eng, self.s, self.before, self.here = eng, s, 0, 0

    def body(self, before):
        self.before, self.here = before, 0

    def then_wait(self, ins, apart=None):
        self.here += 1
        ins.then_inc(self.s, 1)
        if apart is None:
            self.eng.wait_ge(self.s, self.before + self.here)
        else:
            wait_apart(self.eng, apart, self.s, self.before + self.here)


def wait_apart(eng, up, s, count):
    count = count if isinstance(count, int) else eng.to_reg(count)
    eng.wait_ge(up, 1)
    eng.wait_ge(s, count)


def rsqrt(nc, step, v, t, y, ready=None):
    step.then_wait(nc.vector.tensor_scalar(y.bitcast(I32), v.bitcast(I32), 1, None, ALU.logical_shift_right))
    step.then_wait(nc.vector.tensor_scalar(y.bitcast(I32), y.bitcast(I32), -1.0, float(RSQRT_MAGIC), ALU.mult, ALU.add))
    for k in range(NEWTON):
        step.then_wait(nc.vector.tensor_tensor(t, v, y, ALU.mult))
        step.then_wait(nc.vector.scalar_tensor_tensor(t, t, -0.5, y, ALU.mult, ALU.mult))
        last = nc.vector.scalar_tensor_tensor(y, t, 1.5, y, ALU.add, ALU.mult)
        if k < NEWTON - 1 or ready is None:
            step.then_wait(last)
        else:
            last.then_inc(ready, 1)


STATS_STEPS = 4 + RSQRT_STEPS


def token_norm(nc, dve, step, src, dst, stat, squared, squares_wanted, squares_ready, k):
    s, m, v, t, y = (stat[:, i, :] for i in range(5))
    step.then_wait(nc.vector.tensor_reduce(s, src, AX.X, ALU.add))
    step.then_wait(nc.vector.tensor_scalar(m, s, 1.0 / D, None, ALU.mult))
    nc.vector.tensor_tensor(dst, src, m.unsqueeze(2).to_broadcast([P, NT, D]), ALU.subtract).then_inc(squares_wanted, 1)
    dve.wait_ge(squares_ready, k)
    step.then_wait(nc.vector.tensor_reduce(s, squared, AX.X, ALU.add))
    step.then_wait(nc.vector.tensor_scalar(v, s, 1.0 / D, EPS, ALU.mult, ALU.add))
    rsqrt(nc, step, v, t, y)
    return y.unsqueeze(2).to_broadcast([P, NT, D])


def build_global(nc, x1, X, idf, idb, stage, x, g_qk, g_v, g_bits, g_out, g_tr, g_trw, g_scal, bit_eye, g_mask,
                 ident, w_qkv, w_loaded):
    ctx = ExitStack()
    with ctx:
        def sb(name, shape, dt=F32):
            return ctx.enter_context(nc.sbuf_tensor("g_" + name, shape, dt))

        def sem(name):
            return ctx.enter_context(nc.semaphore("g_" + name))

        xin = sb("xin", [P, NT, D])
        squares = sb("squares", [P, NT, D])
        xnT = sb("xnT", [P, NT, P])
        xb = sb("xb", [P, 2, T])
        y = sb("y", [P, NT, D])
        stat = sb("stat", [P, 5, NT])
        qk = sb("qk", [P, 2 * GC, T])
        left = sb("left", [P, GC, T])
        bits = sb("bits", [P, T])
        val = sb("val", [P, TT, D])
        th = sb("th", [P, 2, GS])
        sc = sb("sc", [P, 2, GS])
        pr = sb("pr", [P, 2, GS])
        pT = sb("pT", [P, 2, 3, P])
        mx = sb("mx", [P, GH, TT])
        nmx = sb("nmx", [P, GH, TT])
        total = sb("total", [P, GH, TT])
        rtotal = sb("rtotal", [P, GH, TT])
        o = sb("o", [P, TT, GH, GD])
        oT = sb("oT", [P, T])
        scal = sb("scal", [P, 8])
        tw = sb("tw", [GH, 48])
        twT = sb("twT", [NTR, GH])
        tr = sb("tr", [NTR, NB, 2 * NB])
        wqk = sb("wqk", [P, 2 * GC, P])
        wv = sb("wv", [P, D])
        wbits = sb("wbits", [P, P])
        wout = sb("wout", [P, D])
        eye = sb("eye", [2 * NB, P])
        mix = sb("mix", [2 * NB, GC * P])
        mask = sb("mask", [P, GS], BF16)

        bank = [ctx.enter_context(nc.psum_tensor(f"g_bank{i}", [P, 512], F32)) for i in range(8)]

        x_loaded, id_loaded, w_in = sem("x_loaded"), sem("id_loaded"), sem("weights_loaded")
        dev_ready, squared, normed, step_s = sem("dev_ready"), sem("squared"), sem("normed"), sem("vector_step")
        xt_ready, xt_copied, cleared, mask_ready = sem("xT_ready"), sem("xT_copied"), sem("cleared"), sem("mask_ready")
        half_tanh, tw_shifted, tw_exp, tw_ready = sem("half_tanh"), sem("tw_shifted"), sem("tw_exp"), sem("tw_ready")
        twT_ready, twT_copied, mixed, mix_ready, scal_ready = sem("twT_ready"), sem("twT_copied"), sem("mixed"), sem("mix_ready"), sem("scal_ready")
        xb_ready, qk_ready, qk_copied = sem("xb_ready"), sem("qk_ready"), sem("qk_copied")
        bits_ready, bits_tanh, left_ready, left_copied = sem("bits_ready"), sem("bits_tanh"), sem("left_ready"), sem("left_copied")
        val_ready, val_copied = sem("val_ready"), sem("val_copied")
        raw_ready, raw_tanh, add_ready, scored, max_ready, exped = (
            sem("raw_ready"), sem("raw_tanh"), sem("addend_ready"), sem("scored"), sem("max_ready"), sem("exped"))
        pT_ready, pT_copied, o_ready, o_read = sem("pT_ready"), sem("pT_copied"), sem("o_ready"), sem("o_read")
        oT_ready, oT_copied, y_ready, y_copied = sem("oT_ready"), sem("oT_copied"), sem("y_ready"), sem("y_copied")

        raised = (scored, pT_ready, exped, raw_tanh, o_ready, pT_copied, oT_ready, y_copied, val_ready, o_read)
        LOADS = 9
        block = ctx.enter_context(nc.Block())

        @block.sync
        def _(sp):
            for s in raised:
                sp.sem_inc(s, UP)
            sp.dma_start(x1[:], x.rearrange("(n p) d -> p n d", p=P)).then_inc(x_loaded, 16)
            sp.dma_start(idf[:], ident).then_inc(id_loaded, 16)
            for dst, src in ((scal[:, 0:4], g_scal), (tw[:, 0:NTR], g_trw), (tr[:], g_tr), (eye[:], bit_eye),
                             (wqk[:], g_qk), (wbits[:], g_bits), (wv[:], g_v), (wout[:], g_out), (sc[:, 1, :], g_mask)):
                sp.dma_start(dst, src).then_inc(w_in, 16)
            sp.dma_start(stage[:], w_qkv[0]).then_inc(w_loaded, 16)

        @block.gpsimd
        def _(pool):
            nc.gpsimd.memset(X[:, :, 0:1], 0.0)
            nc.gpsimd.memset(mix[:], 0.0).then_inc(cleared, 1)
            pool.wait_ge(w_in, 16 * LOADS)
            pool.wait_ge(id_loaded, 16)
            nc.gpsimd.tensor_copy(idb[:], idf[:])
            nc.gpsimd.tensor_copy(mask[:], sc[:, 1, :]).then_inc(mask_ready, 1)
            pool.wait_ge(xt_copied, NT // 4)
            with pool.Fori(0, B // 2) as bb:
                for i in range(2):
                    b = bb * 2 + i
                    wait_apart(pool, cleared, val_ready, UP + (b - 1 if i else bb * 2))
                    nc.gpsimd.tensor_copy(xb[:, i, :], xnT[:, bass.ds(b * TT, TT), :].rearrange("p t k -> p (t k)")).then_inc(xb_ready, 1)

        @block.scalar
        def _(act):
            def square(k):
                act.wait_ge(dev_ready, k)
                nc.scalar.activation(squares[:], xin[:], ACT.Square).then_inc(squared, 1)

            square(1)
            act.wait_ge(w_in, 16 * LOADS)
            nc.scalar.activation(scal[:, 4:6], scal[:, 0:2], ACT.Tanh, scale=0.5).then_inc(half_tanh, 1)
            act.wait_ge(tw_shifted, 1)
            nc.scalar.activation(tw[:, 16:16 + NTR], tw[:, 8:8 + NTR], ACT.Exp, scale=1.0 / TEMP,
                                 accum_out=tw[:, 24:25]).then_inc(tw_exp, 1)
            for i in range(NT // 4):
                act.wait_ge(xt_ready, i + 1)
                nc.scalar.activation(xnT[:, 4 * i:4 * i + 4, :], bank[i % 2][:].rearrange("p (n k) -> p n k", n=4),
                                     ACT.Copy).then_inc(xt_copied, 1)
            act.wait_ge(scal_ready, 1)
            with act.Fori(0, B) as b:
                for c in range(2 * GC):
                    act.wait_ge(qk_ready, b * 2 * GC + c + 1)
                    nc.scalar.activation(qk[:, c, :], bank[c % 2][:, 0:T], ACT.Copy).then_inc(qk_copied, 1)
                act.wait_ge(bits_ready, b + 1)
                nc.scalar.activation(bits[:], bank[2][:, 0:T], ACT.Tanh).then_inc(bits_tanh, 1)
                act.wait_ge(val_ready, UP + b + 1)
                nc.scalar.activation(val[:], bank[3][:, 0:T].rearrange("p (t d) -> p t d", t=TT), ACT.Copy).then_inc(val_copied, 1)
                for c in range(GC):
                    act.wait_ge(left_ready, b * GC + c + 1)
                    nc.scalar.activation(left[:, c, :], bank[c % 2][:, 0:T], ACT.Copy).then_inc(left_copied, 1)

                def exps(h):
                    act.wait_ge(max_ready, b * GH + h + 1)
                    act.wait_ge(pT_ready, UP + b * GH + max(h - 1, 0))
                    nc.scalar.activation(pr[:, h % 2, 0:P], sc[:, h % 2, 0:P], ACT.Exp, bias=nmx[:, h, 0:1],
                                         accum_out=total[:, h, 0:1])
                    nc.scalar.activation(pr[:, h % 2, P:GS], sc[:, h % 2, P:GS], ACT.Exp, bias=nmx[:, h, 1:2],
                                         accum_out=total[:, h, 1:2]).then_inc(exped, 1)

                for h in range(GH):
                    act.wait_ge(raw_ready, b * GH + h + 1)
                    act.wait_ge(scored, UP + b * GH + max(h - 1, 0))
                    nc.scalar.activation(th[:, h % 2, :], bank[h % 2][:, 0:GS], ACT.Tanh, scale=scal[:, 6:7]).then_inc(raw_tanh, 1)
                    if h:
                        exps(h - 1)
                exps(GH - 1)
                act.wait_ge(oT_ready, UP + b + 1)
                nc.scalar.activation(oT[:], bank[7][:, 0:T], ACT.Copy).then_inc(oT_copied, 1)
                act.wait_ge(y_ready, b + 1)
                nc.scalar.activation(y[:, bass.ds(b * TT, TT), :], bank[7][:, T:2 * T].rearrange("p (t d) -> p t d", t=TT),
                                     ACT.Copy).then_inc(y_copied, 1)
            square(2)
            square(3)
            for i in range(NT // 4):
                act.wait_ge(xt_ready, NT // 4 + i + 1)
                nc.scalar.activation(X[:, 2 * i:2 * i + 2, 1:1 + T], bank[i % 2][:].rearrange("p (b t) -> p b t", b=2),
                                     ACT.Copy).then_inc(xt_copied, 1)

        @block.vector
        def _(dve):
            step = Steps(dve, step_s)
            dve.wait_ge(x_loaded, 16)
            r = token_norm(nc, dve, step, x1[:], xin[:], stat, squares[:], dev_ready, squared, 1)
            nc.vector.tensor_tensor(xin[:], xin[:], r, ALU.mult).then_inc(normed, 1)
            dve.wait_ge(w_in, 16 * LOADS)
            step.then_wait(nc.vector.tensor_reduce(tw[:, 25:26], tw[:, 0:NTR], AX.X, ALU.max))
            nc.vector.tensor_scalar(tw[:, 8:8 + NTR], tw[:, 0:NTR], tw[:, 25:26], None, ALU.subtract).then_inc(tw_shifted, 1)
            dve.wait_ge(tw_exp, 1)
            step.then_wait(nc.vector.reciprocal(tw[:, 26:27], tw[:, 24:25]))
            nc.vector.tensor_scalar(tw[:, 32:32 + NTR], tw[:, 16:16 + NTR], tw[:, 26:27], None, ALU.mult).then_inc(tw_ready, 1)
            dve.wait_ge(half_tanh, 1)
            nc.vector.tensor_scalar(scal[:, 4:5], scal[:, 4:5], 0.25, 0.25, ALU.mult, ALU.add)
            nc.vector.tensor_scalar(scal[:, 5:6], scal[:, 5:6], 1.0 / NB, 1.0 / NB, ALU.mult, ALU.add)
            nc.vector.reciprocal(scal[:, 6:7], scal[:, 3:4]).then_inc(scal_ready, 1)
            dve.wait_ge(scal_ready, 1)
            dve.wait_ge(twT_ready, 1)
            nc.vector.tensor_copy(twT[:], bank[7][0:NTR, 0:GH]).then_inc(twT_copied, 1)
            dve.wait_ge(mixed, 1)
            dve.wait_ge(cleared, 1)
            step.then_wait(nc.vector.tensor_scalar(mix[:].rearrange("p (h e) -> p h e", h=GH)[:, :, NB:2 * NB],
                                                   bank[6][0:2 * NB, 0:NB * GH].rearrange("p (e h) -> p h e", e=NB),
                                                   scal[0:2 * NB, 5:6], None, ALU.mult))
            for c in range(GC):
                last = nc.vector.scalar_tensor_tensor(mix[:, P * c:P * c + P], eye[:], scal[0:2 * NB, 4:5],
                                                      mix[:, P * c:P * c + P], ALU.mult, ALU.add)
            last.then_inc(mix_ready, 1)
            base = step.here
            BODY = GH + 1

            with dve.Fori(0, B) as b:
                step.body(base + b * BODY)

                def score(h):
                    dve.wait_ge(raw_tanh, UP + b * GH + h + 1)
                    dve.wait_ge(add_ready, b * GH + h + 1)
                    dve.wait_ge(exped, UP + b * GH + max(h - 1, 0))
                    nc.vector.scalar_tensor_tensor(sc[:, h % 2, :], th[:, h % 2, :], scal[:, 2:3], bank[2 + h % 2][:, 0:GS],
                                                   ALU.mult, ALU.add).then_inc(scored, 1)
                    dve.wait_ge(scored, UP + b * GH + h + 1)
                    nc.vector.tensor_reduce(mx[:, h, 0:1], sc[:, h % 2, 0:P], AX.X, ALU.max)
                    step.then_wait(nc.vector.tensor_reduce(mx[:, h, 1:2], sc[:, h % 2, P:GS], AX.X, ALU.max))
                    nc.vector.tensor_scalar(nmx[:, h, :], mx[:, h, :], -1.0, None, ALU.mult).then_inc(max_ready, 1)

                def copy_pT(h):
                    dve.wait_ge(pT_ready, UP + b * GH + h + 1)
                    dve.wait_ge(o_ready, UP + b * GH + max(h - 1, 0))
                    nc.vector.tensor_copy(pT[:, h % 2, :, :], bank[4 + h % 2][:, 0:GS].rearrange("p (t q) -> p t q", t=3)).then_inc(pT_copied, 1)

                for h in range(GH + 2):
                    if h < GH:
                        score(h)
                    if h >= 2:
                        copy_pT(h - 2)
                step.then_wait(nc.vector.reciprocal(rtotal[:], total[:]))
                dve.wait_ge(o_ready, UP + (b + 1) * GH)
                dve.wait_ge(oT_ready, UP + b)
                nc.vector.tensor_tensor(o[:], bank[6][:, 0:T].rearrange("p (t h d) -> p t h d", t=TT, h=GH),
                                        rtotal[:].rearrange("p h t -> p t h").unsqueeze(3).to_broadcast([P, TT, GH, GD]),
                                        ALU.mult).then_inc(o_read, 1)
                assert step.here == BODY
            step.body(base + B * BODY)
            dve.wait_ge(y_copied, UP + B)
            r = token_norm(nc, dve, step, y[:], xin[:], stat, squares[:], dev_ready, squared, 2)
            step.then_wait(nc.vector.tensor_tensor(xin[:], xin[:], r, ALU.mult))
            step.then_wait(nc.vector.tensor_tensor(x1[:], x1[:], xin[:], ALU.add))
            r = token_norm(nc, dve, step, x1[:], xin[:], stat, squares[:], dev_ready, squared, 3)
            nc.vector.tensor_tensor(xin[:], xin[:], r, ALU.mult).then_inc(normed, 1)

        @block.tensor
        def _(pe):
            mm = nc.tensor.matmul

            def to_features(k):
                for i in range(NT // 4):
                    if i >= 2:
                        pe.wait_ge(xt_copied, k * NT // 4 + i - 1)
                    for q in range(4):
                        last = nc.tensor.transpose(bank[i % 2][:, P * q:P * q + P], xin[:, 4 * i + q, :], idf[:])
                    last.then_inc(xt_ready, 1)

            pe.wait_ge(id_loaded, 16)
            pe.wait_ge(normed, 1)
            to_features(0)
            pe.wait_ge(tw_ready, 1)
            nc.tensor.transpose(bank[7][0:NTR, 0:GH], tw[:, 32:32 + NTR], idf[0:GH, 0:GH]).then_inc(twT_ready, 1)
            pe.wait_ge(w_in, 16 * LOADS)
            pe.wait_ge(twT_copied, 1)
            for e in range(NB):
                last = mm(bank[6][0:2 * NB, GH * e:GH * e + GH], tr[:, e, :], twT[:], start=True, stop=True)
            last.then_inc(mixed, 1)
            pe.wait_ge(mix_ready, 1)
            pe.wait_ge(mask_ready, 1)
            pe.wait_ge(xt_copied, NT // 4)

            with pe.Fori(0, B // 2) as bb:
                for i in range(2):
                    b = bb * 2 + i
                    xs = xb[:, i, :]
                    pe.wait_ge(xb_ready, b + 1)
                    pe.wait_ge(raw_tanh, UP + b * GH)
                    pe.wait_ge(scored, UP + b * GH)
                    for c in range(2 * GC):
                        if c >= 2:
                            pe.wait_ge(qk_copied, b * 2 * GC + c - 1)
                        mm(bank[c % 2][:, 0:T], wqk[:, c, :], xs, start=True, stop=True).then_inc(qk_ready, 1)
                    mm(bank[2][:, 0:T], wbits[:], xs, start=True, stop=True).then_inc(bits_ready, 1)
                    for t in range(TT):
                        last = mm(bank[3][:, D * t:D * t + D], xs[:, P * t:P * t + P], wv[:], start=True, stop=True)
                    last.then_inc(val_ready, 1)
                    pe.wait_ge(bits_tanh, b + 1)
                    for c in range(GC):
                        pe.wait_ge(qk_copied, b * 2 * GC + 2 * GC - 1 + min(c, 1))
                        if c >= 2:
                            pe.wait_ge(left_copied, b * GC + c - 1)
                        mm(bank[c % 2][:, 0:T], mix[:, P * c:P * c + P], bits[0:2 * NB, :], start=True, stop=True).then_inc(left_ready, 1)

                    def scores(h):
                        c, r0 = h // 4, 32 * (h % 4)
                        if h < 2:
                            pe.wait_ge(left_copied, (b + 1) * GC)
                            pe.wait_ge(val_copied, b + 1)
                        else:
                            pe.wait_ge(raw_tanh, UP + b * GH + h - 1)
                            pe.wait_ge(scored, UP + b * GH + h - 1)
                        q, k = qk[r0:r0 + GD, c, :], qk[r0:r0 + GD, GC + c, :]
                        mm(bank[h % 2][:, 0:P], q[:, 0:P], k[:, 0:P], start=True, stop=True, tile_position=(r0, 0))
                        mm(bank[h % 2][:, P:GS], q[:, P:T], k, start=True, stop=True, tile_position=(r0, 0)).then_inc(raw_ready, 1)
                        lf, rt = left[r0:r0 + 2 * NB, c, :], bits[r0:r0 + 2 * NB, :]
                        mm(bank[2 + h % 2][:, 0:GS], idb[:], mask[:], start=True, stop=False)
                        mm(bank[2 + h % 2][:, 0:P], lf[:, 0:P], rt[:, 0:P], start=False, stop=False, tile_position=(r0, 0))
                        mm(bank[2 + h % 2][:, P:GS], lf[:, P:T], rt, start=False, stop=True, tile_position=(r0, 0)).then_inc(add_ready, 1)

                    def transpose_probs(h):
                        pe.wait_ge(exped, UP + b * GH + h + 1)
                        pe.wait_ge(pT_copied, UP + b * GH + max(h - 1, 0))
                        for t in range(3):
                            last = nc.tensor.transpose(bank[4 + h % 2][:, P * t:P * t + P], pr[:, h % 2, P * t:P * t + P], idf[:])
                        last.then_inc(pT_ready, 1)

                    def weigh_values(h):
                        pe.wait_ge(pT_copied, UP + b * GH + h + 1)
                        if h == 0:
                            pe.wait_ge(o_read, UP + b)
                        at = GD * h
                        mm(bank[6][:, at:at + GD], pT[:, h % 2, 0, :], val[:, 0, at:at + GD], start=True, stop=True)
                        for t in range(TT):
                            last = mm(bank[6][:, D + at:D + at + GD], pT[:, h % 2, 1 + t, :], val[:, t, at:at + GD],
                                      start=t == 0, stop=t == TT - 1)
                        last.then_inc(o_ready, 1)

                    scores(0)
                    scores(1)
                    for h in range(GH):
                        if h + 2 < GH:
                            scores(h + 2)
                        transpose_probs(h)
                        if h:
                            weigh_values(h - 1)
                    weigh_values(GH - 1)
                    pe.wait_ge(o_read, UP + b + 1)
                    pe.wait_ge(y_copied, UP + b)
                    for t in range(TT):
                        last = nc.tensor.transpose(bank[7][:, P * t:P * t + P], o[:, t, :, :].rearrange("p h d -> p (h d)"), idf[:])
                    last.then_inc(oT_ready, 1)
                    pe.wait_ge(oT_copied, b + 1)
                    for t in range(TT):
                        last = mm(bank[7][:, T + D * t:T + D * t + D], oT[:, P * t:P * t + P], wout[:], start=True, stop=True)
                    last.then_inc(y_ready, 1)
            pe.wait_ge(normed, 2)
            to_features(1)


def build_layers(nc, x1, X, idf, idb, stage, w_loaded, w_qkv, qk_scale, w_o, ffn_par, w_1, w_2, rot, w_mask, pat, sel, out):
    ctx = ExitStack()
    with ctx:
        def sb(name, shape, dt=F32):
            return ctx.enter_context(nc.sbuf_tensor(name, shape, dt))

        def sem(name):
            return ctx.enter_context(nc.semaphore(name))

        WQ = 2 * INNER
        wh = sb("wh", [P, 3 * INNER], F32R)
        wl = sb("wl", [P, 3 * INNER], F32R)
        wsh = sb("wsh", [P, WQ], F32R)
        wsl = sb("wsl", [P, WQ], F32R)
        wo = sb("wo", [P, QC, D])
        w1 = sb("w1", [P, 2 * FC, P])
        w2 = sb("w2", [P, FC, D])
        fpar = sb("fpar", [P, 3 + 2 * FC])
        qks = sb("qks", [P, DEPTH, 4])
        rotb = sb("rotb", [P, 4, T])
        rots = sb("rots", [P, 4, T])
        xh = sb("xh", [P, WIN + T], F32R)
        xl = sb("xl", [P, WIN + T], F32R)
        sq = sb("sq", [P, 2, 2, T])
        patb = sb("patb", [P, 2])
        selb = sb("sel", [2 * H, 2 * QC, P], F32R)
        part = sb("part", [P, 2 * QC, T])
        sinp = sb("sinp", [P, 2, 2, T])
        nrm = sb("nrm", [P, 3, TT * 2 * H])
        rh = sb("rh", [2 * H, T], F32R)
        rl = sb("rl", [2 * H, T], F32R)
        qT = sb("qT", [P, QC, T])
        kT = sb("kT", [P, QC, WIN + T])
        V = sb("V", [KW, NU, H, VW])
        wmask = sb("wmask", [P, NU * KW], BF16)
        mx = sb("mx", [P, 2, NU])
        pr = sb("pr", [P, 2, NU * KW])
        pT = sb("pT", [KW, 2, NU, P])
        rden = sb("rden", [P, 2, TT, 2])
        O = sb("O", [P, TT, H, HD])
        OT = sb("OT", [P, QC, T])
        xf = sb("xf", [P, T])
        dev = sb("dev", [P, T])
        dsq = sb("dsq", [P, T])
        vn = sb("vn", [P, 3, TT])
        dg = sb("dg", [P, TT, P])
        t1 = sb("t1", [P, T])
        xn = sb("xn", [P, T])
        mean1 = sb("mean1", [P, P])
        ones = sb("ones", [P, P])
        gl = sb("gl", [P, 2, T])
        hid = sb("hid", [P, FC, T])
        stat = sb("stat", [P, 5, NT])

        bank = [ctx.enter_context(nc.psum_tensor(f"bank{i}", [P, 512], F32)) for i in range(8)]
        NRM = bank[4][:, 0:TT * 2 * H]
        NRT = bank[5][0:2 * H, 0:T]

        const_in, tail_in = sem("constants_loaded"), sem("tail_weights_loaded")
        cleared, wmask_ready, sel_ready = sem("cleared"), sem("wmask_ready"), sem("sel_ready")
        v_step, t_step, p_step = sem("vector_step"), sem("vector_tail_step"), sem("pool_step")
        w_high, ws_high, w_low, ws_low, rot_ready = sem("w_high"), sem("w_swapped_high"), sem("w_low"), sem("w_swapped_low"), sem("rot_ready")
        xs_ready, raw_ready, squared, turned, summed, norm_done = (
            sem("xs_ready"), sem("raw_ready"), sem("squared"), sem("turned"), sem("summed"), sem("norm_done"))
        root_ready, rt_ready, rn_ready = sem("rnorm_ready"), sem("rnormT_ready"), sem("rnorm_split")
        v_ready, v_copied, rb_ready, scaled = sem("v_ready"), sem("v_copied"), sem("rbroadcast_ready"), sem("qk_scaled")
        s_ready, centered, exped, pt_ready, pt_copied, o_ready, o_read = (
            sem("scores_ready"), sem("centered"), sem("exped"), sem("pT_ready"), sem("pT_copied"), sem("o_ready"), sem("o_read"))
        ot_ready, ot_copied, y_ready, xf_ready = sem("oT_ready"), sem("oT_copied"), sem("y_ready"), sem("xf_ready")
        mean_ready, dev_ready, dsq_ready, var_ready, dg_ready, rs_ready, xn_ready = (
            sem("mean_ready"), sem("dev_ready"), sem("dsq_ready"), sem("var_ready"), sem("diagonal_ready"), sem("rstd_ready"), sem("xn_ready"))
        h_ready, gelu_ready, hid_ready, y2_ready, x_updated = (
            sem("hidden_ready"), sem("gelu_ready"), sem("gated"), sem("ffn_ready"), sem("x_updated"))
        xt_ready, fdev_ready, fsquared, finished, stored = (
            sem("xT_ready"), sem("final_dev_ready"), sem("final_squared"), sem("finished"), sem("stored"))

        raised = (norm_done, summed, o_ready, pt_ready, ot_ready, y_ready, hid_ready, v_ready, centered, pt_copied, o_read)
        CONSTS, TAILS, WPARTS, SWAPPED = 5, 4, 3, 2
        partf = part[:].rearrange("p a t -> p (a t)")
        mask_in = partf[:, 2 * QC * T - NU * KW:2 * QC * T]
        sel_in = partf[0:2 * H, 0:2 * QC * P]
        fdev = partf[:, 0:NT * D].rearrange("p (n d) -> p n d", d=D)
        fy = partf[:, NT * D:2 * NT * D].rearrange("p (n d) -> p n d", d=D)
        fsq = stage[:, 0:NT * D].rearrange("p (n d) -> p n d", d=D)

        ORDER = [p for c in range(NP // 2) for p in (c, NP // 2 + c)]

        def swap(t):
            return t.rearrange("p (h s d) -> p h s d", s=2, d=HD // 2)

        def pair(t):
            return t.rearrange("p (a t) -> p a t", a=2)

        def tail_weights(n):
            return 16 * TAILS * ((n + B - 1) // B)

        def walk(eng, top, step):
            top(0)
            step(0, 0, False)
            with eng.Fori(1, B) as b:
                step(b, b, True)
            with eng.Fori(1, DEPTH) as l:
                top(l)
                with eng.Fori(0, B) as b:
                    step(l * B + b, b, True)

        block = ctx.enter_context(nc.Block())

        @block.sync
        def _(sp):
            for s in raised:
                sp.sem_inc(s, UP)
            sp.sem_inc(x_updated, B)
            for dst, src in ((rotb[:], rot), (qks[:], qk_scale), (mask_in, w_mask), (patb[:], pat), (sel_in, sel)):
                sp.dma_start(dst, src).then_inc(const_in, 16)

            def load_tail(l):
                for dst, src in ((wo[:], w_o), (w1[:], w_1), (w2[:], w_2), (fpar[:], ffn_par)):
                    sp.dma_start(dst, src[l]).then_inc(tail_in, 16)

            load_tail(0)
            with sp.Fori(1, DEPTH) as l:
                low, high = sp.to_reg(WPARTS * l), sp.to_reg(SWAPPED * l)
                sp.wait_ge(w_low, low)
                sp.wait_ge(ws_high, high)
                sp.dma_start(stage[:], w_qkv[l]).then_inc(w_loaded, 16)
                sp.wait_ge(x_updated, B + l * B)
                load_tail(l)

        @block.gpsimd
        def _(pool):
            step = Steps(pool, p_step)
            nc.gpsimd.memset(mean1[:], 1.0 / D)
            nc.gpsimd.memset(ones[:], 1.0)
            nc.gpsimd.memset(V[:, :, :, HD:VW], 1.0)
            nc.gpsimd.memset(kT[:, :, 0:WIN], 0.0)
            nc.gpsimd.memset(xh[:, 0:WIN].bitcast(F32), 0.0)
            nc.gpsimd.memset(xl[:, 0:WIN].bitcast(F32), 0.0).then_inc(cleared, 1)
            pool.wait_ge(cleared, 1)
            pool.wait_ge(const_in, 16 * CONSTS)
            nc.gpsimd.tensor_copy(wmask[:], mask_in).then_inc(wmask_ready, 1)
            pool.wait_ge(wmask_ready, 1)
            nc.gpsimd.tensor_copy(selb[:].rearrange("p c m -> p (c m)"), sel_in).then_inc(sel_ready, 1)
            pool.wait_ge(sel_ready, 1)
            BODY = 1

            def prepare(n, b):
                step.body(n * BODY)
                wait_apart(pool, cleared, x_updated, n + 1)
                wait_apart(pool, cleared, v_ready, UP + n * NV)
                wait_apart(pool, cleared, summed, UP + n * NP)
                nc.gpsimd.tensor_copy(xh[0:64, WIN:WIN + T], X[0:64, b, 1:1 + T])
                step.then_wait(nc.gpsimd.tensor_copy(xh[64:P, WIN:WIN + T], X[64:P, b, 0:T]), cleared)
                nc.gpsimd.tensor_tensor(xl[0:64, WIN:WIN + T], X[0:64, b, 1:1 + T], xh[0:64, WIN:WIN + T].bitcast(F32), ALU.subtract)
                nc.gpsimd.tensor_tensor(xl[64:P, WIN:WIN + T], X[64:P, b, 0:T], xh[64:P, WIN:WIN + T].bitcast(F32),
                                        ALU.subtract).then_inc(xs_ready, 1)
                assert step.here == BODY

            def add_parts(n):
                for p in range(NP):
                    pool.wait_ge(turned, n * NP + p + 1)
                    nc.gpsimd.tensor_tensor(part[:, 2 * p:2 * p + 2, :], part[:, 2 * p:2 * p + 2, :], sinp[:, p % 2, :, :],
                                            ALU.add).then_inc(summed, 1)

            with pool.Fori(0, DEPTH) as l:
                with pool.Fori(0, B) as b:
                    prepare(l * B + b, b)
                    add_parts(l * B + b)

        @block.scalar
        def _(act):
            def top(l):
                act.wait_ge(w_loaded, 16 * (l + 1))
                act.wait_ge(v_ready, UP + l * B * NV)
                for t in range(SWAPPED):
                    at = slice(INNER * t, INNER * t + INNER)
                    for s in range(2):
                        last = nc.scalar.activation(swap(wsh[:, at])[:, :, s, :], swap(stage[:, at])[:, :, 1 - s, :], ACT.Copy)
                    last.then_inc(ws_high, 1)
                    act.wait_ge(w_low, l * WPARTS + t + 1)
                    for s in range(2):
                        last = nc.scalar.activation(swap(wsl[:, at])[:, :, s, :], swap(wl[:, at].bitcast(F32))[:, :, 1 - s, :], ACT.Copy)
                    last.then_inc(ws_low, 1)

            def square(n, p):
                act.wait_ge(raw_ready, n * NP + p + 1)
                act.wait_ge(norm_done, UP + n * NP + max(p - 1, 0))
                nc.scalar.activation(sq[:, p % 2, :, :], pair(bank[2 + p % 2][:]), ACT.Square).then_inc(squared, 1)

            def copy_values(n, j):
                if j == 0:
                    act.wait_ge(o_ready, UP + n * NS)
                act.wait_ge(v_ready, UP + n * NV + j + 1)
                u, half = j // 2, j % 2
                nc.scalar.activation(V[:, u, 8 * half:8 * half + 8, 0:HD], bank[j % 4][0:KW, :].rearrange("p (h d) -> p h d", d=HD),
                                     ACT.Copy).then_inc(v_copied, 1)

            def probs(n, c):
                act.wait_ge(centered, UP + n * NS + c + 1)
                nc.scalar.activation(pr[:, c % 2, :], pr[:, c % 2, :], ACT.Exp, scale=QK_SCALE).then_inc(exped, 1)

            def copy_pT(n, c):
                act.wait_ge(pt_ready, UP + n * NS + c + 1)
                act.wait_ge(o_ready, UP + n * NS + max(c - 1, 0))
                nc.scalar.activation(pT[:, c % 2, :, :], bank[2 + c % 2][0:KW, :].rearrange("p (u q) -> p u q", u=NU), ACT.Copy).then_inc(pt_copied, 1)

            def copy_oT(m, k):
                if k == 0:
                    act.wait_ge(y_ready, UP + m)
                act.wait_ge(ot_ready, UP + m * NO + k + 1)
                i, c = k // 2, 4 * (k % 2)
                nc.scalar.activation(OT[:, c:c + 4, P * i:P * i + P], bank[6 + k % 2][:].rearrange("p (c q) -> p c q", c=4),
                                     ACT.Copy).then_inc(ot_copied, 1)

            def square_dev(m):
                act.wait_ge(dev_ready, m + 1)
                nc.scalar.activation(dsq[:], dev[:], ACT.Square).then_inc(dsq_ready, 1)

            def gelu(m, j):
                act.wait_ge(h_ready, m * FC + j + 1)
                act.wait_ge(hid_ready, UP + m * FC + max(j - 1, 0))
                nc.scalar.activation(gl[:, j % 2, :], bank[6 + j % 2][:, 0:T], ACT.Gelu, bias=fpar[:, 3 + FC + j:4 + FC + j]).then_inc(gelu_ready, 1)

            def step(n, b, tail):
                m = n - 1
                for p in range(NP):
                    square(n, p)
                    if tail and 1 <= p <= NO:
                        copy_oT(m, p - 1)
                for j in range(NV):
                    copy_values(n, j)
                    if tail and j == 0:
                        square_dev(m)
                        act.wait_ge(tail_in, tail_weights(n))
                    if tail and j >= NV - 2:
                        gelu(m, j - NV + 2)
                if tail:
                    gelu(m, 2)
                for c in range(NS + 2):
                    if c < NS:
                        probs(n, c)
                    if c >= 2:
                        copy_pT(n, c - 2)

            walk(act, top, step)
            m = DEPTH * B - 1
            for k in range(NO):
                copy_oT(m, k)
            square_dev(m)
            for j in range(FC):
                gelu(m, j)
            act.wait_ge(fdev_ready, 1)
            nc.scalar.activation(fsq, fdev, ACT.Square).then_inc(fsquared, 1)
            act.wait_ge(finished, 1)
            act.dma_start(out.rearrange("(n p) d -> p n d", p=P), x1[:]).then_inc(stored, 16)
            act.wait_ge(stored, 16)

        @block.vector
        def _(dve):
            step_v, step_t = Steps(dve, v_step), Steps(dve, t_step)
            V_BODY = (1 + RSQRT_STEPS - 1) + 1 + 2 * NS
            T_BODY = 1 + (1 + RSQRT_STEPS) + 1

            def top(l):
                dve.wait_ge(w_loaded, 16 * (l + 1))
                dve.wait_ge(v_ready, UP + l * B * NV)
                for t in range(WPARTS):
                    at = slice(INNER * t, INNER * t + INNER)
                    nc.vector.tensor_copy(wh[:, at], stage[:, at]).then_inc(w_high, 1)
                    dve.wait_ge(w_high, l * WPARTS + t + 1)
                    nc.vector.tensor_tensor(wl[:, at], stage[:, at], wh[:, at].bitcast(F32), ALU.subtract).then_inc(w_low, 1)
                    if t == 0:
                        for k in range(4):
                            last = nc.vector.tensor_scalar(rots[:, k, :], rotb[:, k, :], qks[:, bass.ds(l, 1), k:k + 1].rearrange("p l k -> p (l k)"), None, ALU.mult)
                        last.then_inc(rot_ready, 1)
                wait_apart(dve, cleared, rot_ready, l + 1)

            def rotate(n, p):
                k = 0 if p < NP // 2 else 2
                dve.wait_ge(raw_ready, n * NP + p + 1)
                nc.vector.tensor_tensor(part[:, 2 * p:2 * p + 2, :], pair(bank[p % 2][:]),
                                        rots[:, k, :].unsqueeze(1).to_broadcast([P, 2, T]), ALU.mult)
                dve.wait_ge(squared, n * NP + p + 1)
                dve.wait_ge(summed, UP + n * NP + max(p - 1, 0))
                nc.vector.tensor_tensor(sinp[:, p % 2, :, :], pair(bank[2 + p % 2][:]),
                                        rots[:, k + 1, :].unsqueeze(1).to_broadcast([P, 2, T]), ALU.mult).then_inc(turned, 1)

            def norms(n):
                dve.wait_ge(norm_done, UP + (n + 1) * NP)
                v, t, y = nrm[:, 0, :], nrm[:, 1, :], nrm[:, 2, :]
                step_v.then_wait(nc.vector.tensor_scalar(v, NRM, NORM_FLOOR, None, ALU.max))
                rsqrt(nc, step_v, v, t, y, root_ready)

            def split_norms(n):
                dve.wait_ge(rt_ready, n + 1)
                step_v.then_wait(nc.vector.tensor_copy(rh[:], NRT))
                nc.vector.tensor_tensor(rl[:], NRT, rh[:].bitcast(F32), ALU.subtract).then_inc(rn_ready, 1)

            def scale(n, k):
                p = ORDER[k]
                dve.wait_ge(rb_ready, n * NP + k + 1)
                dve.wait_ge(summed, UP + n * NP + p + 1)
                dst = qT[:, 2 * p:2 * p + 2, :] if p < NP // 2 else kT[:, 2 * p - QC:2 * p - QC + 2, WIN:WIN + T]
                nc.vector.tensor_tensor(dst, part[:, 2 * p:2 * p + 2, :], pair(bank[k % 4][:]), ALU.mult).then_inc(scaled, 1)

            def center(n, c):
                dve.wait_ge(s_ready, n * NS + c + 1)
                dve.wait_ge(pt_ready, UP + n * NS + max(c - 1, 0))
                s3 = bank[4 + c % 2][:, 0:NU * KW].rearrange("p (u k) -> p u k", u=NU)
                step_v.then_wait(nc.vector.tensor_reduce(mx[:, c % 2, :], s3, AX.X, ALU.max))
                nc.vector.tensor_tensor(pr[:, c % 2, :].rearrange("p (u k) -> p u k", u=NU), s3,
                                        mx[:, c % 2, :].unsqueeze(2).to_broadcast([P, NU, KW]), ALU.subtract).then_inc(centered, 1)

            def take_o(n, c):
                dve.wait_ge(o_ready, UP + n * NS + c + 1)
                if c == 0:
                    dve.wait_ge(ot_ready, UP + n * NO)
                ov = bank[c % 2][:].rearrange("p (i x) -> p i x", i=TT)[:, :, 0:2 * VW].rearrange("p i (h v) -> p i h v", h=2)
                step_v.then_wait(nc.vector.reciprocal(rden[:, c % 2].unsqueeze(3), ov[:, :, :, HD:VW]))
                nc.vector.tensor_tensor(O[:, :, 2 * c:2 * c + 2, :], ov[:, :, :, 0:HD],
                                        rden[:, c % 2].unsqueeze(3).to_broadcast([P, TT, 2, HD]), ALU.mult).then_inc(o_read, 1)

            def add_attention(m, b):
                dve.wait_ge(y_ready, UP + m + 1)
                step_t.then_wait(nc.vector.tensor_tensor(X[:, b, 1:1 + T], X[:, b, 1:1 + T], bank[6][:, 0:T], ALU.add), cleared)
                nc.vector.tensor_copy(xf[0:64, :], X[0:64, b, 1:1 + T])
                nc.vector.tensor_copy(xf[64:P, :], X[64:P, b, 0:T]).then_inc(xf_ready, 1)
                dve.wait_ge(xf_ready, m + 1)

            def deviate(m):
                dve.wait_ge(mean_ready, m + 1)
                nc.vector.tensor_tensor(dev[:], xf[:], bank[7][:, 0:T], ALU.subtract).then_inc(dev_ready, 1)

            def root(m):
                dve.wait_ge(var_ready, m + 1)
                v, t, y = vn[:, 0, :], vn[:, 1, :], vn[:, 2, :]
                step_t.then_wait(nc.vector.tensor_scalar(v, bank[6][:, 0:TT], EPS, None, ALU.add))
                rsqrt(nc, step_t, v, t, y)
                for i in range(TT):
                    last = nc.vector.tensor_scalar(dg[:, i, :], idf[:], y[:, i:i + 1], None, ALU.mult)
                last.then_inc(dg_ready, 1)

            def norm_x(m):
                dve.wait_ge(rs_ready, m + 1)
                dve.wait_ge(dev_ready, m + 1)
                step_t.then_wait(nc.vector.tensor_tensor(t1[:], dev[:], bank[7][:, 0:T], ALU.mult))
                nc.vector.tensor_scalar(xn[:], t1[:], fpar[:, 0:1], fpar[:, 1:2], ALU.mult, ALU.add).then_inc(xn_ready, 1)

            def gate(m, j):
                dve.wait_ge(gelu_ready, m * FC + j + 1)
                nc.vector.scalar_tensor_tensor(hid[:, j, :], bank[6 + j % 2][:, T:2 * T], fpar[:, 3 + j:4 + j], gl[:, j % 2, :],
                                               ALU.add, ALU.mult).then_inc(hid_ready, 1)

            def add_ffn(m, b):
                dve.wait_ge(y2_ready, m + 1)
                nc.vector.scalar_tensor_tensor(X[:, b, 1:1 + T], bank[7][:, 0:T], fpar[:, 2:3], X[:, b, 1:1 + T],
                                               ALU.add, ALU.add).then_inc(x_updated, 1)

            def step(n, b, tail):
                m, bm = n - 1, (b + B - 1) % B
                step_v.body(n * V_BODY)
                step_t.body(m * T_BODY)
                for p in range(NP):
                    rotate(n, p)
                    if tail and p == NP - 2:
                        add_attention(m, bm)
                if tail:
                    deviate(m)
                norms(n)
                if tail:
                    dve.wait_ge(tail_in, tail_weights(n))
                    root(m)
                split_norms(n)
                if tail:
                    norm_x(m)
                for k in range(NP):
                    scale(n, k)
                    if tail and k in (1, 3):
                        gate(m, k // 2)
                center(n, 0)
                if tail:
                    gate(m, 2)
                center(n, 1)
                for c in range(NS):
                    if c + 2 < NS:
                        center(n, c + 2)
                    take_o(n, c)
                    if tail and c == 0:
                        add_ffn(m, bm)
                assert step_v.here == V_BODY and step_t.here == (T_BODY if tail else 0)

            dve.wait_ge(const_in, 16 * CONSTS)
            dve.wait_ge(cleared, 1)
            dve.wait_ge(sel_ready, 1)
            walk(dve, top, step)
            m = DEPTH * B - 1
            step_t.body(m * T_BODY)
            add_attention(m, B - 1)
            deviate(m)
            root(m)
            norm_x(m)
            for j in range(FC):
                gate(m, j)
            add_ffn(m, B - 1)
            step_v.body(DEPTH * B * V_BODY)
            for i in range(NT // 4):
                dve.wait_ge(xt_ready, i + 1)
                step_v.then_wait(nc.vector.tensor_copy(fy[:, 4 * i:4 * i + 4, :], bank[i][:].rearrange("p (n d) -> p n d", n=4)))
            r = token_norm(nc, dve, step_v, fy, fdev, stat, fsq, fdev_ready, fsquared, 1)
            step_v.then_wait(nc.vector.tensor_tensor(fdev, fdev, r, ALU.mult))
            nc.vector.tensor_tensor(x1[:], x1[:], fdev, ALU.add).then_inc(finished, 1)

        @block.tensor
        def _(pe):
            mm = nc.tensor.matmul

            def top(l):
                pass

            def raw(n, l, p):
                if p in (0, NP // 2):
                    pe.wait_ge(w_low, WPARTS * l + 1 + 2 * p // NP)
                    pe.wait_ge(ws_low, SWAPPED * l + 1 + 2 * p // NP)
                if p >= 2:
                    pe.wait_ge(turned, n * NP + p - 1)
                for t, (hi, lo) in enumerate(((wh, wl), (wsh, wsl))):
                    for a in range(2):
                        c = 2 * p + a
                        ps = bank[2 * t + p % 2][:, T * a:T * a + T]
                        w_hi, w_lo = hi[:, P * c:P * c + P], lo[:, P * c:P * c + P]
                        mm(ps, w_hi, xh[:, WIN:], start=True, stop=False)
                        mm(ps, w_hi, xl[:, WIN:], start=False, stop=False)
                        last = mm(ps, w_lo, xh[:, WIN:], start=False, stop=True)
                last.then_inc(raw_ready, 1)

            def gather_norms(n, p):
                pe.wait_ge(squared, n * NP + p + 1)
                if p == 0:
                    pe.wait_ge(centered, UP + n * NS)
                for a in range(2):
                    for i in range(TT):
                        at = 2 * H * i + 2 * (2 * p + a)
                        last = mm(NRM[:, at:at + 2], sq[:, p % 2, a, P * i:P * i + P], patb[:], start=True, stop=True)
                last.then_inc(norm_done, 1)

            def values(n, l, j):
                if j == 0:
                    pe.wait_ge(w_low, WPARTS * l + 3)
                    pe.wait_ge(turned, (n + 1) * NP)
                if j >= 4:
                    pe.wait_ge(v_copied, n * NV + j - 3)
                u, half = j // 2, j % 2
                ps = bank[j % 4][0:KW, :]
                at = slice(2 * INNER + 512 * half, 2 * INNER + 512 * half + 512)
                x_hi, x_lo = xh[:, QW * u:QW * u + KW], xl[:, QW * u:QW * u + KW]
                mm(ps, x_hi, wh[:, at], start=True, stop=False)
                mm(ps, x_hi, wl[:, at], start=False, stop=False)
                mm(ps, x_lo, wh[:, at], start=False, stop=True).then_inc(v_ready, 1)

            def turn_norms(n):
                pe.wait_ge(root_ready, n + 1)
                for i in range(TT):
                    last = nc.tensor.transpose(NRT[:, P * i:P * i + P], nrm[:, 2, 2 * H * i:2 * H * i + 2 * H], idf[:])
                last.then_inc(rt_ready, 1)

            def spread_norms(n, k):
                if k == 0:
                    pe.wait_ge(rn_ready, n + 1)
                if k < 4:
                    pe.wait_ge(v_copied, n * NV + NV - 3 + k)
                else:
                    pe.wait_ge(scaled, n * NP + k - 3)
                for a in range(2):
                    c = 2 * ORDER[k] + a
                    ps = bank[k % 4][:, T * a:T * a + T]
                    mm(ps, selb[:, c, :], rh[:], start=True, stop=False)
                    last = mm(ps, selb[:, c, :], rl[:], start=False, stop=True)
                last.then_inc(rb_ready, 1)

            def scores(n, c):
                if c % 2 == 0:
                    pe.wait_ge(scaled, n * NP + c + 2)
                if c >= 2:
                    pe.wait_ge(centered, UP + n * NS + c - 1)
                ps = bank[4 + c % 2]
                mm(ps[:, 0:NU * KW], idb[:], wmask[:], start=True, stop=False)
                for u in range(NU):
                    for r0 in (0, HD):
                        last = mm(ps[r0:r0 + QW, KW * u:KW * u + KW], qT[r0:r0 + HD, c, QW * u:QW * u + QW],
                                  kT[r0:r0 + HD, c, QW * u:QW * u + KW], start=False, stop=u == NU - 1, tile_position=(r0, r0))
                last.then_inc(s_ready, 1)

            def transpose_probs(n, c):
                pe.wait_ge(exped, n * NS + c + 1)
                if c >= 2:
                    pe.wait_ge(pt_copied, UP + n * NS + c - 1)
                elif c == 0:
                    pe.wait_ge(scaled, (n + 1) * NP)
                for u in range(NU):
                    last = nc.tensor.transpose(bank[2 + c % 2][0:KW, P * u:P * u + P], pr[:, c % 2, KW * u:KW * u + KW], idf[:])
                last.then_inc(pt_ready, 1)

            def weigh_values(n, c):
                wait_apart(pe, cleared, pt_copied, UP + n * NS + c + 1)
                if c >= 2:
                    pe.wait_ge(o_read, UP + n * NS + c - 1)
                for u in range(NU):
                    q0, at = QW * (u % 2), T * (u // 2)
                    for hp in range(2):
                        last = mm(bank[c % 2][q0:q0 + QW, at + VW * hp:at + VW * hp + VW], pT[:, c % 2, u, QW * hp:QW * hp + QW],
                                  V[:, u, 2 * c + hp, :], start=True, stop=True, tile_position=(0, q0))
                last.then_inc(o_ready, 1)

            def transpose_o(m, k):
                if k == 0:
                    pe.wait_ge(o_read, UP + (m + 1) * NS)
                    pe.wait_ge(x_updated, B + m)
                if k >= 2:
                    pe.wait_ge(ot_copied, m * NO + k - 1)
                i, c0 = k // 2, 4 * (k % 2)
                for c in range(c0, c0 + 4):
                    last = nc.tensor.transpose(bank[6 + k % 2][:, P * (c - c0):P * (c - c0) + P],
                                               O[:, i, 2 * c:2 * c + 2, :].rearrange("p h d -> p (h d)"), idf[:])
                last.then_inc(ot_ready, 1)

            def project_out(m):
                pe.wait_ge(ot_copied, (m + 1) * NO)
                for c in range(QC):
                    last = mm(bank[6][:, 0:T], wo[:, c, :], OT[:, c, :], start=c == 0, stop=c == QC - 1)
                last.then_inc(y_ready, 1)

            def means(m):
                pe.wait_ge(xf_ready, m + 1)
                mm(bank[7][:, 0:T], mean1[:], xf[:], start=True, stop=True).then_inc(mean_ready, 1)

            def variances(m):
                pe.wait_ge(dsq_ready, m + 1)
                for i in range(TT):
                    last = mm(bank[6][:, i:i + 1], dsq[:, P * i:P * i + P], mean1[:, 0:1], start=True, stop=True)
                last.then_inc(var_ready, 1)

            def spread_root(m):
                pe.wait_ge(dg_ready, m + 1)
                for i in range(TT):
                    last = mm(bank[7][:, P * i:P * i + P], ones[:], dg[:, i, :], start=True, stop=True)
                last.then_inc(rs_ready, 1)

            def hidden(m, j):
                if j == 0:
                    pe.wait_ge(xn_ready, m + 1)
                if j == 2:
                    pe.wait_ge(hid_ready, UP + m * FC + 1)
                mm(bank[6 + j % 2][:, 0:T], w1[:, FC + j, :], xn[:], start=True, stop=True)
                mm(bank[6 + j % 2][:, T:2 * T], w1[:, j, :], xn[:], start=True, stop=True).then_inc(h_ready, 1)

            def ffn_out(m):
                pe.wait_ge(hid_ready, UP + (m + 1) * FC)
                for j in range(FC):
                    last = mm(bank[7][:, 0:T], w2[:, j, :], hid[:, j, :], start=j == 0, stop=j == FC - 1)
                last.then_inc(y2_ready, 1)

            def step(n, b, tail):
                m, l = n - 1, n // B
                pe.wait_ge(xs_ready, n + 1)
                pe.wait_ge(o_read, UP + n * NS)
                pe.wait_ge(pt_copied, UP + n * NS)
                for p in range(NP):
                    raw(n, l, p)
                    if p:
                        gather_norms(n, p - 1)
                    if tail and 1 <= p <= NO:
                        transpose_o(m, p - 1)
                    if tail and p == NO + 1:
                        pe.wait_ge(tail_in, tail_weights(n))
                        project_out(m)
                if tail:
                    means(m)
                gather_norms(n, NP - 1)
                for j in range(NV):
                    values(n, l, j)
                    if tail:
                        {1: variances, 3: spread_root, 5: lambda m: hidden(m, 0), 6: lambda m: hidden(m, 1)}.get(j, lambda m: None)(m)
                    if j == 4:
                        turn_norms(n)
                for k in range(NP):
                    spread_norms(n, k)
                    if tail and k == 3:
                        hidden(m, 2)
                scores(n, 0)
                scores(n, 1)
                if tail:
                    ffn_out(m)
                for c in range(NS):
                    if c + 2 < NS:
                        scores(n, c + 2)
                    transpose_probs(n, c)
                    if c:
                        weigh_values(n, c - 1)
                weigh_values(n, NS - 1)

            pe.wait_ge(sel_ready, 1)
            pe.wait_ge(const_in, 16 * CONSTS)
            walk(pe, top, step)
            m = DEPTH * B - 1
            for k in range(NO):
                transpose_o(m, k)
            project_out(m)
            means(m)
            variances(m)
            spread_root(m)
            for j in range(FC):
                hidden(m, j)
            ffn_out(m)
            pe.wait_ge(x_updated, B + DEPTH * B)
            for i in range(NT // 4):
                for q in range(4):
                    t = 4 * i + q
                    last = nc.tensor.transpose(bank[i][:, P * q:P * q + P], X[:, t // TT, 1 + P * (t % TT):1 + P * (t % TT) + P], idf[:])
                last.then_inc(xt_ready, 1)


def build(nc, a, out):
    with ExitStack() as ctx:
        def sb(name, shape, dt=F32):
            return ctx.enter_context(nc.sbuf_tensor(name, shape, dt))

        x1 = sb("x1", [P, NT, D])
        X = sb("X", [P, B, 1 + T])
        idf = sb("idf", [P, P])
        idb = sb("idb", [P, P], BF16)
        stage = sb("stage", [P, 3 * INNER])
        w_loaded = ctx.enter_context(nc.semaphore("w_loaded"))
        build_global(nc, x1, X, idf, idb, stage, a["x"], a["g_qk"], a["g_v"], a["g_bits"], a["g_out"], a["g_tr"], a["g_trw"],
                     a["g_scal"], a["bit_eye"], a["g_mask"], a["ident"], a["w_qkv"], w_loaded)
        build_layers(nc, x1, X, idf, idb, stage, w_loaded, a["w_qkv"], a["qk_scale"], a["w_o"], a["ffn_par"], a["w_1"], a["w_2"],
                     a["rot"], a["w_mask"], a["pat"], a["sel"], out)


def constants():
    f = np.float32
    neg = -1e37
    q = np.arange(P)
    g_mask = np.zeros((P, GS), f)
    g_mask[:, 0:P] = np.where(q[None, :] > q[:, None], neg, 0)
    g_mask[:, P:] = np.where(np.arange(T)[None, :] > q[:, None] + P, neg, 0)
    a, j = np.arange(P)[:, None, None] % QW, np.arange(KW)[None, None, :]
    u = np.arange(NU)[None, :, None]
    seen = (j >= a) & (j <= a + WIN) & ((u > 0) | (j >= WIN))
    w_mask = np.where(seen, 0, neg).astype(f).reshape(P, NU * KW)
    bit_eye = np.zeros((2 * NB, P), f)
    for i in range(NB):
        bit_eye[i, i::32] = 1
    pat = (q[:, None] // HD == np.arange(2)[None, :]).astype(f)
    sel = (np.arange(2 * QC * P)[None, :] // HD == np.arange(2 * H)[:, None]).astype(f)
    half = np.arange(0, HD, 2, dtype=f)
    inv_freq = (f(1.0) / np.power(f(10000.0), half / f(HD))).astype(f)
    t = np.arange(T, dtype=f)
    freqs = (inv_freq[:, None] * t[None, :]).astype(f)
    base = ((half + f(0.4 * HD)) / f(1.4 * HD)).astype(f)
    scale = np.power(base[:, None].astype(np.float64), ((t - T // 2) / f(WIN // 2))[None, :].astype(np.float64))
    cos, sin = np.cos(freqs.astype(np.float64)), np.sin(freqs.astype(np.float64))

    def over_heads(lo, hi):
        return np.tile(np.concatenate([lo, hi], 0), (2, 1)).astype(f)

    rot = np.stack([over_heads(cos * scale, cos * scale), over_heads(-sin * scale, sin * scale),
                    over_heads(cos / scale, cos / scale), over_heads(-sin / scale, sin / scale)], 1)
    return dict(g_mask=g_mask, w_mask=w_mask, ident=np.eye(P, dtype=f), bit_eye=bit_eye, pat=pat, sel=sel, rot=np.ascontiguousarray(rot))


def lay_out(i):
    f = np.float32
    i = {k: np.asarray(v) for k, v in i.items()}
    a = dict(x=i["L0_attn_x"].reshape(B * T, D))
    wt = i["L0_attn_qkv_w"].T
    g_qk = np.zeros((P, 2 * GC, 4, 32), f)
    g_qk[:, :, :, 0:GD] = wt[:, 0:2 * D].reshape(P, 2 * GC, 4, GD)
    a["g_qk"] = g_qk.reshape(P, 2 * GC, P)
    a["g_v"] = wt[:, 2 * D:]
    g_bits = np.zeros((P, 4, 32), f)
    g_bits[:, :, 0:NB] = i["L0_attn_hex_w"].T[:, None, :]
    g_bits[:, :, NB:2 * NB] = i["L0_attn_q6_w"].T[:, None, :]
    a["g_bits"] = g_bits.reshape(P, P)
    a["g_out"] = i["L0_attn_out_w"].T
    g_tr = np.zeros((NTR, NB, 2 * NB), f)
    g_tr[:, :, NB:] = i["L0_attn_transforms"].transpose(0, 2, 1)
    a["g_tr"] = g_tr
    a["g_trw"] = i["L0_attn_transform_weights"]
    scal = [i["L0_attn_hamming_lambda_logit"], i["L0_attn_scale_logit"], i["L0_attn_sips_alpha"], i["L0_attn_sips_beta"]]
    a["g_scal"] = np.broadcast_to(np.concatenate([s.reshape(1) for s in scal])[None, :], (P, 4))
    a["w_qkv"] = i["L0_ffn_Wqkv"]
    swapped = (np.arange(HD) + HD // 2) % HD
    cols = [i["L0_ffn_q_scale"], i["L0_ffn_q_scale"][:, swapped], i["L0_ffn_k_scale"], i["L0_ffn_k_scale"][:, swapped]]
    a["qk_scale"] = np.tile(np.stack([c.T for c in cols], 2), (2, 1, 1))
    a["w_o"] = i["L0_ffn_Wo"].reshape(DEPTH, QC, P, D).transpose(0, 2, 1, 3)
    w_1 = np.zeros((DEPTH, D, 2, FC * P), f)
    w_1[:, :, :, 0:DIN] = i["L0_ffn_W1"].reshape(DEPTH, D, 2, DIN)
    a["w_1"] = w_1.reshape(DEPTH, D, 2 * FC, P)
    w_2 = np.zeros((DEPTH, FC * P, D), f)
    w_2[:, 0:DIN] = i["L0_ffn_W2"]
    a["w_2"] = w_2.reshape(DEPTH, FC, P, D).transpose(0, 2, 1, 3)
    b_1 = np.zeros((DEPTH, 2, FC * P), f)
    b_1[:, :, 0:DIN] = i["L0_ffn_b1"].reshape(DEPTH, 2, DIN)
    par = np.zeros((DEPTH, P, 3 + 2 * FC), f)
    par[:, :, 0], par[:, :, 1], par[:, :, 2] = i["L0_ffn_ln_g"], i["L0_ffn_ln_b"], i["L0_ffn_b2"]
    par[:, :, 3:] = b_1.reshape(DEPTH, 2 * FC, P).transpose(0, 2, 1)
    a["ffn_par"] = par
    return a


def kernel(**inputs):
    import concourse.bacc as bacc
    from concourse.bass_utils import run_bass_kernel_spmd

    nc = bacc.Bacc("TRN2", target_bir_lowering=False, num_devices=1)
    arrays = {k: np.ascontiguousarray(v) for k, v in {**lay_out(inputs), **constants()}.items()}
    aps = {k: nc.dram_tensor(k + "_dram", v.shape, mybir.dt.from_np(v.dtype), kind="ExternalInput").ap() for k, v in arrays.items()}
    out = nc.dram_tensor("out_dram", (B * T, D), F32, kind="ExternalOutput").ap()
    build(nc, aps, out)
    r = run_bass_kernel_spmd(nc, [{k + "_dram": v for k, v in arrays.items()}], core_ids=[0])
    return r.results[0]["out_dram"].reshape(B, T, D)
```

```python
from contextlib import ExitStack

import numpy as np
import concourse.bass as bass
from concourse import mybir

F32 = mybir.dt.float32
F32R = mybir.dt.float32r
BF16 = mybir.dt.bfloat16
I32 = mybir.dt.int32
ALU = mybir.AluOpType
ACT = mybir.ActivationFunctionType
AX = mybir.AxisListType

P = 128
B, T, D = 8, 256, 128
NT = B * T // P
TT = T // P
GH = 16
GD = D // GH
GC = GH // 4
NTR, NB = 7, 6
TEMP = 0.5
GS = P + T
DEPTH, H, HD, WIN = 6, 16, 64, 32
INNER = H * HD
DIN = D * 4 * 2 // 3
FC = -(-DIN // P)
NU = T // WIN // 2
QW = 2 * WIN
KW = 3 * WIN
QC = INNER // P
NP = QC
NV = 2 * NU
NO = 4
NS = H // 2
VW = HD + 1
QK_SCALE = 8.0
EPS = 1e-5
RSQRT_MAGIC = 0x5F3759DF
NEWTON = 3
RSQRT_STEPS = 2 + 3 * NEWTON
UP = 1
NORM_FLOOR = 1e-24


class Steps:

    def __init__(self, eng, s):
        self.eng, self.s, self.before, self.here = eng, s, 0, 0

    def body(self, before):
        self.before, self.here = before, 0

    def then_wait(self, ins, apart=None):
        self.here += 1
        ins.then_inc(self.s, 1)
        if apart is None:
            self.eng.wait_ge(self.s, self.before + self.here)
        else:
            wait_apart(self.eng, apart, self.s, self.before + self.here)


def wait_apart(eng, up, s, count):
    count = count if isinstance(count, int) else eng.to_reg(count)
    eng.wait_ge(up, 1)
    eng.wait_ge(s, count)


def rsqrt(nc, step, v, t, y, ready=None):
    step.then_wait(nc.vector.tensor_scalar(y.bitcast(I32), v.bitcast(I32), 1, None, ALU.logical_shift_right))
    step.then_wait(nc.vector.tensor_scalar(y.bitcast(I32), y.bitcast(I32), -1.0, float(RSQRT_MAGIC), ALU.mult, ALU.add))
    for k in range(NEWTON):
        step.then_wait(nc.vector.tensor_tensor(t, v, y, ALU.mult))
        step.then_wait(nc.vector.scalar_tensor_tensor(t, t, -0.5, y, ALU.mult, ALU.mult))
        last = nc.vector.scalar_tensor_tensor(y, t, 1.5, y, ALU.add, ALU.mult)
        if k < NEWTON - 1 or ready is None:
            step.then_wait(last)
        else:
            last.then_inc(ready, 1)


def token_norm(nc, dve, step, src, dst, stat, squared, squares_wanted, squares_ready, k):
    s, m, v, t, y = (stat[:, i, :] for i in range(5))
    step.then_wait(nc.vector.tensor_reduce(s, src, AX.X, ALU.add))
    step.then_wait(nc.vector.tensor_scalar(m, s, 1.0 / D, None, ALU.mult))
    nc.vector.tensor_tensor(dst, src, m.unsqueeze(2).to_broadcast([P, NT, D]), ALU.subtract).then_inc(squares_wanted, 1)
    dve.wait_ge(squares_ready, k)
    step.then_wait(nc.vector.tensor_reduce(s, squared, AX.X, ALU.add))
    step.then_wait(nc.vector.tensor_scalar(v, s, 1.0 / D, EPS, ALU.mult, ALU.add))
    rsqrt(nc, step, v, t, y)
    return y.unsqueeze(2).to_broadcast([P, NT, D])


def build_global(nc, x1, X, idf, idb, stage, x, g_qk, g_v, g_bits, g_out, g_tr, g_trw, g_scal, bit_eye, g_low, g_spread, g_mask,
                 ident, w_qkv, w_loaded):
    ctx = ExitStack()
    with ctx:
        def sb(name, shape, dt=F32):
            return ctx.enter_context(nc.sbuf_tensor("g_" + name, shape, dt))

        def sem(name):
            return ctx.enter_context(nc.semaphore("g_" + name))

        xin = sb("xin", [P, NT, D])
        squares = sb("squares", [P, NT, D])
        xnT = sb("xnT", [P, NT, P])
        xb = sb("xb", [P, 2, T])
        y = sb("y", [P, NT, D])
        stat = sb("stat", [P, 5, NT])
        qk = sb("qk", [P, 2 * GC, T], F32R)
        high = sb("high", [P, 2, T], F32R)
        low_rows = sb("low_rows", [P, 3])
        left = sb("left", [P, GC, T], F32R)
        bits = sb("bits", [P, T])
        bits_h = sb("bits_h", [P, P + T], F32R)
        bits_l = sb("bits_l", [P, P + T], F32R)
        val = sb("val", [P, TT, GH, 32])
        th = sb("th", [P, 2, GS])
        sc = sb("sc", [P, 2, GS])
        pr = sb("pr", [P, 2, GS])
        pT = sb("pT", [P, 2, 3, P])
        mx = sb("mx", [P, GH, TT])
        nmx = sb("nmx", [P, GH, TT])
        total = sb("total", [P, GH, TT])
        rtotal = sb("rtotal", [P, GH, TT])
        rT = sb("rT", [GH, T])
        spread = sb("spread", [GH, GC, P])
        o = sb("o", [P, 2, GC, T])
        scal = sb("scal", [P, 8])
        tw = sb("tw", [GH, 48])
        twT = sb("twT", [NTR, GH])
        tr = sb("tr", [NTR, NB, 2 * NB])
        wqk = sb("wqk", [P, 2 * GC, P])
        wv = sb("wv", [P, D])
        wbits = sb("wbits", [P, P])
        wout = sb("wout", [P, GC, D])
        eye = sb("eye", [2 * NB, P])
        mix = sb("mix", [2 * NB, GC * P])
        mask = sb("mask", [P, P + GS], BF16)

        bank = [ctx.enter_context(nc.psum_tensor(f"g_bank{i}", [P, 512], F32)) for i in range(8)]

        x_loaded, id_loaded, w_in = sem("x_loaded"), sem("id_loaded"), sem("weights_loaded")
        dev_ready, squared, normed, step_s = sem("dev_ready"), sem("squared"), sem("normed"), sem("vector_step")
        xt_ready, xt_copied, cleared, mask_ready = sem("xT_ready"), sem("xT_copied"), sem("cleared"), sem("mask_ready")
        half_tanh, tw_shifted, tw_exp, tw_ready = sem("half_tanh"), sem("tw_shifted"), sem("tw_exp"), sem("tw_ready")
        twT_ready, twT_copied, mixed, mix_ready, scal_ready = sem("twT_ready"), sem("twT_copied"), sem("mixed"), sem("mix_ready"), sem("scal_ready")
        xb_ready, qk_ready, qk_copied = sem("xb_ready"), sem("qk_ready"), sem("qk_copied")
        bits_ready, bits_tanh, left_ready, left_copied = sem("bits_ready"), sem("bits_tanh"), sem("left_ready"), sem("left_copied")
        val_ready, val_copied = sem("val_ready"), sem("val_copied")
        high_ready, bits_high, bits_split = sem("high_ready"), sem("bits_high"), sem("bits_split")
        raw_ready, raw_tanh, add_ready, scored, max_ready, exped = (
            sem("raw_ready"), sem("raw_tanh"), sem("addend_ready"), sem("scored"), sem("max_ready"), sem("exped"))
        pT_ready, pT_copied, o_ready, o_copied = sem("pT_ready"), sem("pT_copied"), sem("o_ready"), sem("o_copied")
        r_ready, rT_ready, rT_copied, spread_ready, o_normed = (
            sem("rtotal_ready"), sem("rtotalT_ready"), sem("rtotalT_copied"), sem("rtotal_spread"), sem("o_normed"))
        y_ready, y_copied = sem("y_ready"), sem("y_copied")

        raised = (scored, pT_ready, exped, raw_tanh, o_ready, pT_copied, y_copied, val_ready)
        LOADS = 11
        COLS = slice(P, P + GS)
        block = ctx.enter_context(nc.Block())

        @block.sync
        def _(sp):
            for s in raised:
                sp.sem_inc(s, UP)
            sp.dma_start(x1[:], x.rearrange("(n p) d -> p n d", p=P)).then_inc(x_loaded, 16)
            sp.dma_start(idf[:], ident).then_inc(id_loaded, 16)
            for dst, src in ((scal[:, 0:4], g_scal), (tw[:, 0:NTR], g_trw), (tr[:], g_tr), (eye[:], bit_eye), (low_rows[:], g_low), (spread[:], g_spread),
                             (wqk[:], g_qk), (wbits[:], g_bits), (wv[:], g_v), (wout[:], g_out), (sc[:, 1, :], g_mask)):
                sp.dma_start(dst, src).then_inc(w_in, 16)
            sp.dma_start(stage[:], w_qkv[0]).then_inc(w_loaded, 16)

        @block.gpsimd
        def _(pool):
            nc.gpsimd.memset(X[:, :, 0:1], 0.0)
            nc.gpsimd.memset(mask[:, 0:P], 0.0)
            nc.gpsimd.memset(val[:], 0.0)
            nc.gpsimd.memset(bits_h[:, 0:P].bitcast(F32), 0.0)
            nc.gpsimd.memset(bits_l[:, 0:P].bitcast(F32), 0.0)
            nc.gpsimd.memset(mix[:], 0.0).then_inc(cleared, 1)
            pool.wait_ge(w_in, 16 * LOADS)
            pool.wait_ge(id_loaded, 16)
            nc.gpsimd.tensor_copy(idb[:], idf[:])
            nc.gpsimd.tensor_copy(mask[:, P:], sc[:, 1, :]).then_inc(mask_ready, 1)
            pool.wait_ge(xt_copied, NT // 4)
            with pool.Fori(0, B // 2) as bb:
                for i in range(2):
                    b = bb * 2 + i
                    wait_apart(pool, cleared, val_ready, UP + (b - 1 if i else bb * 2))
                    nc.gpsimd.tensor_copy(xb[:, i, :], xnT[:, bass.ds(b * TT, TT), :].rearrange("p t k -> p (t k)")).then_inc(xb_ready, 1)
                    wait_apart(pool, cleared, bits_tanh, b + 1)
                    nc.gpsimd.tensor_copy(bits_h[:, P:], bits[:]).then_inc(bits_high, 1)
                    wait_apart(pool, cleared, bits_high, b + 1)
                    nc.gpsimd.tensor_tensor(bits_l[:, P:], bits[:], bits_h[:, P:].bitcast(F32), ALU.subtract).then_inc(bits_split, 1)

        @block.scalar
        def _(act):
            def square(k):
                act.wait_ge(dev_ready, k)
                nc.scalar.activation(squares[:], xin[:], ACT.Square).then_inc(squared, 1)

            square(1)
            act.wait_ge(w_in, 16 * LOADS)
            nc.scalar.activation(scal[:, 4:6], scal[:, 0:2], ACT.Tanh, scale=0.5).then_inc(half_tanh, 1)
            act.wait_ge(tw_shifted, 1)
            nc.scalar.activation(tw[:, 16:16 + NTR], tw[:, 8:8 + NTR], ACT.Exp, scale=1.0 / TEMP,
                                 accum_out=tw[:, 24:25]).then_inc(tw_exp, 1)
            for i in range(NT // 4):
                act.wait_ge(xt_ready, i + 1)
                nc.scalar.activation(xnT[:, 4 * i:4 * i + 4, :], bank[i % 2][:].rearrange("p (n k) -> p n k", n=4),
                                     ACT.Copy).then_inc(xt_copied, 1)
            act.wait_ge(scal_ready, 1)
            with act.Fori(0, B) as b:
                for c in range(2 * GC):
                    act.wait_ge(qk_ready, b * 2 * GC + c + 1)
                    nc.scalar.activation(high[:, c % 2, :], bank[c % 2][:, 0:T], ACT.Copy).then_inc(high_ready, 1)
                act.wait_ge(bits_ready, b + 1)
                nc.scalar.activation(bits[:], bank[2][:, 0:T], ACT.Tanh).then_inc(bits_tanh, 1)
                act.wait_ge(val_ready, UP + b + 1)
                nc.scalar.activation(val[:, :, :, 0:GD], bank[3][:, 0:T].rearrange("p (t h d) -> p t h d", t=TT, h=GH),
                                     ACT.Copy).then_inc(val_copied, 1)
                for c in range(GC):
                    act.wait_ge(left_ready, b * GC + c + 1)
                    nc.scalar.activation(high[:, c % 2, :], bank[c % 2][:, 0:T], ACT.Copy).then_inc(high_ready, 1)

                def exps(h):
                    act.wait_ge(max_ready, b * GH + h + 1)
                    act.wait_ge(pT_ready, UP + b * GH + max(h - 1, 0))
                    nc.scalar.activation(pr[:, h % 2, 0:P], sc[:, h % 2, 0:P], ACT.Exp, bias=nmx[:, h, 0:1],
                                         accum_out=total[:, h, 0:1])
                    nc.scalar.activation(pr[:, h % 2, P:GS], sc[:, h % 2, P:GS], ACT.Exp, bias=nmx[:, h, 1:2],
                                         accum_out=total[:, h, 1:2]).then_inc(exped, 1)

                for h in range(GH):
                    act.wait_ge(raw_ready, b * GH + h + 1)
                    act.wait_ge(scored, UP + b * GH + max(h - 1, 0))
                    nc.scalar.activation(th[:, h % 2, :], bank[h % 2][:, COLS], ACT.Tanh, scale=scal[:, 6:7]).then_inc(raw_tanh, 1)
                    if h:
                        exps(h - 1)
                exps(GH - 1)
                act.wait_ge(o_ready, UP + (b + 1) * GH)
                for i in range(2):
                    nc.scalar.activation(o[:, 0, 2 * i:2 * i + 2, :], bank[6 + i][:].rearrange("p (c q) -> p c q", c=2),
                                         ACT.Copy).then_inc(o_copied, 1)
                act.wait_ge(y_ready, b + 1)
                nc.scalar.activation(y[:, bass.ds(b * TT, TT), :], bank[6][:, 0:T].rearrange("p (t d) -> p t d", t=TT),
                                     ACT.Copy).then_inc(y_copied, 1)
            square(2)
            square(3)
            for i in range(NT // 4):
                act.wait_ge(xt_ready, NT // 4 + i + 1)
                nc.scalar.activation(X[:, 2 * i:2 * i + 2, 1:1 + T], bank[i % 2][:].rearrange("p (b t) -> p b t", b=2),
                                     ACT.Copy).then_inc(xt_copied, 1)

        @block.vector
        def _(dve):
            step = Steps(dve, step_s)
            dve.wait_ge(x_loaded, 16)
            r = token_norm(nc, dve, step, x1[:], xin[:], stat, squares[:], dev_ready, squared, 1)
            nc.vector.tensor_tensor(xin[:], xin[:], r, ALU.mult).then_inc(normed, 1)
            dve.wait_ge(w_in, 16 * LOADS)
            step.then_wait(nc.vector.tensor_reduce(tw[:, 25:26], tw[:, 0:NTR], AX.X, ALU.max))
            nc.vector.tensor_scalar(tw[:, 8:8 + NTR], tw[:, 0:NTR], tw[:, 25:26], None, ALU.subtract).then_inc(tw_shifted, 1)
            dve.wait_ge(tw_exp, 1)
            step.then_wait(nc.vector.reciprocal(tw[:, 26:27], tw[:, 24:25]))
            nc.vector.tensor_scalar(tw[:, 32:32 + NTR], tw[:, 16:16 + NTR], tw[:, 26:27], None, ALU.mult).then_inc(tw_ready, 1)
            dve.wait_ge(half_tanh, 1)
            nc.vector.tensor_scalar(scal[:, 4:5], scal[:, 4:5], 0.25, 0.25, ALU.mult, ALU.add)
            nc.vector.tensor_scalar(scal[:, 5:6], scal[:, 5:6], 1.0 / NB, 1.0 / NB, ALU.mult, ALU.add)
            nc.vector.reciprocal(scal[:, 6:7], scal[:, 3:4]).then_inc(scal_ready, 1)
            dve.wait_ge(scal_ready, 1)
            dve.wait_ge(twT_ready, 1)
            nc.vector.tensor_copy(twT[:], bank[7][0:NTR, 0:GH]).then_inc(twT_copied, 1)
            dve.wait_ge(mixed, 1)
            dve.wait_ge(cleared, 1)
            for copy in range(2):
                at = 2 * NB * copy + NB
                last = nc.vector.tensor_scalar(mix[:].rearrange("p (h e) -> p h e", h=GH)[:, :, at:at + NB],
                                               bank[6][0:2 * NB, 0:NB * GH].rearrange("p (e h) -> p h e", e=NB),
                                               scal[0:2 * NB, 5:6], None, ALU.mult)
            step.then_wait(last)
            for c in range(GC):
                last = nc.vector.scalar_tensor_tensor(mix[:, P * c:P * c + P], eye[:], scal[0:2 * NB, 4:5],
                                                      mix[:, P * c:P * c + P], ALU.mult, ALU.add)
            last.then_inc(mix_ready, 1)
            base = step.here
            BODY = GH

            with dve.Fori(0, B) as b:
                step.body(base + b * BODY)

                def stack(dst, c, k, kind, done):
                    dve.wait_ge(high_ready, b * 3 * GC + k + 1)
                    nc.vector.scalar_tensor_tensor(dst, high[:, c % 2, :].bitcast(F32), low_rows[:, kind:kind + 1],
                                                   bank[c % 2][:, 0:T], ALU.mult, ALU.add).then_inc(done, 1)

                for c in range(2 * GC):
                    stack(qk[:, c, :], c, c, c // GC, qk_copied)
                for c in range(GC):
                    stack(left[:, c, :], c, 2 * GC + c, 2, left_copied)

                def score(h):
                    dve.wait_ge(raw_tanh, UP + b * GH + h + 1)
                    dve.wait_ge(add_ready, b * GH + h + 1)
                    dve.wait_ge(exped, UP + b * GH + max(h - 1, 0))
                    nc.vector.scalar_tensor_tensor(sc[:, h % 2, :], th[:, h % 2, :], scal[:, 2:3], bank[2 + h % 2][:, COLS],
                                                   ALU.mult, ALU.add).then_inc(scored, 1)
                    dve.wait_ge(scored, UP + b * GH + h + 1)
                    nc.vector.tensor_reduce(mx[:, h, 0:1], sc[:, h % 2, 0:P], AX.X, ALU.max)
                    step.then_wait(nc.vector.tensor_reduce(mx[:, h, 1:2], sc[:, h % 2, P:GS], AX.X, ALU.max))
                    nc.vector.tensor_scalar(nmx[:, h, :], mx[:, h, :], -1.0, None, ALU.mult).then_inc(max_ready, 1)

                def copy_pT(h):
                    dve.wait_ge(pT_ready, UP + b * GH + h + 1)
                    dve.wait_ge(o_ready, UP + b * GH + max(h - 1, 0))
                    nc.vector.tensor_copy(pT[:, h % 2, :, :], bank[4 + h % 2][:, 0:GS].rearrange("p (t q) -> p t q", t=3)).then_inc(pT_copied, 1)

                for h in range(GH + 2):
                    if h < GH:
                        score(h)
                    if h == GH:
                        dve.wait_ge(exped, UP + (b + 1) * GH)
                        nc.vector.reciprocal(rtotal[:], total[:]).then_inc(r_ready, 1)
                    if h >= 2:
                        copy_pT(h - 2)
                dve.wait_ge(rT_ready, b + 1)
                nc.vector.tensor_copy(rT[:], bank[3][0:GH, 0:T]).then_inc(rT_copied, 1)
                dve.wait_ge(spread_ready, b + 1)
                for i in range(2):
                    dve.wait_ge(o_copied, b * 2 + i + 1)
                    nc.vector.tensor_tensor(o[:, 1, 2 * i:2 * i + 2, :], o[:, 0, 2 * i:2 * i + 2, :],
                                            bank[4 + i][:].rearrange("p (c q) -> p c q", c=2), ALU.mult).then_inc(o_normed, 1)
                assert step.here == BODY
            step.body(base + B * BODY)
            dve.wait_ge(y_copied, UP + B)
            r = token_norm(nc, dve, step, y[:], xin[:], stat, squares[:], dev_ready, squared, 2)
            step.then_wait(nc.vector.tensor_tensor(xin[:], xin[:], r, ALU.mult))
            step.then_wait(nc.vector.tensor_tensor(x1[:], x1[:], xin[:], ALU.add))
            r = token_norm(nc, dve, step, x1[:], xin[:], stat, squares[:], dev_ready, squared, 3)
            nc.vector.tensor_tensor(xin[:], xin[:], r, ALU.mult).then_inc(normed, 1)

        @block.tensor
        def _(pe):
            mm = nc.tensor.matmul

            def to_features(k):
                for i in range(NT // 4):
                    if i >= 2:
                        pe.wait_ge(xt_copied, k * NT // 4 + i - 1)
                    for q in range(4):
                        last = nc.tensor.transpose(bank[i % 2][:, P * q:P * q + P], xin[:, 4 * i + q, :], idf[:])
                    last.then_inc(xt_ready, 1)

            pe.wait_ge(id_loaded, 16)
            pe.wait_ge(normed, 1)
            to_features(0)
            pe.wait_ge(tw_ready, 1)
            nc.tensor.transpose(bank[7][0:NTR, 0:GH], tw[:, 32:32 + NTR], idf[0:GH, 0:GH]).then_inc(twT_ready, 1)
            pe.wait_ge(w_in, 16 * LOADS)
            pe.wait_ge(twT_copied, 1)
            for e in range(NB):
                last = mm(bank[6][0:2 * NB, GH * e:GH * e + GH], tr[:, e, :], twT[:], start=True, stop=True)
            last.then_inc(mixed, 1)
            pe.wait_ge(mix_ready, 1)
            pe.wait_ge(mask_ready, 1)
            pe.wait_ge(xt_copied, NT // 4)

            with pe.Fori(0, B // 2) as bb:
                for i in range(2):
                    b = bb * 2 + i
                    xs = xb[:, i, :]
                    pe.wait_ge(xb_ready, b + 1)
                    pe.wait_ge(raw_tanh, UP + b * GH)
                    pe.wait_ge(scored, UP + b * GH)
                    for c in range(2 * GC):
                        if c >= 2:
                            pe.wait_ge(qk_copied, b * 2 * GC + c - 1)
                        mm(bank[c % 2][:, 0:T], wqk[:, c, :], xs, start=True, stop=True).then_inc(qk_ready, 1)
                    mm(bank[2][:, 0:T], wbits[:], xs, start=True, stop=True).then_inc(bits_ready, 1)
                    for t in range(TT):
                        last = mm(bank[3][:, D * t:D * t + D], xs[:, P * t:P * t + P], wv[:], start=True, stop=True)
                    last.then_inc(val_ready, 1)
                    pe.wait_ge(bits_tanh, b + 1)
                    for c in range(GC):
                        pe.wait_ge(qk_copied, b * 2 * GC + 2 * GC - 1 + min(c, 1))
                        if c >= 2:
                            pe.wait_ge(left_copied, b * GC + c - 1)
                        mm(bank[c % 2][:, 0:T], mix[:, P * c:P * c + P], bits[0:2 * NB, :], start=True, stop=True).then_inc(left_ready, 1)

                    def scores(h):
                        c, r0 = h // 4, 32 * (h % 4)
                        if h < 2:
                            pe.wait_ge(left_copied, (b + 1) * GC)
                            pe.wait_ge(bits_split, b + 1)
                            pe.wait_ge(val_copied, b + 1)
                        else:
                            pe.wait_ge(raw_tanh, UP + b * GH + h - 1)
                            pe.wait_ge(scored, UP + b * GH + h - 1)
                        raw, add = bank[h % 2], bank[2 + h % 2]
                        k_at, rows, few = (GC + c) * T, slice(r0, r0 + 3 * GD), slice(r0, r0 + 2 * NB)
                        q, k = qk[rows, c, :], qk[rows, :, :].rearrange("p c t -> p (c t)")
                        mm(raw[:, 0:T], q[:, 0:P], k[:, k_at - P:k_at + P], start=True, stop=True, tile_position=(r0, 0))
                        mm(raw[:, T:2 * T], q[:, P:T], k[:, k_at:k_at + T], start=True, stop=True, tile_position=(r0, 0)).then_inc(raw_ready, 1)
                        mm(add[:], idb[:], mask[:], start=True, stop=False)
                        for t in range(TT):
                            dst, lf = add[:, T * t:T * t + T], left[:, c, P * t:P * t + P]
                            keys = slice(P * t, P * t + T)
                            mm(dst, lf[r0:r0 + 4 * NB], bits_h[r0:r0 + 4 * NB, keys], start=False, stop=False, tile_position=(r0, 0))
                            last = mm(dst, lf[few], bits_l[few, keys], start=False, stop=t == TT - 1, tile_position=(r0, 0))
                        last.then_inc(add_ready, 1)

                    def transpose_probs(h):
                        pe.wait_ge(exped, UP + b * GH + h + 1)
                        pe.wait_ge(pT_copied, UP + b * GH + max(h - 1, 0))
                        for t in range(3):
                            last = nc.tensor.transpose(bank[4 + h % 2][:, P * t:P * t + P], pr[:, h % 2, P * t:P * t + P], idf[:])
                        last.then_inc(pT_ready, 1)

                    def weigh_values(h):
                        pe.wait_ge(pT_copied, UP + b * GH + h + 1)
                        if h == 0:
                            pe.wait_ge(y_copied, UP + b)
                        c, r0 = h // 4, 32 * (h % 4)
                        dst, at = bank[6 + c // 2][r0:r0 + 32, :], T * (c % 2)
                        mm(dst[:, at:at + T], val[:, 0, h, :], pT[:, h % 2, 0:2, :].rearrange("p t q -> p (t q)"),
                           start=True, stop=False, tile_position=(0, r0))
                        mm(dst[:, at + P:at + T], val[:, 1, h, :], pT[:, h % 2, 2, :], start=False, stop=True,
                           tile_position=(0, r0)).then_inc(o_ready, 1)

                    scores(0)
                    scores(1)
                    for h in range(GH):
                        if h + 2 < GH:
                            scores(h + 2)
                        transpose_probs(h)
                        if h:
                            weigh_values(h - 1)
                    pe.wait_ge(r_ready, b + 1)
                    for t in range(TT):
                        last = nc.tensor.transpose(bank[3][0:GH, P * t:P * t + P], rtotal[:, :, t], idf[:])
                    last.then_inc(rT_ready, 1)
                    weigh_values(GH - 1)
                    pe.wait_ge(rT_copied, b + 1)
                    for c in range(GC):
                        last = mm(bank[4 + c // 2][:, T * (c % 2):T * (c % 2) + T], spread[:, c, :], rT[:], start=True, stop=True)
                    last.then_inc(spread_ready, 1)
                    pe.wait_ge(o_normed, (b + 1) * 2)
                    for t in range(TT):
                        for c in range(GC):
                            last = mm(bank[6][:, D * t:D * t + D], o[:, 1, c, P * t:P * t + P], wout[:, c, :],
                                      start=c == 0, stop=c == GC - 1)
                    last.then_inc(y_ready, 1)
            pe.wait_ge(normed, 2)
            to_features(1)


def build_layers(nc, x1, X, idf, idb, stage, w_loaded, w_qkv, qk_scale, w_o, ffn_par, w_1, w_2, rot, w_mask, pat, sel, out):
    ctx = ExitStack()
    with ctx:
        def sb(name, shape, dt=F32):
            return ctx.enter_context(nc.sbuf_tensor(name, shape, dt))

        def sem(name):
            return ctx.enter_context(nc.semaphore(name))

        WQ = 2 * INNER
        wh = sb("wh", [P, 3 * INNER], F32R)
        wl = sb("wl", [P, 3 * INNER], F32R)
        wsh = sb("wsh", [P, WQ], F32R)
        wsl = sb("wsl", [P, WQ], F32R)
        wo = sb("wo", [P, QC, D])
        w1 = sb("w1", [P, 2 * FC, P])
        w2 = sb("w2", [P, FC, D])
        fpar = sb("fpar", [P, 3 + 2 * FC])
        qks = sb("qks", [P, DEPTH, 4])
        rotb = sb("rotb", [P, 4, T])
        rots = sb("rots", [P, 4, T])
        xh = sb("xh", [P, WIN + T], F32R)
        xl = sb("xl", [P, WIN + T], F32R)
        sq = sb("sq", [P, 2, 2, T])
        patb = sb("patb", [P, 2])
        selb = sb("sel", [2 * H, 2 * QC, P], F32R)
        part = sb("part", [P, 2 * QC, T])
        sinp = sb("sinp", [P, 2, 2, T])
        nrm = sb("nrm", [P, 3, TT * 2 * H + TT])
        rh = sb("rh", [2 * H, T], F32R)
        rl = sb("rl", [2 * H, T], F32R)
        qT = sb("qT", [P, QC, T])
        kT = sb("kT", [P, QC, WIN + T])
        V = sb("V", [KW, NU, H, VW])
        wmask = sb("wmask", [P, NU * KW], BF16)
        mx = sb("mx", [P, 2, NU])
        pr = sb("pr", [P, 2, NU * KW])
        pT = sb("pT", [KW, 2, NU, P])
        rden = sb("rden", [P, 2, TT, 2])
        O = sb("O", [P, TT, H, HD])
        OT = sb("OT", [P, QC, T])
        xf = sb("xf", [P, T])
        dev = sb("dev", [P, T])
        dsq = sb("dsq", [P, T])
        dg = sb("dg", [P, TT, P])
        t1 = sb("t1", [P, T])
        xn = sb("xn", [P, T])
        mean1 = sb("mean1", [P, P])
        ones = sb("ones", [P, P])
        gl = sb("gl", [P, 2, T])
        hid = sb("hid", [P, FC, T])
        stat = sb("stat", [P, 5, NT])

        bank = [ctx.enter_context(nc.psum_tensor(f"bank{i}", [P, 512], F32)) for i in range(8)]
        NRM = bank[4][:, 0:TT * 2 * H]
        NRT = bank[5][0:2 * H, 0:T]

        const_in, tail_in = sem("constants_loaded"), sem("tail_weights_loaded")
        cleared, wmask_ready, sel_ready = sem("cleared"), sem("wmask_ready"), sem("sel_ready")
        v_step, t_step, p_step = sem("vector_step"), sem("vector_tail_step"), sem("pool_step")
        w_high, ws_high, w_low, ws_low, rot_ready = sem("w_high"), sem("w_swapped_high"), sem("w_low"), sem("w_swapped_low"), sem("rot_ready")
        xs_ready, raw_ready, squared, turned, summed, norm_done = (
            sem("xs_ready"), sem("raw_ready"), sem("squared"), sem("turned"), sem("summed"), sem("norm_done"))
        root_ready, rt_ready, rn_ready = sem("rnorm_ready"), sem("rnormT_ready"), sem("rnorm_split")
        v_ready, v_copied, rb_ready, scaled = sem("v_ready"), sem("v_copied"), sem("rbroadcast_ready"), sem("qk_scaled")
        s_ready, centered, exped, pt_ready, pt_copied, o_ready, o_read = (
            sem("scores_ready"), sem("centered"), sem("exped"), sem("pT_ready"), sem("pT_copied"), sem("o_ready"), sem("o_read"))
        ot_ready, ot_copied, y_ready, xf_ready = sem("oT_ready"), sem("oT_copied"), sem("y_ready"), sem("xf_ready")
        mean_ready, dev_ready, dsq_ready, var_ready, dg_ready, rs_ready, xn_ready = (
            sem("mean_ready"), sem("dev_ready"), sem("dsq_ready"), sem("var_ready"), sem("diagonal_ready"), sem("rstd_ready"), sem("xn_ready"))
        h_ready, gelu_ready, hid_ready, y2_ready, x_updated = (
            sem("hidden_ready"), sem("gelu_ready"), sem("gated"), sem("ffn_ready"), sem("x_updated"))
        xt_ready, fdev_ready, fsquared, finished, stored = (
            sem("xT_ready"), sem("final_dev_ready"), sem("final_squared"), sem("finished"), sem("stored"))

        raised = (norm_done, summed, o_ready, pt_ready, ot_ready, y_ready, hid_ready, v_ready, centered, pt_copied, o_read)
        NORMS = TT * 2 * H
        CONSTS, TAILS, WPARTS, SWAPPED = 5, 4, 3, 2
        partf = part[:].rearrange("p a t -> p (a t)")
        mask_in = partf[:, 2 * QC * T - NU * KW:2 * QC * T]
        sel_in = partf[0:2 * H, 0:2 * QC * P]
        fdev = partf[:, 0:NT * D].rearrange("p (n d) -> p n d", d=D)
        fy = partf[:, NT * D:2 * NT * D].rearrange("p (n d) -> p n d", d=D)
        fsq = stage[:, 0:NT * D].rearrange("p (n d) -> p n d", d=D)

        ORDER = [p for c in range(NP // 2) for p in (c, NP // 2 + c)]

        def swap(t):
            return t.rearrange("p (h s d) -> p h s d", s=2, d=HD // 2)

        def pair(t):
            return t.rearrange("p (a t) -> p a t", a=2)

        def tail_weights(n):
            return 16 * TAILS * ((n + B - 1) // B)

        def walk(eng, top, step):
            top(0)
            step(0, 0, False)
            with eng.Fori(1, B) as b:
                step(b, b, True)
            with eng.Fori(1, DEPTH) as l:
                top(l)
                with eng.Fori(0, B) as b:
                    step(l * B + b, b, True)

        block = ctx.enter_context(nc.Block())

        @block.sync
        def _(sp):
            for s in raised:
                sp.sem_inc(s, UP)
            sp.sem_inc(x_updated, B)
            for dst, src in ((rotb[:], rot), (qks[:], qk_scale), (mask_in, w_mask), (patb[:], pat), (sel_in, sel)):
                sp.dma_start(dst, src).then_inc(const_in, 16)

            def load_tail(l):
                for dst, src in ((wo[:], w_o), (w1[:], w_1), (w2[:], w_2), (fpar[:], ffn_par)):
                    sp.dma_start(dst, src[l]).then_inc(tail_in, 16)

            load_tail(0)
            with sp.Fori(1, DEPTH) as l:
                low, high = sp.to_reg(WPARTS * l), sp.to_reg(SWAPPED * l)
                sp.wait_ge(w_low, low)
                sp.wait_ge(ws_high, high)
                sp.dma_start(stage[:], w_qkv[l]).then_inc(w_loaded, 16)
                sp.wait_ge(x_updated, B + l * B)
                load_tail(l)

        @block.gpsimd
        def _(pool):
            step = Steps(pool, p_step)
            nc.gpsimd.memset(mean1[:], 1.0 / D)
            nc.gpsimd.memset(ones[:], 1.0)
            nc.gpsimd.memset(V[:, :, :, HD:VW], 1.0)
            nc.gpsimd.memset(kT[:, :, 0:WIN], 0.0)
            nc.gpsimd.memset(xh[:, 0:WIN].bitcast(F32), 0.0)
            nc.gpsimd.memset(xl[:, 0:WIN].bitcast(F32), 0.0).then_inc(cleared, 1)
            pool.wait_ge(cleared, 1)
            pool.wait_ge(const_in, 16 * CONSTS)
            nc.gpsimd.tensor_copy(wmask[:], mask_in).then_inc(wmask_ready, 1)
            pool.wait_ge(wmask_ready, 1)
            BODY = 1

            def prepare(n, b):
                step.body(n * BODY)
                wait_apart(pool, cleared, x_updated, n + 1)
                wait_apart(pool, cleared, v_ready, UP + n * NV)
                wait_apart(pool, cleared, summed, UP + n * NP)
                nc.gpsimd.tensor_copy(xh[0:64, WIN:WIN + T], X[0:64, b, 1:1 + T])
                step.then_wait(nc.gpsimd.tensor_copy(xh[64:P, WIN:WIN + T], X[64:P, b, 0:T]), cleared)
                nc.gpsimd.tensor_tensor(xl[0:64, WIN:WIN + T], X[0:64, b, 1:1 + T], xh[0:64, WIN:WIN + T].bitcast(F32), ALU.subtract)
                nc.gpsimd.tensor_tensor(xl[64:P, WIN:WIN + T], X[64:P, b, 0:T], xh[64:P, WIN:WIN + T].bitcast(F32),
                                        ALU.subtract).then_inc(xs_ready, 1)
                assert step.here == BODY

            def add_parts(n):
                for p in range(NP):
                    pool.wait_ge(turned, n * NP + p + 1)
                    nc.gpsimd.tensor_tensor(part[:, 2 * p:2 * p + 2, :], part[:, 2 * p:2 * p + 2, :], sinp[:, p % 2, :, :],
                                            ALU.add).then_inc(summed, 1)

            with pool.Fori(0, DEPTH) as l:
                with pool.Fori(0, B) as b:
                    prepare(l * B + b, b)
                    add_parts(l * B + b)

        @block.scalar
        def _(act):
            def top(l):
                act.wait_ge(w_loaded, 16 * (l + 1))
                act.wait_ge(v_ready, UP + l * B * NV)
                for t in range(SWAPPED):
                    at = slice(INNER * t, INNER * t + INNER)
                    for s in range(2):
                        last = nc.scalar.activation(swap(wsh[:, at])[:, :, s, :], swap(stage[:, at])[:, :, 1 - s, :], ACT.Copy)
                    last.then_inc(ws_high, 1)
                    act.wait_ge(w_low, l * WPARTS + t + 1)
                    for s in range(2):
                        last = nc.scalar.activation(swap(wsl[:, at])[:, :, s, :], swap(wl[:, at].bitcast(F32))[:, :, 1 - s, :], ACT.Copy)
                    last.then_inc(ws_low, 1)

            def square(n, p):
                act.wait_ge(raw_ready, n * NP + p + 1)
                act.wait_ge(norm_done, UP + n * NP + max(p - 1, 0))
                nc.scalar.activation(sq[:, p % 2, :, :], pair(bank[2 + p % 2][:]), ACT.Square).then_inc(squared, 1)

            def copy_values(n, j):
                if j == 0:
                    act.wait_ge(o_ready, UP + n * NS)
                act.wait_ge(v_ready, UP + n * NV + j + 1)
                u, half = j // 2, j % 2
                nc.scalar.activation(V[:, u, 8 * half:8 * half + 8, 0:HD], bank[j % 4][0:KW, :].rearrange("p (h d) -> p h d", d=HD),
                                     ACT.Copy).then_inc(v_copied, 1)

            def probs(n, c):
                act.wait_ge(centered, UP + n * NS + c + 1)
                nc.scalar.activation(pr[:, c % 2, :], pr[:, c % 2, :], ACT.Exp, scale=QK_SCALE).then_inc(exped, 1)

            def copy_pT(n, c):
                act.wait_ge(pt_ready, UP + n * NS + c + 1)
                act.wait_ge(o_ready, UP + n * NS + max(c - 1, 0))
                nc.scalar.activation(pT[:, c % 2, :, :], bank[2 + c % 2][0:KW, :].rearrange("p (u q) -> p u q", u=NU), ACT.Copy).then_inc(pt_copied, 1)

            def copy_oT(m, k):
                if k == 0:
                    act.wait_ge(y_ready, UP + m)
                act.wait_ge(ot_ready, UP + m * NO + k + 1)
                i, c = k // 2, 4 * (k % 2)
                nc.scalar.activation(OT[:, c:c + 4, P * i:P * i + P], bank[6 + k % 2][:].rearrange("p (c q) -> p c q", c=4),
                                     ACT.Copy).then_inc(ot_copied, 1)

            def square_dev(m):
                act.wait_ge(dev_ready, m + 1)
                nc.scalar.activation(dsq[:], dev[:], ACT.Square).then_inc(dsq_ready, 1)

            def gelu(m, j):
                act.wait_ge(h_ready, m * FC + j + 1)
                act.wait_ge(hid_ready, UP + m * FC + max(j - 1, 0))
                nc.scalar.activation(gl[:, j % 2, :], bank[6 + j % 2][:, 0:T], ACT.Gelu, bias=fpar[:, 3 + FC + j:4 + FC + j]).then_inc(gelu_ready, 1)

            def step(n, b, tail):
                m = n - 1
                for p in range(NP):
                    square(n, p)
                    if tail and 1 <= p <= NO:
                        copy_oT(m, p - 1)
                if tail:
                    square_dev(m)
                    act.wait_ge(tail_in, tail_weights(n))
                for j in range(NV):
                    copy_values(n, j)
                    if tail and j >= NV - 2:
                        gelu(m, j - NV + 2)
                if tail:
                    gelu(m, 2)
                probs(n, 0)
                for c in range(NS):
                    copy_pT(n, c)
                    if c + 1 < NS:
                        probs(n, c + 1)

            act.wait_ge(const_in, 16 * CONSTS)
            nc.scalar.activation(selb[:].rearrange("p c m -> p (c m)"), sel_in, ACT.Copy).then_inc(sel_ready, 1)
            walk(act, top, step)
            m = DEPTH * B - 1
            for k in range(NO):
                copy_oT(m, k)
            square_dev(m)
            for j in range(FC):
                gelu(m, j)
            act.wait_ge(fdev_ready, 1)
            nc.scalar.activation(fsq, fdev, ACT.Square).then_inc(fsquared, 1)
            act.wait_ge(finished, 1)
            act.dma_start(out.rearrange("(n p) d -> p n d", p=P), x1[:]).then_inc(stored, 16)
            act.wait_ge(stored, 16)

        @block.vector
        def _(dve):
            step_v, step_t = Steps(dve, v_step), Steps(dve, t_step)
            V_BODY = (1 + RSQRT_STEPS - 1) + 1 + 2 * NS
            T_BODY = 1 + 1

            def top(l):
                dve.wait_ge(w_loaded, 16 * (l + 1))
                dve.wait_ge(v_ready, UP + l * B * NV)
                for t in range(WPARTS):
                    at = slice(INNER * t, INNER * t + INNER)
                    nc.vector.tensor_copy(wh[:, at], stage[:, at]).then_inc(w_high, 1)
                    dve.wait_ge(w_high, l * WPARTS + t + 1)
                    nc.vector.tensor_tensor(wl[:, at], stage[:, at], wh[:, at].bitcast(F32), ALU.subtract).then_inc(w_low, 1)
                    if t == 0:
                        dve.wait_ge(const_in, 16 * CONSTS)
                        for k in range(4):
                            last = nc.vector.tensor_scalar(rots[:, k, :], rotb[:, k, :], qks[:, bass.ds(l, 1), k:k + 1].rearrange("p l k -> p (l k)"), None, ALU.mult)
                        last.then_inc(rot_ready, 1)
                dve.wait_ge(sel_ready, 1)
                dve.wait_ge(wmask_ready, 1)
                wait_apart(dve, cleared, rot_ready, l + 1)

            def rotate(n, p):
                k = 0 if p < NP // 2 else 2
                dve.wait_ge(raw_ready, n * NP + p + 1)
                nc.vector.tensor_tensor(part[:, 2 * p:2 * p + 2, :], pair(bank[p % 2][:]),
                                        rots[:, k, :].unsqueeze(1).to_broadcast([P, 2, T]), ALU.mult)
                dve.wait_ge(squared, n * NP + p + 1)
                dve.wait_ge(summed, UP + n * NP + max(p - 1, 0))
                nc.vector.tensor_tensor(sinp[:, p % 2, :, :], pair(bank[2 + p % 2][:]),
                                        rots[:, k + 1, :].unsqueeze(1).to_broadcast([P, 2, T]), ALU.mult).then_inc(turned, 1)

            def roots(n, m, tail, heads=True):
                lo, hi = 0 if heads else NORMS, NORMS + TT if tail else NORMS
                v, t, y = (nrm[:, i, lo:hi] for i in range(3))
                if heads:
                    dve.wait_ge(norm_done, UP + (n + 1) * NP)
                    last = nc.vector.tensor_scalar(nrm[:, 0, 0:NORMS], NRM, NORM_FLOOR, None, ALU.max)
                if tail:
                    dve.wait_ge(var_ready, m + 1)
                    last = nc.vector.tensor_scalar(nrm[:, 0, NORMS:NORMS + TT], bank[6][:, 0:TT], EPS, None, ALU.add)
                step_v.then_wait(last)
                rsqrt(nc, step_v, v, t, y, root_ready)
                dve.wait_ge(root_ready, n + 1)

            def split_norms(n):
                dve.wait_ge(rt_ready, n + 1)
                step_v.then_wait(nc.vector.tensor_copy(rh[:], NRT))
                nc.vector.tensor_tensor(rl[:], NRT, rh[:].bitcast(F32), ALU.subtract).then_inc(rn_ready, 1)

            def scale(n, k):
                p = ORDER[k]
                dve.wait_ge(rb_ready, n * NP + k + 1)
                dve.wait_ge(summed, UP + n * NP + p + 1)
                dst = qT[:, 2 * p:2 * p + 2, :] if p < NP // 2 else kT[:, 2 * p - QC:2 * p - QC + 2, WIN:WIN + T]
                nc.vector.tensor_tensor(dst, part[:, 2 * p:2 * p + 2, :], pair(bank[k % 4][:]), ALU.mult).then_inc(scaled, 1)

            def center(n, c):
                dve.wait_ge(s_ready, n * NS + c + 1)
                dve.wait_ge(pt_ready, UP + n * NS + max(c - 1, 0))
                s3 = bank[4 + c % 2][:, 0:NU * KW].rearrange("p (u k) -> p u k", u=NU)
                step_v.then_wait(nc.vector.tensor_reduce(mx[:, c % 2, :], s3, AX.X, ALU.max))
                nc.vector.tensor_tensor(pr[:, c % 2, :].rearrange("p (u k) -> p u k", u=NU), s3,
                                        mx[:, c % 2, :].unsqueeze(2).to_broadcast([P, NU, KW]), ALU.subtract).then_inc(centered, 1)

            def take_o(n, c):
                dve.wait_ge(o_ready, UP + n * NS + c + 1)
                if c == 0:
                    dve.wait_ge(ot_ready, UP + n * NO)
                ov = bank[c % 2][:].rearrange("p (i x) -> p i x", i=TT)[:, :, 0:2 * VW].rearrange("p i (h v) -> p i h v", h=2)
                step_v.then_wait(nc.vector.reciprocal(rden[:, c % 2].unsqueeze(3), ov[:, :, :, HD:VW]))
                nc.vector.tensor_tensor(O[:, :, 2 * c:2 * c + 2, :], ov[:, :, :, 0:HD],
                                        rden[:, c % 2].unsqueeze(3).to_broadcast([P, TT, 2, HD]), ALU.mult).then_inc(o_read, 1)

            def add_attention(m, b):
                dve.wait_ge(y_ready, UP + m + 1)
                step_t.then_wait(nc.vector.tensor_tensor(X[:, b, 1:1 + T], X[:, b, 1:1 + T], bank[6][:, 0:T], ALU.add), cleared)
                nc.vector.tensor_copy(xf[0:64, :], X[0:64, b, 1:1 + T])
                nc.vector.tensor_copy(xf[64:P, :], X[64:P, b, 0:T]).then_inc(xf_ready, 1)
                dve.wait_ge(xf_ready, m + 1)

            def deviate(m):
                dve.wait_ge(mean_ready, m + 1)
                nc.vector.tensor_tensor(dev[:], xf[:], bank[7][:, 0:T], ALU.subtract).then_inc(dev_ready, 1)

            def diagonals(m):
                for i in range(TT):
                    last = nc.vector.tensor_scalar(dg[:, i, :], idf[:], nrm[:, 2, NORMS + i:NORMS + i + 1], None, ALU.mult)
                last.then_inc(dg_ready, 1)

            def norm_x(m):
                dve.wait_ge(rs_ready, m + 1)
                dve.wait_ge(dev_ready, m + 1)
                step_t.then_wait(nc.vector.tensor_tensor(t1[:], dev[:], bank[7][:, 0:T], ALU.mult))
                nc.vector.tensor_scalar(xn[:], t1[:], fpar[:, 0:1], fpar[:, 1:2], ALU.mult, ALU.add).then_inc(xn_ready, 1)

            def gate(m, j):
                dve.wait_ge(gelu_ready, m * FC + j + 1)
                nc.vector.scalar_tensor_tensor(hid[:, j, :], bank[6 + j % 2][:, T:2 * T], fpar[:, 3 + j:4 + j], gl[:, j % 2, :],
                                               ALU.add, ALU.mult).then_inc(hid_ready, 1)

            def add_ffn(m, b):
                dve.wait_ge(y2_ready, m + 1)
                nc.vector.scalar_tensor_tensor(X[:, b, 1:1 + T], bank[7][:, 0:T], fpar[:, 2:3], X[:, b, 1:1 + T],
                                               ALU.add, ALU.add).then_inc(x_updated, 1)

            def step(n, b, tail):
                m, bm = n - 1, (b + B - 1) % B
                step_v.body(n * V_BODY)
                step_t.body(m * T_BODY)
                for p in range(NP):
                    rotate(n, p)
                    if tail and p == NP - 3:
                        add_attention(m, bm)
                    if tail and p == NP - 2:
                        deviate(m)
                roots(n, m, tail)
                if tail:
                    dve.wait_ge(tail_in, tail_weights(n))
                    diagonals(m)
                split_norms(n)
                if tail:
                    norm_x(m)
                for k in range(NP):
                    scale(n, k)
                    if tail and k in (1, 3, 5):
                        gate(m, k // 2)
                for c in range(NS + 3):
                    if c < NS:
                        center(n, c)
                    if tail and c == 1:
                        add_ffn(m, bm)
                    if c >= 3:
                        take_o(n, c - 3)
                assert step_v.here == V_BODY and step_t.here == (T_BODY if tail else 0)

            dve.wait_ge(cleared, 1)
            walk(dve, top, step)
            m = DEPTH * B - 1
            step_t.body(m * T_BODY)
            add_attention(m, B - 1)
            deviate(m)
            step_v.body(DEPTH * B * V_BODY)
            roots(DEPTH * B, m, True, heads=False)
            diagonals(m)
            norm_x(m)
            for j in range(FC):
                gate(m, j)
            add_ffn(m, B - 1)
            for i in range(NT // 4):
                dve.wait_ge(xt_ready, i + 1)
                step_v.then_wait(nc.vector.tensor_copy(fy[:, 4 * i:4 * i + 4, :], bank[i][:].rearrange("p (n d) -> p n d", n=4)))
            r = token_norm(nc, dve, step_v, fy, fdev, stat, fsq, fdev_ready, fsquared, 1)
            step_v.then_wait(nc.vector.tensor_tensor(fdev, fdev, r, ALU.mult))
            nc.vector.tensor_tensor(x1[:], x1[:], fdev, ALU.add).then_inc(finished, 1)

        @block.tensor
        def _(pe):
            mm = nc.tensor.matmul

            def top(l):
                pass

            def raw(n, l, p):
                if p in (0, NP // 2):
                    pe.wait_ge(w_low, WPARTS * l + 1 + 2 * p // NP)
                    pe.wait_ge(ws_low, SWAPPED * l + 1 + 2 * p // NP)
                if p >= 2:
                    pe.wait_ge(turned, n * NP + p - 1)
                for t, (hi, lo) in enumerate(((wh, wl), (wsh, wsl))):
                    for a in range(2):
                        c = 2 * p + a
                        ps = bank[2 * t + p % 2][:, T * a:T * a + T]
                        w_hi, w_lo = hi[:, P * c:P * c + P], lo[:, P * c:P * c + P]
                        mm(ps, w_hi, xh[:, WIN:], start=True, stop=False)
                        mm(ps, w_hi, xl[:, WIN:], start=False, stop=False)
                        last = mm(ps, w_lo, xh[:, WIN:], start=False, stop=True)
                last.then_inc(raw_ready, 1)

            def gather_norms(n, p):
                pe.wait_ge(squared, n * NP + p + 1)
                if p == 0:
                    pe.wait_ge(centered, UP + n * NS)
                for a in range(2):
                    for i in range(TT):
                        at = 2 * H * i + 2 * (2 * p + a)
                        last = mm(NRM[:, at:at + 2], sq[:, p % 2, a, P * i:P * i + P], patb[:], start=True, stop=True)
                last.then_inc(norm_done, 1)

            def values(n, l, j):
                if j == 0:
                    pe.wait_ge(w_low, WPARTS * l + 3)
                    pe.wait_ge(turned, (n + 1) * NP)
                if j >= 4:
                    pe.wait_ge(v_copied, n * NV + j - 3)
                u, half = j // 2, j % 2
                ps = bank[j % 4][0:KW, :]
                at = slice(2 * INNER + 512 * half, 2 * INNER + 512 * half + 512)
                x_hi, x_lo = xh[:, QW * u:QW * u + KW], xl[:, QW * u:QW * u + KW]
                mm(ps, x_hi, wh[:, at], start=True, stop=False)
                mm(ps, x_hi, wl[:, at], start=False, stop=False)
                mm(ps, x_lo, wh[:, at], start=False, stop=True).then_inc(v_ready, 1)

            def turn_norms(n):
                pe.wait_ge(root_ready, n + 1)
                for i in range(TT):
                    last = nc.tensor.transpose(NRT[:, P * i:P * i + P], nrm[:, 2, 2 * H * i:2 * H * i + 2 * H], idf[:])
                last.then_inc(rt_ready, 1)

            def spread_norms(n, k):
                if k == 0:
                    pe.wait_ge(rn_ready, n + 1)
                if k < 4:
                    pe.wait_ge(v_copied, n * NV + NV - 3 + k)
                else:
                    pe.wait_ge(scaled, n * NP + k - 3)
                for a in range(2):
                    c = 2 * ORDER[k] + a
                    ps = bank[k % 4][:, T * a:T * a + T]
                    mm(ps, selb[:, c, :], rh[:], start=True, stop=False)
                    last = mm(ps, selb[:, c, :], rl[:], start=False, stop=True)
                last.then_inc(rb_ready, 1)

            def scores(n, c):
                if c % 2 == 0:
                    pe.wait_ge(scaled, n * NP + c + 2)
                if c >= 2:
                    pe.wait_ge(centered, UP + n * NS + c - 1)
                ps = bank[4 + c % 2]
                mm(ps[:, 0:NU * KW], idb[:], wmask[:], start=True, stop=False)
                for u in range(NU):
                    for r0 in (0, HD):
                        last = mm(ps[r0:r0 + QW, KW * u:KW * u + KW], qT[r0:r0 + HD, c, QW * u:QW * u + QW],
                                  kT[r0:r0 + HD, c, QW * u:QW * u + KW], start=False, stop=u == NU - 1, tile_position=(r0, r0))
                last.then_inc(s_ready, 1)

            def transpose_probs(n, c):
                pe.wait_ge(exped, n * NS + c + 1)
                if c >= 2:
                    pe.wait_ge(pt_copied, UP + n * NS + c - 1)
                elif c == 0:
                    pe.wait_ge(scaled, (n + 1) * NP)
                for u in range(NU):
                    last = nc.tensor.transpose(bank[2 + c % 2][0:KW, P * u:P * u + P], pr[:, c % 2, KW * u:KW * u + KW], idf[:])
                last.then_inc(pt_ready, 1)

            def weigh_values(n, c):
                wait_apart(pe, cleared, pt_copied, UP + n * NS + c + 1)
                if c >= 2:
                    pe.wait_ge(o_read, UP + n * NS + c - 1)
                for u in range(NU):
                    q0, at = QW * (u % 2), T * (u // 2)
                    for hp in range(2):
                        last = mm(bank[c % 2][q0:q0 + QW, at + VW * hp:at + VW * hp + VW], pT[:, c % 2, u, QW * hp:QW * hp + QW],
                                  V[:, u, 2 * c + hp, :], start=True, stop=True, tile_position=(0, q0))
                last.then_inc(o_ready, 1)

            def transpose_o(m, k):
                if k == 0:
                    pe.wait_ge(o_read, UP + (m + 1) * NS)
                    pe.wait_ge(x_updated, B + m)
                if k >= 2:
                    pe.wait_ge(ot_copied, m * NO + k - 1)
                i, c0 = k // 2, 4 * (k % 2)
                for c in range(c0, c0 + 4):
                    last = nc.tensor.transpose(bank[6 + k % 2][:, P * (c - c0):P * (c - c0) + P],
                                               O[:, i, 2 * c:2 * c + 2, :].rearrange("p h d -> p (h d)"), idf[:])
                last.then_inc(ot_ready, 1)

            def project_out(m):
                pe.wait_ge(ot_copied, (m + 1) * NO)
                for c in range(QC):
                    last = mm(bank[6][:, 0:T], wo[:, c, :], OT[:, c, :], start=c == 0, stop=c == QC - 1)
                last.then_inc(y_ready, 1)

            def means(m):
                pe.wait_ge(xf_ready, m + 1)
                mm(bank[7][:, 0:T], mean1[:], xf[:], start=True, stop=True).then_inc(mean_ready, 1)

            def variances(m):
                pe.wait_ge(dsq_ready, m + 1)
                for i in range(TT):
                    last = mm(bank[6][:, i:i + 1], dsq[:, P * i:P * i + P], mean1[:, 0:1], start=True, stop=True)
                last.then_inc(var_ready, 1)

            def spread_root(m):
                pe.wait_ge(dg_ready, m + 1)
                for i in range(TT):
                    last = mm(bank[7][:, P * i:P * i + P], ones[:], dg[:, i, :], start=True, stop=True)
                last.then_inc(rs_ready, 1)

            def hidden(m, j):
                if j == 0:
                    pe.wait_ge(xn_ready, m + 1)
                if j == 2:
                    pe.wait_ge(hid_ready, UP + m * FC + 1)
                mm(bank[6 + j % 2][:, 0:T], w1[:, FC + j, :], xn[:], start=True, stop=True)
                mm(bank[6 + j % 2][:, T:2 * T], w1[:, j, :], xn[:], start=True, stop=True).then_inc(h_ready, 1)

            def ffn_out(m):
                pe.wait_ge(hid_ready, UP + (m + 1) * FC)
                for j in range(FC):
                    last = mm(bank[7][:, 0:T], w2[:, j, :], hid[:, j, :], start=j == 0, stop=j == FC - 1)
                last.then_inc(y2_ready, 1)

            def step(n, b, tail):
                m, l = n - 1, n // B
                pe.wait_ge(xs_ready, n + 1)
                for p in range(NP):
                    if tail and p < 2:
                        pe.wait_ge(o_read, UP + n * NS - 1 + p)
                        pe.wait_ge(pt_copied, UP + n * NS - 1 + p)
                    raw(n, l, p)
                    if p:
                        gather_norms(n, p - 1)
                    if tail and 1 <= p <= NO:
                        transpose_o(m, p - 1)
                    if tail and p == NO + 1:
                        pe.wait_ge(tail_in, tail_weights(n))
                        project_out(m)
                    if tail and p == NP - 2:
                        means(m)
                gather_norms(n, NP - 1)
                if tail:
                    variances(m)
                for j in range(NV):
                    values(n, l, j)
                    if tail:
                        if j == 4:
                            spread_root(m)
                        if j >= NV - 2:
                            hidden(m, j - NV + 2)
                    if j == 3:
                        turn_norms(n)
                for k in range(NP):
                    spread_norms(n, k)
                    if tail and k == 3:
                        hidden(m, 2)
                scores(n, 0)
                scores(n, 1)
                if tail:
                    ffn_out(m)
                for c in range(NS + 1):
                    if c < NS:
                        transpose_probs(n, c)
                    if c + 2 < NS:
                        scores(n, c + 2)
                    if c:
                        weigh_values(n, c - 1)

            pe.wait_ge(sel_ready, 1)
            pe.wait_ge(wmask_ready, 1)
            pe.wait_ge(const_in, 16 * CONSTS)
            walk(pe, top, step)
            m = DEPTH * B - 1
            for k in range(NO):
                transpose_o(m, k)
            project_out(m)
            means(m)
            variances(m)
            spread_root(m)
            for j in range(FC):
                hidden(m, j)
            ffn_out(m)
            pe.wait_ge(x_updated, B + DEPTH * B)
            for i in range(NT // 4):
                for q in range(4):
                    t = 4 * i + q
                    last = nc.tensor.transpose(bank[i][:, P * q:P * q + P], X[:, t // TT, 1 + P * (t % TT):1 + P * (t % TT) + P], idf[:])
                last.then_inc(xt_ready, 1)


def build(nc, a, out):
    with ExitStack() as ctx:
        def sb(name, shape, dt=F32):
            return ctx.enter_context(nc.sbuf_tensor(name, shape, dt))

        x1 = sb("x1", [P, NT, D])
        X = sb("X", [P, B, 1 + T])
        idf = sb("idf", [P, P])
        idb = sb("idb", [P, P], BF16)
        stage = sb("stage", [P, 3 * INNER])
        w_loaded = ctx.enter_context(nc.semaphore("w_loaded"))
        build_global(nc, x1, X, idf, idb, stage, a["x"], a["g_qk"], a["g_v"], a["g_bits"], a["g_out"], a["g_tr"], a["g_trw"],
                     a["g_scal"], a["bit_eye"], a["g_low"], a["g_spread"], a["g_mask"], a["ident"], a["w_qkv"], w_loaded)
        build_layers(nc, x1, X, idf, idb, stage, w_loaded, a["w_qkv"], a["qk_scale"], a["w_o"], a["ffn_par"], a["w_1"], a["w_2"],
                     a["rot"], a["w_mask"], a["pat"], a["sel"], out)


def constants():
    f = np.float32
    neg = -1e37
    q = np.arange(P)
    g_mask = np.zeros((P, GS), f)
    g_mask[:, 0:P] = np.where(q[None, :] > q[:, None], neg, 0)
    g_mask[:, P:] = np.where(np.arange(T)[None, :] > q[:, None] + P, neg, 0)
    a, j = np.arange(P)[:, None, None] % QW, np.arange(KW)[None, None, :]
    u = np.arange(NU)[None, :, None]
    seen = (j >= a) & (j <= a + WIN) & ((u > 0) | (j >= WIN))
    w_mask = np.where(seen, 0, neg).astype(f).reshape(P, NU * KW)
    bit_eye = np.zeros((2 * NB, P), f)
    for i in range(NB):
        bit_eye[i, i::32] = 1
        bit_eye[i, 2 * NB + i::32] = 1
    r = q % 32
    low = [(r >= 2 * GD) & (r < 3 * GD), (r >= GD) & (r < 2 * GD), (r >= 2 * NB) & (r < 4 * NB)]
    g_spread = (q[None, None, :] // 32 + 4 * np.arange(GC)[None, :, None] == np.arange(GH)[:, None, None]).astype(f)
    g_low = -np.stack(low, 1).astype(f)
    pat = (q[:, None] // HD == np.arange(2)[None, :]).astype(f)
    sel = (np.arange(2 * QC * P)[None, :] // HD == np.arange(2 * H)[:, None]).astype(f)
    half = np.arange(0, HD, 2, dtype=f)
    inv_freq = (f(1.0) / np.power(f(10000.0), half / f(HD))).astype(f)
    t = np.arange(T, dtype=f)
    freqs = (inv_freq[:, None] * t[None, :]).astype(f)
    base = ((half + f(0.4 * HD)) / f(1.4 * HD)).astype(f)
    scale = np.power(base[:, None].astype(np.float64), ((t - T // 2) / f(WIN // 2))[None, :].astype(np.float64))
    cos, sin = np.cos(freqs.astype(np.float64)), np.sin(freqs.astype(np.float64))

    def over_heads(lo, hi):
        return np.tile(np.concatenate([lo, hi], 0), (2, 1)).astype(f)

    rot = np.stack([over_heads(cos * scale, cos * scale), over_heads(-sin * scale, sin * scale),
                    over_heads(cos / scale, cos / scale), over_heads(-sin / scale, sin / scale)], 1)
    return dict(g_mask=g_mask, w_mask=w_mask, ident=np.eye(P, dtype=f), bit_eye=bit_eye, g_low=g_low, g_spread=g_spread, pat=pat, sel=sel, rot=np.ascontiguousarray(rot))


def lay_out(i):
    f = np.float32
    i = {k: np.asarray(v) for k, v in i.items()}
    a = dict(x=i["L0_attn_x"].reshape(B * T, D))
    wt = i["L0_attn_qkv_w"].T
    g_qk = np.zeros((P, 2 * GC, 4, 32), f)
    for copy in range(3):
        g_qk[:, :, :, GD * copy:GD * copy + GD] = wt[:, 0:2 * D].reshape(P, 2 * GC, 4, GD)
    a["g_qk"] = g_qk.reshape(P, 2 * GC, P)
    a["g_v"] = wt[:, 2 * D:]
    g_bits = np.zeros((P, 4, 32), f)
    for at in (0, 2 * NB):
        g_bits[:, :, at:at + NB] = i["L0_attn_hex_w"].T[:, None, :]
        g_bits[:, :, at + NB:at + 2 * NB] = i["L0_attn_q6_w"].T[:, None, :]
    a["g_bits"] = g_bits.reshape(P, P)
    g_out = np.zeros((4, 32, GC, D), f)
    g_out[:, 0:GD] = i["L0_attn_out_w"].T.reshape(GC, 4, GD, D).transpose(1, 2, 0, 3)
    a["g_out"] = g_out.reshape(P, GC, D)
    g_tr = np.zeros((NTR, NB, 2 * NB), f)
    g_tr[:, :, NB:] = i["L0_attn_transforms"].transpose(0, 2, 1)
    a["g_tr"] = g_tr
    a["g_trw"] = i["L0_attn_transform_weights"]
    scal = [i["L0_attn_hamming_lambda_logit"], i["L0_attn_scale_logit"], i["L0_attn_sips_alpha"], i["L0_attn_sips_beta"]]
    a["g_scal"] = np.broadcast_to(np.concatenate([s.reshape(1) for s in scal])[None, :], (P, 4))
    a["w_qkv"] = i["L0_ffn_Wqkv"]
    swapped = (np.arange(HD) + HD // 2) % HD
    cols = [i["L0_ffn_q_scale"], i["L0_ffn_q_scale"][:, swapped], i["L0_ffn_k_scale"], i["L0_ffn_k_scale"][:, swapped]]
    a["qk_scale"] = np.tile(np.stack([c.T for c in cols], 2), (2, 1, 1))
    a["w_o"] = i["L0_ffn_Wo"].reshape(DEPTH, QC, P, D).transpose(0, 2, 1, 3)
    w_1 = np.zeros((DEPTH, D, 2, FC * P), f)
    w_1[:, :, :, 0:DIN] = i["L0_ffn_W1"].reshape(DEPTH, D, 2, DIN)
    a["w_1"] = w_1.reshape(DEPTH, D, 2 * FC, P)
    w_2 = np.zeros((DEPTH, FC * P, D), f)
    w_2[:, 0:DIN] = i["L0_ffn_W2"]
    a["w_2"] = w_2.reshape(DEPTH, FC, P, D).transpose(0, 2, 1, 3)
    b_1 = np.zeros((DEPTH, 2, FC * P), f)
    b_1[:, :, 0:DIN] = i["L0_ffn_b1"].reshape(DEPTH, 2, DIN)
    par = np.zeros((DEPTH, P, 3 + 2 * FC), f)
    par[:, :, 0], par[:, :, 1], par[:, :, 2] = i["L0_ffn_ln_g"], i["L0_ffn_ln_b"], i["L0_ffn_b2"]
    par[:, :, 3:] = b_1.reshape(DEPTH, 2 * FC, P).transpose(0, 2, 1)
    a["ffn_par"] = par
    return a


def kernel(**inputs):
    import concourse.bacc as bacc
    from concourse.bass_utils import run_bass_kernel_spmd

    nc = bacc.Bacc("TRN2", target_bir_lowering=False, num_devices=1)
    arrays = {k: np.ascontiguousarray(v) for k, v in {**lay_out(inputs), **constants()}.items()}
    aps = {k: nc.dram_tensor(k + "_dram", v.shape, mybir.dt.from_np(v.dtype), kind="ExternalInput").ap() for k, v in arrays.items()}
    out = nc.dram_tensor("out_dram", (B * T, D), F32, kind="ExternalOutput").ap()
    build(nc, aps, out)
    r = run_bass_kernel_spmd(nc, [{k + "_dram": v for k, v in arrays.items()}], core_ids=[0])
    return r.results[0]["out_dram"].reshape(B, T, D)
```
